# Optimizing a Trainium2 kernel written in Bass

```python
import numpy as np
import jax
import jax.numpy as jnp

def _softmax(x, axis=-1):
    return jax.nn.softmax(x, axis=axis)

def _gelu(x):
    return jax.nn.gelu(x, approximate=True)

def _silu(x):
    return jax.nn.silu(x)

def _sigmoid(x):
    return jax.nn.sigmoid(x)

def _layernorm(x, axis=-1, eps=1e-05):
    m = jnp.mean(x, axis=axis, keepdims=True)
    v = jnp.var(x, axis=axis, keepdims=True)
    return (x - m) / jnp.sqrt(v + eps)

def _scatter_add(tgt, idx, src, axis=0):
    return tgt.at[idx].add(src)

def _segment_sum(src, seg, n):
    return jax.ops.segment_sum(src, seg, n)
kernel_name = 'mk_conv_attn_hybrid_d2_conv_nhwc512_r4_dab20a'

def setup_inputs(seed: int=0):
    np.random.seed(seed)
    _w = jnp.asarray

    def _rec_inputs():
        import jax
        import jax.numpy as jnp
        _gk = jax.random.key(seed)
        x = -0.000125 + 0.9999 * jax.random.normal(jax.random.fold_in(_gk, 1), (32, 16, 32, 128), jnp.float32)
        return x
    x = _rec_inputs()

    def _L0_conv_setup():
        import jax, jax.numpy as jnp
        import numpy as np
        EMB = 128
        HEADS = 8
        N_AGENTS = 16
        SAMPLES = 5
        B, T = (32, 32)
        NEG = -1000000000.0
        key = jax.random.key(seed)
        ks = jax.random.split(key, 12)
        s = 1.0 / np.sqrt(EMB)
        inp = {'x': jax.random.normal(ks[0], (B, N_AGENTS, T, EMB), jnp.float32), 'coalition': jax.random.permutation(ks[1], N_AGENTS).astype(jnp.int32), 'masks': jax.random.randint(ks[2], (SAMPLES, N_AGENTS, N_AGENTS), 0, 2, jnp.int32), 'agent_temporal_mask': jnp.ones((B, T), jnp.int32), 'emb_W': jax.random.normal(ks[3], (N_AGENTS, EMB), jnp.float32), 'Wq': jax.random.uniform(ks[4], (EMB, EMB), jnp.float32, -s, s), 'bq': jnp.zeros((EMB,), jnp.float32), 'Wk': jax.random.uniform(ks[5], (EMB, EMB), jnp.float32, -s, s), 'bk': jnp.zeros((EMB,), jnp.float32), 'Wv': jax.random.uniform(ks[6], (EMB, EMB), jnp.float32, -s, s), 'bv': jnp.zeros((EMB,), jnp.float32), 'Wo': jax.random.uniform(ks[7], (EMB, EMB), jnp.float32, -s, s), 'bo': jnp.zeros((EMB,), jnp.float32)}
        return inp
    _L0_conv_all = _L0_conv_setup()
    _L0_conv_in = {k: v for k, v in _L0_conv_all.items() if k in ('coalition', 'masks', 'agent_temporal_mask', 'emb_W', 'Wq', 'bq', 'Wk', 'bk', 'Wv', 'bv', 'Wo', 'bo')}
    del _L0_conv_all

    def _L1_attn_setup():
        import jax, jax.numpy as jnp
        import numpy as np
        EPS = 1e-06
        H = 8

        def _feature_map(t):
            return jax.nn.elu(t) + 1.0
        key = jax.random.key(seed)
        ks = jax.random.split(key, 4)
        B, L, C = (4, 4096, 128)
        scale = 1.0 / np.sqrt(C)
        x = jax.random.normal(ks[0], (B, L, C), dtype=jnp.float32)
        Wq = jax.random.normal(ks[1], (C, C), dtype=jnp.float32) * scale
        Wk = jax.random.normal(ks[2], (C, C), dtype=jnp.float32) * scale
        Wv = jax.random.normal(ks[3], (C, C), dtype=jnp.float32) * scale
        bq = jnp.zeros((C,), dtype=jnp.float32)
        bk = jnp.zeros((C,), dtype=jnp.float32)
        bv = jnp.zeros((C,), dtype=jnp.float32)
        return {'x': x, 'Wq': Wq, 'bq': bq, 'Wk': Wk, 'bk': bk, 'Wv': Wv, 'bv': bv}
    _L1_attn_all = _L1_attn_setup()
    _L1_attn_in = {k: v for k, v in _L1_attn_all.items() if k in ('Wq', 'bq', 'Wk', 'bk', 'Wv', 'bv')}
    del _L1_attn_all

    def _L1_ffn_setup():
        import jax, jax.numpy as jnp
        import numpy as np
        TOP_K = 2

        def quick_gelu(x):
            return x * jax.nn.sigmoid(1.702 * x)
        key = jax.random.key(seed)
        ks = jax.random.split(key, 6)
        B, S, H, I, E = (8, 1024, 128, 256, 8)
        s_h = 1.0 / np.sqrt(H).astype(np.float32)
        s_i = 1.0 / np.sqrt(I).astype(np.float32)
        return {'hidden_states': jax.random.normal(ks[0], (B, S, H), jnp.float32), 'router_w': jax.random.normal(ks[1], (H, E), jnp.float32) * s_h, 'router_b': jnp.zeros((E,), jnp.float32), 'gate_up_proj': jax.random.normal(ks[2], (E, H, 2 * I), jnp.float32) * s_h, 'gate_up_proj_bias': jnp.zeros((E, 2 * I), jnp.float32), 'down_proj': jax.random.normal(ks[3], (E, I, H), jnp.float32) * s_i, 'down_proj_bias': jnp.zeros((E, H), jnp.float32)}
    _L1_ffn_all = _L1_ffn_setup()
    _L1_ffn_in = {k: v for k, v in _L1_ffn_all.items() if k in ('router_w', 'router_b', 'gate_up_proj', 'gate_up_proj_bias', 'down_proj', 'down_proj_bias')}
    del _L1_ffn_all
    return {'x': x, 'L0_conv_coalition': _L0_conv_in['coalition'], 'L0_conv_masks': _L0_conv_in['masks'], 'L0_conv_agent_temporal_mask': _L0_conv_in['agent_temporal_mask'], 'L0_conv_emb_W': _L0_conv_in['emb_W'], 'L0_conv_Wq': _L0_conv_in['Wq'], 'L0_conv_bq': _L0_conv_in['bq'], 'L0_conv_Wk': _L0_conv_in['Wk'], 'L0_conv_bk': _L0_conv_in['bk'], 'L0_conv_Wv': _L0_conv_in['Wv'], 'L0_conv_bv': _L0_conv_in['bv'], 'L0_conv_Wo': _L0_conv_in['Wo'], 'L0_conv_bo': _L0_conv_in['bo'], 'L1_attn_Wq': _L1_attn_in['Wq'], 'L1_attn_bq': _L1_attn_in['bq'], 'L1_attn_Wk': _L1_attn_in['Wk'], 'L1_attn_bk': _L1_attn_in['bk'], 'L1_attn_Wv': _L1_attn_in['Wv'], 'L1_attn_bv': _L1_attn_in['bv'], 'L1_ffn_router_w': _L1_ffn_in['router_w'], 'L1_ffn_router_b': _L1_ffn_in['router_b'], 'L1_ffn_gate_up_proj': _L1_ffn_in['gate_up_proj'], 'L1_ffn_gate_up_proj_bias': _L1_ffn_in['gate_up_proj_bias'], 'L1_ffn_down_proj': _L1_ffn_in['down_proj'], 'L1_ffn_down_proj_bias': _L1_ffn_in['down_proj_bias']}

def reference(x, L0_conv_coalition, L0_conv_masks, L0_conv_agent_temporal_mask, L0_conv_emb_W, L0_conv_Wq, L0_conv_bq, L0_conv_Wk, L0_conv_bk, L0_conv_Wv, L0_conv_bv, L0_conv_Wo, L0_conv_bo, L1_attn_Wq, L1_attn_bq, L1_attn_Wk, L1_attn_bk, L1_attn_Wv, L1_attn_bv, L1_ffn_router_w, L1_ffn_router_b, L1_ffn_gate_up_proj, L1_ffn_gate_up_proj_bias, L1_ffn_down_proj, L1_ffn_down_proj_bias):
    import jax
    import jax.numpy as jnp

    def _L0_conv_ref(x, coalition, masks, agent_temporal_mask, emb_W, Wq, bq, Wk, bk, Wv, bv, Wo, bo):
        import jax, jax.numpy as jnp
        import numpy as np
        EMB = 128
        HEADS = 8
        N_AGENTS = 16
        SAMPLES = 5
        B, T = (32, 32)
        NEG = -1000000000.0
        b, n_a, t, e = x.shape
        hd = e // HEADS
        xi = jnp.transpose(x, (0, 2, 1, 3)).reshape(b * t, n_a, e)
        xi = xi + emb_W[coalition][None, :, :]

        def proj(W, bias):
            y = jnp.einsum('bae,ef->baf', xi, W) + bias
            return y.reshape(b * t, n_a, HEADS, hd).transpose(0, 2, 1, 3)
        q, k, v = (proj(Wq, bq), proj(Wk, bk), proj(Wv, bv))
        scores = jnp.einsum('bhqd,bhkd->bhqk', q, k) / jnp.sqrt(jnp.float32(hd))
        eye = jnp.eye(n_a, dtype=jnp.float32)
        m = masks.astype(jnp.float32) * (1.0 - eye) + eye
        masked = jnp.where(m[:, None, None, :, :] > 0, scores[None], NEG)
        attn = jax.nn.softmax(masked, axis=-1)
        out_h = jnp.einsum('sbhqk,bhkd->bhqd', attn, v) / SAMPLES
        out = out_h.transpose(0, 2, 1, 3).reshape(b * t, n_a, e)
        out = jnp.einsum('bae,ef->baf', out, Wo) + bo
        return out.reshape(b, t, n_a, e).transpose(0, 2, 1, 3)

    def _L1_attn_ref(x, Wq, bq, Wk, bk, Wv, bv):
        import jax, jax.numpy as jnp
        import numpy as np
        EPS = 1e-06
        H = 8

        def _feature_map(t):
            return jax.nn.elu(t) + 1.0
        B, L, C = x.shape
        D = C // H
        q = (x @ Wq + bq).reshape(B, L, H, D)
        k = (x @ Wk + bk).reshape(B, L, H, D)
        v = (x @ Wv + bv).reshape(B, L, H, D)
        Q = _feature_map(q)
        K = _feature_map(k)
        S = v.shape[1]
        v_scaled = v / S
        KV = jnp.einsum('nshd,nshv->nhdv', K, v_scaled)
        Z = 1.0 / (jnp.einsum('nlhd,nhd->nlh', Q, K.sum(axis=1)) + EPS)
        out = jnp.einsum('nlhd,nhdv,nlh->nlhv', Q, KV, Z) * S
        return out.reshape(B, L, C)

    def _L1_ffn_ref(hidden_states, router_w, router_b, gate_up_proj, gate_up_proj_bias, down_proj, down_proj_bias):
        import jax, jax.numpy as jnp
        import numpy as np
        TOP_K = 2

        def quick_gelu(x):
            return x * jax.nn.sigmoid(1.702 * x)
        B, S, H = hidden_states.shape
        E = router_b.shape[0]
        x = hidden_states.reshape(-1, H)
        T = x.shape[0]
        logits = x @ router_w + router_b
        top_w, sel = jax.lax.top_k(logits, TOP_K)
        top_w = jax.nn.softmax(top_w, axis=-1)
        tok_w = jnp.zeros((T, E), x.dtype).at[jnp.arange(T)[:, None], sel].add(top_w)

        def body(acc, params):
            Wgu, bgu, Wd, bd, w_e = params
            gu = x @ Wgu + bgu
            gate, up = jnp.split(gu, 2, axis=-1)
            act = (up + 1.0) * quick_gelu(gate)
            out = act @ Wd + bd
            return (acc + out * w_e[:, None], None)
        acc0 = jnp.zeros((T, H), x.dtype)
        acc, _ = jax.lax.scan(body, acc0, (gate_up_proj, gate_up_proj_bias, down_proj, down_proj_bias, tok_w.T))
        return acc.reshape(B, S, H)

    def _gn(v, G=32, eps=1e-05):
        B_, H_, W_, C_ = v.shape
        g = v.reshape(B_, H_, W_, G, C_ // G)
        m = jnp.mean(g, axis=(1, 2, 4), keepdims=True)
        s = jnp.var(g, axis=(1, 2, 4), keepdims=True)
        return ((g - m) / jnp.sqrt(s + eps)).reshape(v.shape)

    def _ln_c(v, eps=1e-06):
        m = jnp.mean(v, axis=-1, keepdims=True)
        s = jnp.var(v, axis=-1, keepdims=True)
        return (v - m) / jnp.sqrt(s + eps)

    def _ln_t(v, eps=1e-05):
        m = jnp.mean(v, axis=-1, keepdims=True)
        s = jnp.var(v, axis=-1, keepdims=True)
        return (v - m) / jnp.sqrt(s + eps)

    def _to_tokens(v):
        B_, H_, W_, C_ = v.shape
        return v.reshape(B_, H_ * W_, C_)

    def _from_tokens(t, like):
        return t.reshape(like.shape)
    x = x + _L0_conv_ref(_gn(x), L0_conv_coalition, L0_conv_masks, L0_conv_agent_temporal_mask, L0_conv_emb_W, L0_conv_Wq, L0_conv_bq, L0_conv_Wk, L0_conv_bk, L0_conv_Wv, L0_conv_bv, L0_conv_Wo, L0_conv_bo)
    t = _to_tokens(x)
    t = t + _L1_attn_ref(_ln_t(t), L1_attn_Wq, L1_attn_bq, L1_attn_Wk, L1_attn_bk, L1_attn_Wv, L1_attn_bv)
    t = t + _L1_ffn_ref(_ln_t(t), L1_ffn_router_w, L1_ffn_router_b, L1_ffn_gate_up_proj, L1_ffn_gate_up_proj_bias, L1_ffn_down_proj, L1_ffn_down_proj_bias)
    x = _from_tokens(t, x)
    return x

_drawn_inputs = setup_inputs


def setup_inputs(seed=0):
    import zlib

    import numpy as np

    out = dict(_drawn_inputs(seed))
    spreads = {'L0_conv_bq': (0.0, 0.1),
     'L0_conv_bk': (0.0, 0.8),
     'L0_conv_bv': (0.0, 0.1),
     'L0_conv_bo': (0.0, 0.1),
     'L1_attn_bq': (0.0, 0.509),
     'L1_attn_bk': (0.0, 0.672),
     'L1_attn_bv': (0.0, 0.1),
     'L1_ffn_router_b': (0.0, 0.1),
     'L1_ffn_gate_up_proj_bias': (0.0, 0.1),
     'L1_ffn_down_proj_bias': (0.0, 0.1)}
    factors = {}
    for name, (base, spread) in spreads.items():
        noise = np.random.default_rng([zlib.crc32(name.encode()), seed]).standard_normal(out[name].shape)
        drawn = base * np.exp(spread * noise) if base else spread * noise
        out[name] = jnp.asarray(drawn.astype(out[name].dtype))
    for name, factor in factors.items():
        out[name] = (out[name] * factor).astype(out[name].dtype)
    return out
```

```python
from contextlib import ExitStack

import numpy as np

import concourse.bass as bass
from concourse import mybir

F32, F16, I32 = mybir.dt.float32, mybir.dt.float16, mybir.dt.int32
ALU = mybir.AluOpType
ACT = mybir.ActivationFunctionType
AX = mybir.AxisListType

P = 128
B, A, T, C = 32, 16, 32, 128
H, HD = 8, 16
S = 5
TILES = A * T // P
TOK = A * T
PAIRS = B // 2
WS = 64.0
GN_EPS, LN_EPS, ATT_EPS = 1e-5, 1e-5, 1e-6
TABLE_STEP = 18
E, I = 8, 256
BLOCK = 256
REGION = B * TOK + BLOCK
BLOCKS = 2 * B * TOK // BLOCK + E
ROW = C + 4
LN_STEPS, ROUTE_STEPS, PLACE_STEPS = 7, 22, 15
NO_SLOT = 1e6
SP_ = 64

CONST = {}


def _constants():
    parts, at = {0: [], 1: []}, [0, 0]

    def put(late, name, a):
        full = np.zeros((P, a.shape[1]), np.float32)
        full[: a.shape[0]] = a
        CONST[name] = (at[late], a.shape[1])
        at[late] += a.shape[1]
        parts[late].append(full)

    r = np.arange(P)
    put(0, "ident", np.eye(P))
    put(0, "block8", r[:, None] // HD == np.arange(H)[None, :])
    put(0, "group", (r[:, None] // 4 == r[None, :] // 4) / 8.0)
    put(0, "eye_qk", np.tile(np.eye(A), (S, 1)))
    put(1, "block_kv", (r[:, None] // HD == r[None, :] // HD) / float(TOK))
    put(1, "block_ks", (r[:, None] // HD == np.arange(H)[None, :]) / float(TOK))
    put(1, "before", (r[:, None] < r[None, :]) * 1.0)
    put(1, "rank_of", np.tile(float(E) - np.arange(E), (P, 8)))
    put(1, "region", np.tile(np.arange(E) * float(REGION), (P, 8)))
    put(1, "block_no", np.tile(np.arange(BLOCKS) * 1.0, (P, 1)))
    tok = np.arange(B)[None, :, None] * TOK + r[:, None, None] * TILES + np.arange(TILES)[None, None, :]
    put(1, "slot1", (2.0 * tok + 1).reshape(P, -1))
    return np.concatenate(parts[0], 1), np.concatenate(parts[1], 1)


EARLY, LATE = _constants()


class Named(dict):

    def __getattr__(self, name):
        return self[name]


def const(cst, name):
    at, n = CONST[name]
    return cst[:, at:at + n]


def need(eng, sem, count):
    if isinstance(count, int) and count <= 0:
        return
    eng.wait_ge(sem, count)


def pipelined(eng, steps, depth, body):
    for m in range(depth):
        body(m, lambda k, m=m: m - k >= 0)
    with eng.Fori(depth, steps) as m:
        body(m, lambda k: True)
    for m in range(steps, steps + depth - 1):
        body(m, lambda k, m=m: m - k < steps)


def pipelined_by_two(eng, steps, depth, body):
    for m in range(depth):
        body(m, m % 2, lambda k, m=m: m - k >= 0)
    with eng.Fori(depth // 2, steps // 2) as turn:
        for odd in range(2):
            body(2 * turn + odd, odd, lambda k: True)
    for m in range(steps, steps + depth - 1):
        body(m, m % 2, lambda k, m=m: m - k < steps)


def agent_attention(nc, cst, resid, ones16, x, coalition, masks, emb_W, Wq, bq, Wk, bk, Wv, bv, Wo, bo, consts):
    with ExitStack() as ctx:
        def sb(name, shape, dt=F32):
            return ctx.enter_context(nc.sbuf_tensor(name, shape, dt))

        def sem(name):
            return ctx.enter_context(nc.semaphore(name))

        x_tok = x.rearrange("b a (tl j) c -> b (a tl) (j c)", j=TILES)

        arena = sb("arena", [P, 2 * 2 * 2 * TOK * H], F16)
        gxb = arena[:, 0:4 * 2 * TOK].bitcast(F32).rearrange("p (n c) -> p n c", n=4)
        carved = [4 * 2 * TOK]

        def carve(shape, dt=F32):
            n = int(np.prod(shape[1:])) * 2
            at = carved[0]
            carved[0] += n
            ap = arena[0:shape[0], at:at + n].bitcast(dt)
            if len(shape) == 3:
                ap = ap.rearrange("p (m n) -> p m n", m=shape[1])
            return ap

        ident, group, block8 = const(cst, "ident"), const(cst, "group"), const(cst, "block8")
        wstage = carve([P, 4, C])
        w_f = carve([P, 4, C])
        w_hl = sb("w_hl", [P, 2, 4, C], F16)
        bias0 = sb("bias0", [P, 4])
        bo_row = sb("bo_row", [1, C])
        brow = sb("brow", [1, C])
        bo_hl = sb("bo_hl", [64, TOK], F16)
        emb16 = sb("emb16", [A, C])
        embT = sb("embT", [P, A])
        coal = sb("coal", [A, 1], I32)
        shift = sb("shift", [P, B, A])
        gst6 = carve([P, B, 6])
        gstat = carve([P, B, 2])
        gsum = carve([P, 2, B])
        gmean = carve([P, 2, B])
        gtmp = carve([P, 2, B])
        half = carve([P, B])
        rstd = sb("rstd", [P, B])
        nmr = carve([P, B])
        mraw = carve([S * A, A], I32)
        mflt = carve([S * A, A])
        mrep = carve([S * A, H, A])
        mkq = carve([P, S, A])
        msum = sb("msum", [P, A, SP_])
        mspread = sb("mspread", [P, A // 2, P])
        bd = arena[:].rearrange("p (n u l g h q) -> p n u l g h q", n=2, u=2, l=2, h=H, q=A)
        bdq, bdp = bd[:, 0], bd[:, 1]
        xb = sb("xb", [P, 2, TOK])
        xi = sb("xi", [P, 2, TOK])
        xhl = sb("xhl", [P, 2, 2, TOK], F16)
        t32 = sb("t32", [P, 4, TOK])
        qhl = sb("qhl", [P, 2, 2, TOK], F16)
        khl = sb("khl", [P, 2, 2, TOK], F16)
        vhl = sb("vhl", [P, 6, 2, TOK], F16)
        sm = sb("sm", [P, 2, TOK])
        rmax = sb("rmax", [P, 2, T])
        pt = sb("pt", [P, 2, TOK])
        phl = sb("phl", [P, 2, 2, TOK], F16)
        recip = sb("recip", [P, A // 2, 2 * TILES * H])
        o32 = sb("o32", [P, 2, TOK])
        othl = sb("othl", [P, 2, 2, TOK], F16)

        ps = ctx.enter_context(nc.psum_tensor("ps", [P, 8, TOK], F32))
        bank_xy, bank_q, bank_k, bank_vo, bank_s, bank_t, bank_d = (ps[:, n, :] for n in range(7))

        s = Named({n: sem(n) for n in """
            consts_in weights_in masks_in coal_in emb_in resid_in gx0_in gx1_in gx2_in gx3_in x0_in x1_in
            setup_v spread_done half_set setup_pe gT_psum gst_done gvar_done gsum_done gmean_psum rstd_done shift_done
            xT_psum xi_done xh_done xl_done q_psum k_psum v_psum q32_done qh_done ql_done k32_done kh_done
            kl_done v32_done vh_done vl_done bdq_done s_psum rmax_done sm_done e_done et_psum et_done d_psum
            recip_done w_psum p_done ph_done pl_done bdp_done o_psum o32_done ot_psum ot32_done oth_done
            otl_done y_psum x1_done out_done""".split()})
        gx_in, x_in = [s.gx0_in, s.gx1_in, s.gx2_in, s.gx3_in], [s.x0_in, s.x1_in]

        block = ctx.enter_context(nc.Block())

        @block.sync
        def _(sp):
            sp.dma_start(cst[:], consts).then_inc(s.consts_in, 16)
            sp.dma_start(coal[:], coalition.rearrange("(a o) -> a o", o=1)).then_inc(s.coal_in, 16)
            sp.dma_start(mraw[:], masks.rearrange("s q k -> (s q) k")).then_inc(s.masks_in, 16)
            for n, w in enumerate((Wq, Wk, Wv, Wo)):
                sp.dma_start(wstage[:, n, :], w).then_inc(s.weights_in, 16)
            for n, v in enumerate((bq, bk, bv)):
                sp.dma_start(bias0[:, n:n + 1], v.rearrange("(c o) -> c o", o=1)).then_inc(s.weights_in, 16)
            sp.dma_start(bo_row[:], bo.rearrange("(o c) -> o c", o=1)).then_inc(s.weights_in, 16)

            def first_pass(m):
                for u in range(4):
                    need(sp, s.gT_psum, 4 * m + u - 3)
                    sp.dma_start(gxb[:, u, :], x_tok[4 * m + u]).then_inc(gx_in[u], 16)
            first_pass(0)
            with sp.Fori(1, B // 4) as m:
                first_pass(m)

            def second_pass(m):
                for u in range(2):
                    need(sp, s.xT_psum, 2 * m + u - 1)
                    sp.dma_start(xb[:, u, :], x_tok[2 * m + u]).then_inc(x_in[u], 16)
            second_pass(0)
            with sp.Fori(0, B) as b:
                sp.dma_start(resid[:, b, :], x_tok[b]).then_inc(s.resid_in, 16)
            with sp.Fori(1, PAIRS) as m:
                second_pass(m)

        @block.gpsimd
        def _(pool):
            g = nc.gpsimd
            g.memset(half[:], -0.5).then_inc(s.half_set, 1)
            pool.wait_ge(s.coal_in, 16)
            g.indirect_dma_start(emb16[:], None, emb_W, bass.IndirectOffsetOnAxis(ap=coal[:], axis=0)).then_inc(s.emb_in, 16)
            pool.wait_ge(s.half_set, 1)
            pool.wait_ge(s.gvar_done, 1)
            g.tensor_tensor(rstd[:], gtmp[:, 1, :], half[:], ALU.pow).then_inc(s.rstd_done, 1)

            def low(dst, full, high, full_done, high_done, done, n, free, freed):
                need(pool, full_done, n + 1)
                need(pool, high_done, n + 1)
                need(pool, free, freed)
                g.tensor_tensor(dst, full, high, ALU.subtract).then_inc(done, 1)

            def xl(b, u):
                low(xhl[:, u, 1, :], xi[:, u, :], xhl[:, u, 0, :], s.xi_done, s.xh_done, s.xl_done, b, s.v_psum, b - 1)

            def pl(d, u):
                low(phl[:, u, 1, :], pt[:, u, :], phl[:, u, 0, :], s.p_done, s.ph_done, s.pl_done, d, s.bdp_done, d - 1)

            def ql_kl(b, u):
                low(qhl[:, u, 1, :], t32[:, 0, :], qhl[:, u, 0, :], s.q32_done, s.qh_done, s.ql_done, b, s.bdq_done, b - 1)
                low(khl[:, u, 1, :], t32[:, 1, :], khl[:, u, 0, :], s.k32_done, s.kh_done, s.kl_done, b, s.s_psum, b - 1)

            def vl(b, u):
                slot = b % 6
                low(vhl[:, slot, 1, :], t32[:, 2, :], vhl[:, slot, 0, :], s.v32_done, s.vh_done, s.vl_done, b, s.o_psum, b - 5)

            def otl(e, u):
                low(othl[:, u, 1, :], t32[:, 3, :], othl[:, u, 0, :], s.ot32_done, s.oth_done, s.otl_done, e, s.y_psum, e - 1)

            def body(m, on):
                b, d, e = 2 * m, 2 * m - 4, 2 * m - 6
                for u in range(2):
                    if on(0):
                        xl(b + u, u)
                for u in range(2):
                    if on(2):
                        pl(d + u, u)
                if on(0):
                    ql_kl(b, 0)
                    vl(b, 0)
                if on(3):
                    otl(e, 0)
                if on(0):
                    ql_kl(b + 1, 1)
                    vl(b + 1, 1)
                if on(3):
                    otl(e + 1, 1)
            pipelined(pool, PAIRS, 4, body)

        @block.scalar
        def _(act):
            a = nc.scalar

            def xh(b, u):
                need(act, s.xi_done, b + 1)
                need(act, s.v_psum, b - 1)
                need(act, s.xl_done, b - 1)
                a.activation(xhl[:, u, 0, :], xi[:, u, :], ACT.Copy).then_inc(s.xh_done, 1)

            def exp(c, u):
                need(act, s.sm_done, c + 1)
                a.activation(sm[:, u, :], sm[:, u, :], ACT.Exp, scale=HD ** -0.5).then_inc(s.e_done, 1)

            def ph(d, u):
                need(act, s.p_done, d + 1)
                need(act, s.bdp_done, d - 1)
                need(act, s.pl_done, d - 1)
                a.activation(phl[:, u, 0, :], pt[:, u, :], ACT.Copy).then_inc(s.ph_done, 1)

            def o(e, u):
                need(act, s.o_psum, e + 1)
                need(act, s.ot_psum, e - 1)
                a.activation(o32[:, u, :], bank_vo, ACT.Copy, scale=1.0 / S).then_inc(s.o32_done, 1)

            def et(c, u):
                need(act, s.et_psum, c + 1)
                need(act, s.ph_done, c - 1)
                need(act, s.pl_done, c - 1)
                a.activation(pt[:, u, :], bank_t, ACT.Copy).then_inc(s.et_done, 1)

            def project(bank, n, bias, psum, low_done, full_done, dst, high_done, b, free, freed):
                need(act, psum, b + 1)
                need(act, low_done, b)
                need(act, free, freed)
                if bias is None:
                    a.activation(t32[:, n, :], bank, ACT.Copy, scale=1.0 / WS).then_inc(full_done, 1)
                    a.activation(dst, bank, ACT.Copy, scale=1.0 / WS).then_inc(high_done, 1)
                else:
                    a.activation(t32[:, n, :], bank, ACT.Identity, bias=bias, scale=1.0 / WS).then_inc(full_done, 1)
                    a.activation(dst, bank, ACT.Identity, bias=bias, scale=1.0 / WS).then_inc(high_done, 1)

            def q_k(b, u):
                project(bank_q, 0, bias0[:, 0:1], s.q_psum, s.ql_done, s.q32_done, qhl[:, u, 0, :], s.qh_done, b,
                        s.bdq_done, b - 1)
                project(bank_k, 1, bias0[:, 1:2], s.k_psum, s.kl_done, s.k32_done, khl[:, u, 0, :], s.kh_done, b,
                        s.s_psum, b - 1)

            def v(b, u):
                project(bank_vo, 2, None, s.v_psum, s.vl_done, s.v32_done, vhl[:, b % 6, 0, :], s.vh_done, b,
                        s.o_psum, b - 5)

            def ot(e, u):
                need(act, s.ot_psum, e + 1)
                need(act, s.otl_done, e)
                need(act, s.y_psum, e - 1)
                src = bank_t.rearrange("p (t j q) -> p j q t", j=TILES, q=A)
                a.activation(t32[:, 3, :].rearrange("p (j q t) -> p j q t", j=TILES, q=A), src, ACT.Copy).then_inc(s.ot32_done, 1)
                a.activation(othl[:, u, 0, :].rearrange("p (j q t) -> p j q t", j=TILES, q=A), src, ACT.Copy).then_inc(s.oth_done, 1)

            act.wait_ge(s.weights_in, 16 * 8)

            def body(m, on):
                b, c, d, e = 2 * m, 2 * m - 2, 2 * m - 4, 2 * m - 6
                if on(0):
                    xh(b, 0)
                if on(1):
                    exp(c, 0)
                if on(0):
                    xh(b + 1, 1)
                if on(2):
                    ph(d, 0)
                if on(1):
                    exp(c + 1, 1)
                if on(2):
                    ph(d + 1, 1)
                if on(3):
                    o(e, 0)
                if on(1):
                    et(c, 0)
                if on(0):
                    q_k(b, 0)
                if on(3):
                    o(e + 1, 1)
                if on(1):
                    et(c + 1, 1)
                if on(0):
                    v(b, 0)
                if on(3):
                    ot(e, 0)
                if on(0):
                    q_k(b + 1, 1)
                    v(b + 1, 1)
                if on(3):
                    ot(e + 1, 1)
            pipelined(act, PAIRS, 4, body)

        @block.tensor
        def _(pe):
            t = nc.tensor

            def first(m):
                for u in range(4):
                    pe.wait_ge(gx_in[u], 16 * (m + 1))
                    need(pe, s.gst_done, 4 * m + u - 3)
                    for j in range(TILES):
                        last = t.transpose(ps[:, u, j * P:(j + 1) * P], gxb[:, u, j * P:(j + 1) * P], ident)
                    last.then_inc(s.gT_psum, 1)
            pe.wait_ge(s.consts_in, 16)
            first(0)
            pe.wait_ge(s.setup_v, 4)
            t.matmul(ps[:, 4, 0:S * A], mrep[:], ident[0:S * A, 0:S * A], start=True, stop=True).then_inc(s.setup_pe, 1)
            pe.wait_ge(s.emb_in, 16)
            t.transpose(ps[:, 5, 0:A], emb16[:], ident[0:A, 0:A]).then_inc(s.setup_pe, 1)
            pe.wait_ge(s.weights_in, 16 * 8)
            t.matmul(ps[0:1, 6, 0:C], bias0[:, 2:3], wstage[:, 3, :], start=True, stop=True).then_inc(s.setup_pe, 1)
            with pe.Fori(1, B // 4) as m:
                first(m)
            pe.wait_ge(s.setup_v, TABLE_STEP)
            pe.wait_ge(s.gst_done, B)
            for q in range(A):
                last = t.transpose(ps[0:SP_, q // 4, (q % 4) * P:(q % 4 + 1) * P], msum[:, q, :], ident)
            last.then_inc(s.setup_pe, 1)
            pe.wait_ge(s.gsum_done, 1)
            t.matmul(ps[:, 7, 0:2 * B], group, gsum[:].rearrange("p n b -> p (n b)"), start=True, stop=True).then_inc(s.gmean_psum, 1)
            pe.wait_ge(s.spread_done, 1)

            def xT(b, u):
                need(pe, x_in[u], 16 * (b // 2 + 1) if isinstance(b, int) else 8 * (b - u + 2))
                need(pe, s.xi_done, b)
                need(pe, s.x1_done, b - 6 - u)
                for j in range(TILES):
                    last = t.transpose(bank_xy.rearrange("p (n j) -> p j n", j=TILES)[:, j, :], xb[:, u, j * P:(j + 1) * P], ident)
                last.then_inc(s.xT_psum, 1)

            def qk(c, u):
                need(pe, s.bdq_done, c + 1)
                need(pe, s.kl_done, c + 1)
                need(pe, s.sm_done, c)
                for n in range(T):
                    o, k = bank_s[:, n * A:(n + 1) * A], khl[:, u, :, n * A:(n + 1) * A]
                    t.matmul(o, bdq[:, u, 0, n], k[:, 0, :], start=True, stop=False)
                    t.matmul(o, bdq[:, u, 0, n], k[:, 1, :], start=False, stop=False)
                    last = t.matmul(o, bdq[:, u, 1, n], k[:, 0, :], start=False, stop=True)
                last.then_inc(s.s_psum, 1)

            def products(out, lhs, rhs, start=True, stop=True):
                t.matmul(out, lhs[0], rhs[0], start=start, stop=False)
                t.matmul(out, lhs[0], rhs[1], start=False, stop=False)
                return t.matmul(out, lhs[1], rhs[0], start=False, stop=stop)

            def q_k(b, u):
                need(pe, s.xl_done, b + 1)
                x2 = [xhl[:, u, l, :] for l in range(2)]
                need(pe, s.qh_done, b)
                products(bank_q, [w_hl[:, l, 0, :] for l in range(2)], x2).then_inc(s.q_psum, 1)
                need(pe, s.kh_done, b)
                products(bank_k, [w_hl[:, l, 1, :] for l in range(2)], x2).then_inc(s.k_psum, 1)

            def v(b, u, on3, e):
                need(pe, s.vh_done, b)
                if on3:
                    need(pe, s.o32_done, e + 2)
                for j in range(TILES):
                    last = products(bank_vo[:, j * P:(j + 1) * P], [xhl[:, u, l, j * P:(j + 1) * P] for l in range(2)],
                                    [w_hl[:, l, 2, :] for l in range(2)])
                last.then_inc(s.v_psum, 1)

            def et(c, u):
                need(pe, s.e_done, c + 1)
                need(pe, s.et_done, c)
                if u == 0:
                    need(pe, s.oth_done, c - 4)
                for j in range(TILES):
                    last = t.transpose(bank_t[:, j * P:(j + 1) * P], sm[:, u, j * P:(j + 1) * P], ident)
                last.then_inc(s.et_psum, 1)

            def sums(m1, on2):
                need(pe, s.et_done, 2 * m1 + 2)
                if on2:
                    need(pe, s.p_done, 2 * m1)
                e4 = pt[:].rearrange("p u (g q) -> p q u g", q=A)
                for q in range(A):
                    lo = SP_ * (q % 2)
                    dst = bank_d[lo:lo + SP_, (q // 2) * 64:(q // 2 + 1) * 64]
                    last = t.matmul(dst, msum[:, q, :], e4[:, q], start=True, stop=True)
                last.then_inc(s.d_psum, 1)

            def weights(m2):
                need(pe, s.recip_done, m2 + 1)
                need(pe, s.p_done, 2 * m2)
                for q in range(A):
                    lo = SP_ * (q % 2)
                    last = t.matmul(ps[:, 6 + q % 2, (q // 2) * 64:(q // 2 + 1) * 64], mspread[lo:lo + S * 8, q // 2, :],
                                    recip[lo:lo + S * 8, q // 2, :], start=True, stop=True)
                last.then_inc(s.w_psum, 1)

            def pv(e, u):
                need(pe, s.bdp_done, e + 1)
                if u:
                    need(pe, s.o32_done, e)
                else:
                    need(pe, s.vh_done, min(e + 6, B) if isinstance(e, int) else e + 6)
                    need(pe, s.vl_done, e + 2)
                slot = e % 6
                for j in range(TILES):
                    for h in range(H):
                        n = j * H + h
                        last = products(bank_vo[:, n * HD:(n + 1) * HD], [bdp[:, u, l, n] for l in range(2)],
                                        [vhl[:, slot, l, n * HD:(n + 1) * HD] for l in range(2)])
                last.then_inc(s.o_psum, 1)

            def ot(e, u, on1):
                need(pe, s.o32_done, e + 1)
                need(pe, s.oth_done, e)
                if on1 and u == 0:
                    need(pe, s.et_done, e + 6)
                for j in range(TILES):
                    last = t.transpose(bank_t[:, j * P:(j + 1) * P], o32[:, u, j * P:(j + 1) * P], ident)
                last.then_inc(s.ot_psum, 1)

            def y(e, u, on0):
                need(pe, s.otl_done, e + 1)
                need(pe, s.x1_done, e)
                if on0 and u == 0:
                    need(pe, s.xi_done, e + 8)
                t.matmul(bank_xy, ones16[0:64, :], bo_hl[:], start=True, stop=False)
                for j in range(TILES):
                    o = bank_xy[:, j * P:(j + 1) * P]
                    last = products(o, [othl[:, u, l, j * P:(j + 1) * P] for l in range(2)],
                                    [w_hl[:, l, 3, :] for l in range(2)], start=False, stop=j == TILES - 1)
                last.then_inc(s.y_psum, 1)

            def body(m, on):
                b, c, d, e = 2 * m, 2 * m - 2, 2 * m - 4, 2 * m - 6
                if on(0):
                    xT(b, 0)
                if on(1):
                    qk(c, 0)
                if on(0):
                    xT(b + 1, 1)
                if on(2):
                    weights(m - 2)
                if on(1):
                    qk(c + 1, 1)
                if on(3):
                    pv(e, 0)
                if on(1):
                    et(c, 0)
                if on(3):
                    pv(e + 1, 1)
                if on(0):
                    q_k(b, 0)
                if on(1):
                    et(c + 1, 1)
                if on(0):
                    v(b, 0, on(3), e)
                if on(1):
                    sums(m - 1, on(2))
                if on(3):
                    ot(e, 0, on(1))
                if on(0):
                    q_k(b + 1, 1)
                    v(b + 1, 1, on(3), e)
                if on(3):
                    ot(e + 1, 1, on(1))
                    y(e, 0, on(0))
                    y(e + 1, 1, on(0))
            pipelined(pe, PAIRS, 4, body)

        @block.vector
        def _(dve):
            v = nc.vector
            steps = [0]

            def step(ins):
                ins.then_inc(s.setup_v, 1)
                steps[0] += 1
                dve.wait_ge(s.setup_v, steps[0])

            dve.wait_ge(s.consts_in, 16)
            dve.wait_ge(s.masks_in, 16)
            step(v.memset(ones16[:], 1.0))
            step(v.tensor_scalar(mflt[:], mraw[:], 0.0, None, ALU.is_gt))
            step(v.tensor_tensor(mflt[:], mflt[:], const(cst, "eye_qk")[0:S * A, :], ALU.max))
            step(v.tensor_copy(mrep[:], mflt[:].rearrange("p (o k) -> p o k", o=1).to_broadcast([S * A, H, A])))
            step(v.memset(bo_hl[:], 0.0))
            dve.wait_ge(s.weights_in, 16 * 8)
            step(v.tensor_scalar(w_f[:], wstage[:], WS, None, ALU.mult))
            step(v.tensor_copy(w_hl[:, 0], w_f[:]))
            step(v.tensor_tensor(w_hl[:, 1], w_f[:], w_hl[:, 0], ALU.subtract))
            dve.wait_ge(s.setup_pe, 1)
            step(v.tensor_copy(mkq[:].rearrange("p s q -> p (s q)"), ps[:, 4, 0:S * A]))
            for n in range(8):
                step(v.tensor_scalar(msum[:, :, n * S:(n + 1) * S], mkq[:].rearrange("p s q -> p q s"),
                                     block8[:, n:n + 1], None, ALU.mult))
            step(v.tensor_copy(msum[:, :, 8 * S:SP_], msum[:, :, 0:SP_ - 8 * S]))
            dve.wait_ge(s.setup_pe, 2)
            step(v.tensor_copy(embT[:], ps[:, 5, 0:A]))
            dve.wait_ge(s.setup_pe, 3)
            step(v.tensor_tensor(brow[:], ps[0:1, 6, 0:C], bo_row[:], ALU.add))
            step(v.tensor_scalar(brow[:], brow[:], WS, None, ALU.mult))
            row = brow[:].rearrange("p (o c) -> p o c", o=1).to_broadcast([1, TILES, C])
            hi, lo = (bo_hl[r:r + 1, :].rearrange("p (o c) -> p o c", o=TILES) for r in (0, 32))
            step(v.tensor_copy(hi, row))
            step(v.tensor_copy(lo, row))
            step(v.tensor_tensor(brow[:], brow[:], bo_hl[0:1, 0:C], ALU.subtract))
            step(v.tensor_copy(lo, row))

            with dve.Fori(0, B // 4) as m:
                for u in range(4):
                    dve.wait_ge(s.gT_psum, 4 * m + u + 1)
                    v.bn_stats(gst6[:, 4 * m + u, :], ps[:, u, :]).then_inc(s.gst_done, 1)
            dve.wait_ge(s.gst_done, B)
            even, dev_even, odd, dev_odd = (gst6[:, :, n] for n in (1, 2, 4, 5))
            step(v.tensor_tensor(gtmp[:, 0, :], even, even, ALU.mult))
            step(v.tensor_tensor(gtmp[:, 1, :], odd, odd, ALU.mult))
            step(v.tensor_tensor(gtmp[:, 1, :], gtmp[:, 0, :], gtmp[:, 1, :], ALU.add))
            step(v.tensor_tensor(gtmp[:, 0, :], dev_even, dev_odd, ALU.add))
            step(v.scalar_tensor_tensor(gsum[:, 1, :], gtmp[:, 0, :], 2.0 / TOK, gtmp[:, 1, :], ALU.mult, ALU.add))
            v.tensor_tensor(gsum[:, 0, :], even, odd, ALU.add).then_inc(s.gsum_done, 1)
            dve.wait_ge(s.setup_pe, 4)
            for q4 in range(4):
                src = ps[0:SP_, q4, :].rearrange("p (n r c) -> p n r c", n=2, r=2)
                for r in range(2):
                    ins = v.tensor_copy(mspread[SP_ * r:SP_ * (r + 1), 2 * q4:2 * q4 + 2, :], src[:, :, r, :])
            ins.then_inc(s.spread_done, 1)
            dve.wait_ge(s.spread_done, 1)
            dve.wait_ge(s.gmean_psum, 1)
            v.tensor_copy(gmean[:].rearrange("p n b -> p (n b)"), ps[:, 7, 0:2 * B]).then_inc(s.gst_done, 1)
            dve.wait_ge(s.gst_done, B + 1)
            step(v.tensor_tensor(gtmp[:, 0, :], gmean[:, 0, :], gmean[:, 0, :], ALU.mult))
            v.scalar_tensor_tensor(gtmp[:, 1, :], gmean[:, 1, :], GN_EPS, gtmp[:, 0, :], ALU.add, ALU.subtract).then_inc(s.gvar_done, 1)
            dve.wait_ge(s.rstd_done, 1)
            step(v.scalar_tensor_tensor(nmr[:], gmean[:, 0, :], -1.0, rstd[:], ALU.mult, ALU.mult))
            step(v.tensor_tensor(shift[:], embT[:].rearrange("p (o a) -> p o a", o=1).to_broadcast([P, B, A]),
                                 nmr[:].rearrange("p (b o) -> p b o", o=1).to_broadcast([P, B, A]), ALU.add))

            def xi_(b, u):
                need(dve, s.xT_psum, b + 1)
                need(dve, s.xl_done, b - 1)
                need(dve, s.xh_done, b - 1)
                v.scalar_tensor_tensor(xi[:, u, :].rearrange("p (t a) -> p t a", a=A), bank_xy.rearrange("p (a t) -> p t a", a=A),
                                       rstd[:, bass.ds(b, 1)],
                                       shift[:, bass.ds(b, 1), :].to_broadcast([P, T, A]), ALU.mult, ALU.add).then_inc(s.xi_done, 1)

            def shifted(c, u):
                need(dve, s.s_psum, c + 1)
                s3 = bank_s.rearrange("p (t k) -> p t k", k=A)
                v.tensor_reduce(rmax[:, u, :], s3, AX.X, ALU.max).then_inc(s.rmax_done, 1)
                need(dve, s.rmax_done, c + 1)
                need(dve, s.et_psum, c - 1)
                v.tensor_tensor(sm[:, u, :].rearrange("p (t k) -> p t k", k=A), s3,
                                rmax[:, u, :].rearrange("p (t o) -> p t o", o=1).to_broadcast([P, T, A]), ALU.subtract).then_inc(s.sm_done, 1)

            def p(d, u, m2):
                need(dve, s.w_psum, m2 + 1)
                w = ps[:, 6:8, :].rearrange("p r (n u g) -> p u g n r", n=A // 2, u=2)[:, u]
                e4 = pt[:, u, :].rearrange("p (g n r) -> p g n r", n=A // 2, r=2)
                v.tensor_tensor(e4, e4, w, ALU.mult).then_inc(s.p_done, 1)

            def spread(dst, src, ready, free, freed, done):
                for sem_, count in ready:
                    need(dve, sem_, count)
                need(dve, free, freed)
                for n in range(8):
                    ins = v.tensor_scalar(dst[:, :, :, n, :], src.rearrange("p l (g q) -> p l g q", q=A), block8[:, n:n + 1], None, ALU.mult)
                ins.then_inc(done, 1)

            def add(e, u):
                need(dve, s.y_psum, e + 1)
                r = resid[:, e, :]
                v.scalar_tensor_tensor(r, bank_xy, 1.0 / WS, r, ALU.mult, ALU.add).then_inc(s.x1_done, 1)

            def body(m, on):
                b, c, d, e = 2 * m, 2 * m - 2, 2 * m - 4, 2 * m - 6
                if on(0):
                    xi_(b, 0)
                if on(1):
                    shifted(c, 0)
                if on(0):
                    xi_(b + 1, 1)
                if on(2):
                    p(d, 0, m - 2)
                if on(1):
                    shifted(c + 1, 1)
                if on(2):
                    p(d + 1, 1, m - 2)
                    spread(bdp[:, 0], phl[:, 0], [(s.ph_done, d + 1), (s.pl_done, d + 1)], s.o_psum, d - 1, s.bdp_done)
                if on(2):
                    spread(bdp[:, 1], phl[:, 1], [(s.ph_done, d + 2), (s.pl_done, d + 2)], s.o_psum, d, s.bdp_done)
                if on(1):
                    need(dve, s.d_psum, m)
                    need(dve, s.w_psum, m - 1)
                    v.reciprocal(recip[:].rearrange("p n g -> p (n g)"), bank_d).then_inc(s.recip_done, 1)
                if on(0):
                    spread(bdq[:, 0], qhl[:, 0], [(s.qh_done, b + 1), (s.ql_done, b + 1)], s.s_psum, b - 1, s.bdq_done)
                if on(3):
                    if isinstance(m, int) and m == 3:
                        pass
                    add(e, 0)
                if on(0):
                    spread(bdq[:, 1], qhl[:, 1], [(s.qh_done, b + 2), (s.ql_done, b + 2)], s.s_psum, b, s.bdq_done)
                if on(3):
                    add(e + 1, 1)
            dve.wait_ge(s.resid_in, 16 * B)
            pipelined(dve, PAIRS, 4, body)


def chain(eng, sem, base):
    done = [0]

    def step(ins, wait=True):
        ins.then_inc(sem, 1)
        done[0] += 1
        if wait:
            eng.wait_ge(sem, base + done[0])
    return step


def token_mixer(nc, cst, resid, ones16, ident, late, ffn, rows_dram, Wq, bq, Wk, bk, Wv, bv, router_w, router_b,
                gate_up, gate_up_bias, down, down_bias):
    rank_of = const(cst, "rank_of")
    w1_hl, b1_hl, w2_hl, b2_hl = ffn["w1_hl"], ffn["b1_hl"], ffn["w2_hl"], ffn["b2_hl"]
    with ExitStack() as ctx:
        def sb(name, shape, dt=F32):
            return ctx.enter_context(nc.sbuf_tensor(name, shape, dt))

        wq = sb("m_wq", [P, C])
        wkv = sb("m_wkv", [P, 2, C])
        wr = sb("m_wr", [P, E])
        bq_col = sb("m_bq", [P, 1])
        bkv_f = sb("m_bkv_f", [1, 2, C])
        bkv_t = sb("m_bkv_t", [1, 2, C])
        bkv_hl = sb("m_bkv_hl", [64, 2, 2 * C], F16)
        rb = sb("m_rb", [P, E])
        w1_f = sb("m_w1_f", [P, E, 2 * I])
        w2_f = sb("m_w2_f", [P, E, 2, C])
        b1_f = sb("m_b1_f", [1, E * 2 * I])
        b2_f = sb("m_b2_f", [1, E * C])
        before16 = sb("m_before16", [P, P], F16)
        half = sb("m_half", [P, 8])
        st6 = sb("m_st6", [P, 2, 8, 6])
        stw = sb("m_stw", [P, 2, 6, 8])
        xn = sb("m_xn", [P, 2, TOK])
        xt = sb("m_xt", [P, 2, TOK])
        ef = sb("m_ef", [P, 2, TOK])
        rf = sb("m_rf", [P, 2, TOK])
        qf = sb("m_qf", [P, 2, TOK])
        kf = sb("m_kf", [P, 2, TOK])
        vo = sb("m_vo", [P, 2, TILES, C + 2])
        kv = sb("m_kv", [P, 2, C + H])
        den = sb("m_den", [P, 2, TILES, H])
        mix = sb("m_mix", [P, TOK])
        xn2 = sb("m_xn2", [P, 2, TOK])
        xt2 = sb("m_xt2", [P, 2, TOK])
        rows = sb("m_rows", [P, 4, TILES, ROW])
        place = sb("m_place", [P, 4, TILES, 2], I32)
        lg = sb("m_lg", [P, 8, E])
        oh = sb("m_oh", [P, 2, 8, E])
        tmp = sb("m_tmp", [P, 2, 8, E])
        best = sb("m_best", [P, 8, 8])
        oh16 = sb("m_oh16", [P, 8, E], F16)
        ahead16 = sb("m_ahead16", [P, 9, E], F16)
        spot = sb("m_spot", [P, 8, E])

        ps = ctx.enter_context(nc.psum_tensor("m_ps", [P, 8, TOK], F32))
        bank_x, bank_q, banks_kv, bank_s, banks_o, bank_r = ps[:, 0], ps[:, 1], ps[:, 2:4], ps[:, 4], ps[:, 5:7], ps[:, 7]

        s = Named({n: ctx.enter_context(nc.semaphore("m_" + n)) for n in """
            small_in w1_in w2_in b_in set_v set_a set_g kv_bias w1f_done w1h_done
            stat1 stat2 pow1 pow2 norm1 xT xt_done q_psum kv_psum qe_done ke_done v_done qf_done kf_done
            s_psum kv_done o_psum mix_step add_done norm2 hi_done lo_done xT2 xt2_done lg_psum route ew_done
            rank_psum place_step place_done rows_out table late_in""".split()})

        block = ctx.enter_context(nc.Block())

        @block.sync
        def _(sp):
            sp.dma_start(cst[:], late).then_inc(s.late_in, 16)
            sp.dma_start(wq[:], Wq).then_inc(s.small_in, 16)
            sp.dma_start(wkv[:, 0, :], Wk).then_inc(s.small_in, 16)
            sp.dma_start(wkv[:, 1, :], Wv).then_inc(s.small_in, 16)
            sp.dma_start(wr[:], router_w).then_inc(s.small_in, 16)
            sp.dma_start(bq_col[:], bq.rearrange("(c o) -> c o", o=1)).then_inc(s.small_in, 16)
            sp.dma_start(bkv_f[:, 0, :], bk.rearrange("(o c) -> o c", o=1)).then_inc(s.small_in, 16)
            sp.dma_start(bkv_f[:, 1, :], bv.rearrange("(o c) -> o c", o=1)).then_inc(s.small_in, 16)
            sp.dma_start(rb[:], router_b.rearrange("(o e) -> o e", o=1).to_broadcast([P, E])).then_inc(s.small_in, 16)
            sp.dma_start(w1_f[:], gate_up.rearrange("e c i -> c e i")).then_inc(s.w1_in, 16)
            sp.dma_start(w2_f[:], down.rearrange("e (n i) c -> i e n c", n=2)).then_inc(s.w2_in, 16)
            sp.dma_start(b1_f[:], gate_up_bias.rearrange("(o e) i -> o (e i)", o=1)).then_inc(s.b_in, 16)
            sp.dma_start(b2_f[:], down_bias.rearrange("(o e) c -> o (e c)", o=1)).then_inc(s.b_in, 16)

        @block.gpsimd
        def _(pool):
            g = nc.gpsimd
            g.memset(half[:], -0.5).then_inc(s.set_g, 1)
            pool.wait_ge(s.set_g, 1)

            def power(n, k, stat, steps, norm, pow_done):
                pool.wait_ge(stat, steps * (k + 1))
                need(pool, norm, 2 * k)
                g.tensor_tensor(stw[:, n, 5, :], stw[:, n, 4, :], half[:], ALU.pow).then_inc(pow_done, 1)

            def rows_ready(k):
                pool.wait_ge(s.place_done, k + 1)
                pool.wait_ge(s.lo_done, 2 * k + 2)
                need(pool, s.rows_out, 16 * 16 * k)

            def send(slot):
                for j in range(TILES):
                    for n in range(2):
                        g.indirect_dma_start(rows_dram, bass.IndirectOffsetOnAxis(ap=place[:, slot, j, n:n + 1], axis=0),
                                             rows[:, slot, j, :], None).then_inc(s.rows_out, 16)

            def body(m, odd, on):
                if on(0):
                    power(0, m, s.stat1, LN_STEPS, s.norm1, s.pow1)
                if on(5):
                    rows_ready(m - 5)
                if on(3):
                    power(1, m - 3, s.stat2, LN_STEPS, s.norm2, s.pow2)
                if on(5):
                    send(2 * (1 - odd))
                    send(2 * (1 - odd) + 1)
            pipelined_by_two(pool, PAIRS, 6, body)
            pool.wait_ge(s.rows_out, 16 * 16 * PAIRS)

        @block.scalar
        def _(act):
            a = nc.scalar
            act.wait_ge(s.small_in, 16 * 8)
            act.wait_ge(s.w1_in, 16)
            a.activation(w1_f[:], w1_f[:], ACT.Copy, scale=2 * WS).then_inc(s.w1f_done, 1)
            act.wait_ge(s.w2_in, 16)
            a.activation(w2_f[:], w2_f[:], ACT.Copy, scale=WS).then_inc(s.w1f_done, 1)
            act.wait_ge(s.w1f_done, 2)
            a.activation(w1_hl[:, :, 0, :], w1_f[:], ACT.Copy).then_inc(s.w1h_done, 1)
            a.activation(w2_hl[:, :, 0], w2_f[:], ACT.Copy).then_inc(s.w1h_done, 1)

            def xt_(b, u):
                need(act, s.xT, b + 1)
                need(act, s.kv_psum, b - 1)
                a.activation(xt[:, u, :], bank_x, ACT.Copy).then_inc(s.xt_done, 1)

            def q(b, u):
                need(act, s.q_psum, b + 1)
                need(act, s.qf_done, b)
                a.activation(ef[:, 0, :], bank_q, ACT.Exp, bias=bq_col[:]).then_inc(s.qe_done, 1)
                a.activation(rf[:, 0, :], bank_q, ACT.Relu, bias=bq_col[:]).then_inc(s.qe_done, 1)

            def k_v(b, u):
                need(act, s.kv_psum, b + 1)
                need(act, s.kf_done, b)
                kv4 = banks_kv.rearrange("p n (i w c) -> p (n i) w c", i=2, w=2)
                a.activation(ef[:, 1, :].rearrange("p (j c) -> p j c", j=TILES), kv4[:, :, 0, :], ACT.Exp).then_inc(s.ke_done, 1)
                a.activation(rf[:, 1, :].rearrange("p (j c) -> p j c", j=TILES), kv4[:, :, 0, :], ACT.Relu).then_inc(s.ke_done, 1)
                need(act, s.s_psum, b - 1)
                a.activation(vo[:, u, :, 0:C], kv4[:, :, 1, :], ACT.Copy).then_inc(s.v_done, 1)

            def xt2_(d, u):
                need(act, s.xT2, d + 1)
                need(act, s.lg_psum, d - 1)
                a.activation(xt2[:, u, :], bank_r, ACT.Copy).then_inc(s.xt2_done, 1)

            def hi(d, u, k, slot):
                need(act, s.norm2, d + 1)
                need(act, s.rows_out, 16 * 16 * (k - 1))
                dst = rows[:, slot].bitcast(F16)[:, :, 0:C]
                a.activation(dst, xn2[:, u, :].rearrange("p (j c) -> p j c", j=TILES), ACT.Copy).then_inc(s.hi_done, 1)

            def ew(k):
                need(act, s.route, ROUTE_STEPS * k + 13)
                a.activation(best[:, 3, :], best[:, 2, :], ACT.Exp).then_inc(s.ew_done, 1)

            def body(m, odd, on):
                b, d = 2 * m - 2, 2 * m - 8
                if on(1):
                    xt_(b, 0)
                    xt_(b + 1, 1)
                if on(4):
                    hi(d, 0, m - 4, 2 * odd)
                    hi(d + 1, 1, m - 4, 2 * odd + 1)
                    xt2_(d, 0)
                    xt2_(d + 1, 1)
                if on(1):
                    q(b, 0)
                    k_v(b, 0)
                if on(4):
                    ew(m - 4)
                if on(1):
                    q(b + 1, 1)
                    k_v(b + 1, 1)
            pipelined_by_two(act, PAIRS, 6, body)

        @block.tensor
        def _(pe):
            t = nc.tensor
            pe.wait_ge(s.set_v, 11)

            def xT(b, u, m):
                need(pe, s.norm1, b + 1)
                need(pe, s.xt_done, b)
                if u == 0:
                    need(pe, s.place_done, m - 4)
                for j in range(TILES):
                    last = t.transpose(bank_x[:, j * P:(j + 1) * P], xn[:, u, j * P:(j + 1) * P], ident)
                last.then_inc(s.xT, 1)

            def q(b, u):
                need(pe, s.xt_done, b + 1)
                need(pe, s.qe_done, 2 * b)
                t.matmul(bank_q, wq[:], xt[:, u, :], start=True, stop=True).then_inc(s.q_psum, 1)

            def k_v(b, u):
                need(pe, s.v_done, b)
                for n in range(2):
                    t.matmul(banks_kv[:, n], ones16[0:64, :], bkv_hl[:].rearrange("p i c -> p (i c)"), start=True, stop=False)
                    for i in range(2):
                        j = 2 * n + i
                        last = t.matmul(banks_kv[:, n, i * 2 * C:(i + 1) * 2 * C], xt[:, u, j * P:(j + 1) * P],
                                        wkv[:].rearrange("p w c -> p (w c)"), start=False, stop=i == 1)
                last.then_inc(s.kv_psum, 1)

            def sums(c, u):
                need(pe, s.kf_done, c + 1)
                need(pe, s.v_done, c + 1)
                need(pe, s.kv_done, c)
                for j in range(TILES):
                    last = t.matmul(bank_s[:, 0:C + 2], kf[:, u, j * P:(j + 1) * P], vo[:, u, j, :], start=j == 0, stop=j == TILES - 1)
                last.then_inc(s.s_psum, 1)

            def outs(c, u):
                need(pe, s.kv_done, c + 1)
                need(pe, s.qf_done, c + 1)
                need(pe, s.add_done, c)
                for j in range(TILES):
                    last = t.matmul(banks_o[:, j // 2, (j % 2) * 256:(j % 2) * 256 + C + H], qf[:, u, j * P:(j + 1) * P], kv[:, u, :],
                                    start=True, stop=True)
                last.then_inc(s.o_psum, 1)

            def xT2(d, u):
                need(pe, s.norm2, d + 1)
                need(pe, s.xt2_done, d)
                for j in range(TILES):
                    last = t.transpose(bank_r[:, j * P:(j + 1) * P], xn2[:, u, j * P:(j + 1) * P], ident)
                last.then_inc(s.xT2, 1)

            def logits(d, u, k, b_next):
                need(pe, s.xt2_done, d + 1)
                need(pe, s.place_done, k)
                if b_next is not None:
                    need(pe, s.xt_done, b_next)
                for j in range(TILES):
                    n = (u * TILES + j) * E
                    last = t.matmul(bank_x[:, n:n + E], xt2[:, u, j * P:(j + 1) * P], wr[:], start=True, stop=True)
                last.then_inc(s.lg_psum, 1)

            def ranks(k):
                need(pe, s.route, ROUTE_STEPS * k + ROUTE_STEPS)
                flat = bank_x[:, 64:64 + 8 * E]
                t.matmul(flat, before16[:], oh16[:].rearrange("p n e -> p (n e)"), start=True, stop=False)
                t.matmul(flat, ones16[:], ahead16[:, 0:8, :].rearrange("p n e -> p (n e)"), start=False, stop=True).then_inc(s.rank_psum, 1)

            def body(m, odd, on):
                b, c, d = 2 * m - 2, 2 * m - 4, 2 * m - 8
                for u in range(2):
                    if on(1):
                        xT(b + u, u, m)
                    if on(2):
                        sums(c + u, u)
                if on(4):
                    xT2(d, 0)
                    xT2(d + 1, 1)
                for u in range(2):
                    if on(1):
                        q(b + u, u)
                        k_v(b + u, u)
                    if on(2):
                        outs(c + u, u)
                    if on(4) and u == 0:
                        logits(d, 0, m - 4, 2 * m if on(1) else None)
                        logits(d + 1, 1, m - 4, None)
                if on(4):
                    ranks(m - 4)
            pipelined_by_two(pe, PAIRS, 6, body)
            pe.wait_ge(s.place_done, PAIRS)
            t.matmul(bank_s[:, 0:E], ones16[:], ahead16[:, 0, :], start=True, stop=True).then_inc(s.rank_psum, 1)

        @block.vector
        def _(dve):
            v = nc.vector
            dve.wait_ge(s.small_in, 16 * 8)
            dve.wait_ge(s.late_in, 16)
            step = chain(dve, s.set_v, 0)
            step(v.tensor_scalar(wq[:], wq[:], 2.0, None, ALU.mult), False)
            step(v.tensor_scalar(wkv[:], wkv[:], 2.0, None, ALU.mult), False)
            step(v.tensor_scalar(wr[:], wr[:], 2.0, None, ALU.mult), False)
            step(v.memset(bkv_hl[:], 0.0), False)
            step(v.memset(vo[:, :, :, C:C + 1], 1.0), False)
            step(v.memset(vo[:, :, :, C + 1:C + 2], 0.0), False)
            step(v.memset(ahead16[:], 0.0), False)
            step(v.tensor_copy(before16[:], const(cst, "before")))
            row = bkv_f[:].rearrange("p w c -> p (w c)")
            both = row.rearrange("p (o c) -> p o c", o=1).to_broadcast([1, 2, 2 * C])
            step(v.tensor_copy(bkv_hl[0:1], both))
            tmp_row = bkv_t[:].rearrange("p w c -> p (w c)")
            step(v.tensor_tensor(tmp_row, row, bkv_hl[0:1, 0, :], ALU.subtract))
            step(v.tensor_copy(bkv_hl[32:33], tmp_row.rearrange("p (o c) -> p o c", o=1).to_broadcast([1, 2, 2 * C])))
            step(v.memset(b1_hl[:], 0.0), False)
            step(v.memset(b2_hl[:], 0.0))
            dve.wait_ge(s.b_in, 32)
            for f, hl in ((b1_f[:], b1_hl[:].rearrange("p e i -> p (e i)")), (b2_f[:], b2_hl[:].rearrange("p e c -> p (e c)"))):
                step(v.tensor_scalar(f, f, WS, None, ALU.mult))
                step(v.tensor_copy(hl[0:1, :], f))
                step(v.tensor_tensor(f, f, hl[0:1, :], ALU.subtract))
                step(v.tensor_copy(hl[32:33, :], f))
            dve.wait_ge(s.w1h_done, 2)
            step(v.tensor_tensor(w1_hl[:, :, 1, :], w1_f[:], w1_hl[:, :, 0, :], ALU.subtract))
            step(v.tensor_tensor(w2_hl[:, :, 1], w2_f[:], w2_hl[:, :, 0], ALU.subtract))

            def stats(n, b, k, sem):
                step = chain(dve, sem, LN_STEPS * k)
                if n == 1:
                    need(dve, s.add_done, b + 2)
                for u in range(2):
                    for j in range(TILES):
                        ins = v.bn_stats(st6[:, n, u * TILES + j, :], resid[:, b + u, j * C:(j + 1) * C])
                step(ins)
                even, dev_even, odd, dev_odd = (st6[:, n, :, i] for i in (1, 2, 4, 5))
                w = stw[:, n]
                step(v.tensor_tensor(w[:, 0], even, odd, ALU.subtract), False)
                step(v.tensor_tensor(w[:, 1], even, odd, ALU.add), False)
                step(v.scalar_tensor_tensor(w[:, 2], dev_even, C * LN_EPS, dev_odd, ALU.add, ALU.add))
                step(v.tensor_tensor(w[:, 0], w[:, 0], w[:, 0], ALU.mult), False)
                step(v.tensor_scalar(w[:, 3], w[:, 1], 0.5, None, ALU.mult))
                step(v.scalar_tensor_tensor(w[:, 4], w[:, 2], 4.0 / C, w[:, 0], ALU.mult, ALU.add))

            def norm(n, b, u, k, dst, pow_done, free, done):
                need(dve, pow_done, k + 1)
                for sem_, count in free:
                    need(dve, sem_, count)
                for j in range(TILES):
                    i = u * TILES + j
                    ins = v.tensor_scalar(dst[:, u, j * C:(j + 1) * C], resid[:, b, j * C:(j + 1) * C],
                                          stw[:, n, 3, i:i + 1], stw[:, n, 5, i:i + 1], ALU.subtract, ALU.mult)
                ins.then_inc(done, 1)

            def feature(b, u):
                need(dve, s.qe_done, 2 * b + 2)
                need(dve, s.o_psum, b - 1)
                v.scalar_tensor_tensor(qf[:, u, :], ef[:, 0, :], 1.0, rf[:, 0, :], ALU.min, ALU.add).then_inc(s.qf_done, 1)
                need(dve, s.ke_done, 2 * b + 2)
                need(dve, s.s_psum, b - 1)
                v.scalar_tensor_tensor(kf[:, u, :], ef[:, 1, :], 1.0, rf[:, 1, :], ALU.min, ALU.add).then_inc(s.kf_done, 1)

            def keys_values(c, u):
                need(dve, s.s_psum, c + 1)
                need(dve, s.o_psum, c - 1)
                v.tensor_tensor(kv[:, u, 0:C], bank_s[:, 0:C], const(cst, "block_kv"), ALU.mult)
                v.tensor_tensor(kv[:, u, C:C + H], bank_s[:, C:C + 1].to_broadcast([P, H]), const(cst, "block_ks"), ALU.mult).then_inc(s.kv_done, 1)

            def mixed(c, u):
                step = chain(dve, s.mix_step, 3 * c)
                need(dve, s.o_psum, c + 1)
                need(dve, s.add_done, c)
                o4 = banks_o.rearrange("p n (i c) -> p (n i) c", i=2)
                step(v.tensor_scalar(den[:, 0], o4[:, :, C:C + H], ATT_EPS / TOK, None, ALU.add))
                step(v.reciprocal(den[:, 1], den[:, 0]))
                weight = den[:, 1].rearrange("p j (h o) -> p j h o", o=1).to_broadcast([P, TILES, H, HD])
                step(v.tensor_tensor(mix[:].rearrange("p (j h d) -> p j h d", j=TILES, h=H),
                                     o4[:, :, 0:C].rearrange("p j (h d) -> p j h d", h=H), weight, ALU.mult))
                v.tensor_tensor(resid[:, c, :], resid[:, c, :], mix[:], ALU.add).then_inc(s.add_done, 1)

            def lo(d, u, slot):
                need(dve, s.hi_done, d + 1)
                r = rows[:, slot].bitcast(F16)
                v.tensor_tensor(r[:, :, C:2 * C], xn2[:, u, :].rearrange("p (j c) -> p j c", j=TILES), r[:, :, 0:C],
                                ALU.subtract).then_inc(s.lo_done, 1)

            def route(k, d):
                step = chain(dve, s.route, ROUTE_STEPS * k)
                need(dve, s.lg_psum, 2 * k + 2)
                shape = [P, 8, E]
                wide = lambda ap: ap.rearrange("p (n o) -> p n o", o=1).to_broadcast(shape)
                rank3 = rank_of.rearrange("p (n e) -> p n e", e=E)
                bias = rb[:].rearrange("p (o e) -> p o e", o=1).to_broadcast(shape)
                step(v.tensor_tensor(lg[:], bank_x[:, 0:8 * E].rearrange("p (n e) -> p n e", e=E), bias, ALU.add))
                for n in range(2):
                    step(v.tensor_reduce(best[:, n, :], lg[:], AX.X, ALU.max))
                    step(v.tensor_tensor(tmp[:, n], lg[:], wide(best[:, n, :]), ALU.is_equal))
                    step(v.tensor_tensor(tmp[:, n], tmp[:, n], rank3, ALU.mult))
                    step(v.tensor_reduce(best[:, 4 + n, :], tmp[:, n], AX.X, ALU.max))
                    if n == 0:
                        step(v.tensor_tensor(oh[:, 0], tmp[:, 0], wide(best[:, 4, :]), ALU.is_equal))
                        step(v.scalar_tensor_tensor(lg[:], oh[:, 0], -3e38, lg[:], ALU.mult, ALU.add))
                step(v.tensor_tensor(oh[:, 1], tmp[:, 1], wide(best[:, 5, :]), ALU.is_equal), False)
                step(v.tensor_tensor(best[:, 2, :], best[:, 1, :], best[:, 0, :], ALU.subtract))
                step(v.tensor_tensor(oh16[:], oh[:, 0], oh[:, 1], ALU.add))
                for n in range(8):
                    step(v.tensor_tensor(ahead16[:, n + 1, :], ahead16[:, n, :], oh16[:, n, :], ALU.add))

            def placed(k, d, slot):
                step = chain(dve, s.place_step, PLACE_STEPS * k)
                need(dve, s.ew_done, k + 1)
                step(v.tensor_scalar(best[:, 6, :], best[:, 3, :], 1.0, None, ALU.add))
                step(v.reciprocal(best[:, 7, :], best[:, 6, :]))
                step(v.tensor_tensor(best[:, 6, :], best[:, 3, :], best[:, 7, :], ALU.mult))
                step(v.tensor_tensor(best[:, 7, :], best[:, 7, :], best[:, 6, :], ALU.subtract))
                w3 = lambda n: best[:, n, :].rearrange("p (u j) -> p u j", u=2)
                word = lambda n: rows[:, slot:slot + 2, :, C + n]
                step(v.tensor_scalar(word(0), w3(6), 1.0 / WS, None, ALU.mult), False)
                step(v.tensor_scalar(word(1), w3(7), 1.0 / WS, None, ALU.mult), False)
                step(v.tensor_copy(word(2), w3(4)), False)
                ids = const(cst, "slot1").rearrange("p (b j) -> p b j", j=TILES)
                step(v.tensor_copy(word(3), ids[:, bass.ds(d, 2), :]), False)
                need(dve, s.rank_psum, k + 1)
                region = const(cst, "region").rearrange("p (n e) -> p n e", e=E)
                step(v.tensor_tensor(spot[:], bank_x[:, 64:64 + 8 * E].rearrange("p (n e) -> p n e", e=E), region, ALU.add))
                step(v.tensor_tensor(tmp[:, 0], spot[:], oh[:, 0], ALU.mult), False)
                step(v.tensor_tensor(tmp[:, 1], spot[:], oh[:, 1], ALU.mult))
                for n in range(2):
                    step(v.tensor_reduce(best[:, n, :], tmp[:, n], AX.X, ALU.add))
                    v_place = place[:, slot:slot + 2, :, n]
                    step(v.tensor_copy(v_place, w3(n)))
                v.tensor_copy(ahead16[:, 0, :], ahead16[:, 8, :]).then_inc(s.place_done, 1)
                need(dve, s.place_done, k + 1)

            def body(m, odd, on):
                b, c, d = 2 * m - 2, 2 * m - 4, 2 * m - 8
                if on(1):
                    norm(0, b, 0, m - 1, xn, s.pow1, [(s.xT, b - 1)], s.norm1)
                    norm(0, b + 1, 1, m - 1, xn, s.pow1, [(s.xT, b)], s.norm1)
                if on(4):
                    for u in range(2):
                        norm(1, d + u, u, m - 4, xn2, s.pow2, [(s.xT2, d + u - 1), (s.lo_done, d + u - 1)], s.norm2)
                if on(2):
                    keys_values(c, 0)
                if on(0):
                    stats(0, 2 * m, m, s.stat1)
                if on(2):
                    keys_values(c + 1, 1)
                if on(4):
                    lo(d, 0, 2 * odd)
                    lo(d + 1, 1, 2 * odd + 1)
                if on(1):
                    feature(b, 0)
                if on(2):
                    mixed(c, 0)
                if on(3):
                    stats(1, 2 * m - 6, m - 3, s.stat2)
                if on(4):
                    route(m - 4, d)
                if on(1):
                    feature(b + 1, 1)
                if on(2):
                    mixed(c + 1, 1)
                if on(4):
                    placed(m - 4, d, 2 * odd)
            pipelined_by_two(dve, PAIRS, 6, body)
            dve.wait_ge(s.rank_psum, PAIRS + 1)
            step = chain(dve, s.table, 0)
            cnt, cnti, nb, delta, cum = (ffn[n] for n in ("cnt", "cnti", "nb", "delta", "cum"))
            step(v.tensor_copy(cnt[:], bank_s[:, 0:E]))
            step(v.tensor_tensor(ffn["tail_i"][:], cnt[:], const(cst, "region")[:, 0:E], ALU.add), False)
            step(v.tensor_scalar(cnti[:], cnt[:], float(BLOCK - 1), None, ALU.add))
            step(v.tensor_scalar(cnti[:], cnti[:], BLOCK.bit_length() - 1, None, ALU.arith_shift_right))
            step(v.tensor_copy(nb[:], cnti[:]))
            step(v.tensor_scalar(delta[:], nb[:], -float(BLOCK), float(REGION), ALU.mult, ALU.add))
            step(v.tensor_copy(cum[:], nb[:]))
            for e in range(1, E):
                step(v.tensor_tensor(cum[:, e:e + 1], cum[:, e - 1:e], nb[:, e:e + 1], ALU.add))
            expert, first, over = ffn["expert"], ffn["first"], ffn["over"]
            number = const(cst, "block_no")
            step(v.memset(expert[:], float(E)), False)
            step(v.tensor_scalar(first[:], number, float(BLOCK), None, ALU.mult))
            for e in range(E):
                step(v.tensor_scalar(over[:], number, cum[:, e:e + 1], None, ALU.is_ge))
                step(v.tensor_tensor(expert[:], expert[:], over[:], ALU.subtract), False)
                step(v.scalar_tensor_tensor(first[:], over[:], delta[:, e:e + 1], first[:], ALU.mult, ALU.add))
            step(v.tensor_scalar(expert[:], expert[:], 1.0, None, ALU.max), False)
            step(v.tensor_scalar(first[:], first[:], float(E * REGION), None, ALU.min))
            step(v.tensor_scalar(ffn["expert_i"][:], expert[:], -1.0, float(E), ALU.mult, ALU.add), False)
            step(v.tensor_copy(ffn["first_i"][:], first[:]))
            step(v.memset(ffn["nobody"][:], 0.0))
            step(v.memset(ffn["nobody"][:, :, C + 3:C + 4], NO_SLOT))


META_STEPS = 4


def in_turns(eng, *stages):
    def turn(m, exists):
        for p in range(4):
            for lag, f in stages:
                if exists(4 * m + p - lag):
                    f(4 * m + p - lag, (p - lag) % 4)
    turn(0, lambda k: k >= 0)
    with eng.Fori(1, BLOCKS // 4) as m:
        turn(m, lambda k: True)
    turn(BLOCKS // 4, lambda k: k < BLOCKS)


def experts(nc, ident, ffn, rows_dram, res_dram):
    w1_hl, b1_hl, w2_hl, b2_hl = ffn["w1_hl"], ffn["b1_hl"], ffn["w2_hl"], ffn["b2_hl"]
    with ExitStack() as ctx:
        def sb(name, shape, dt=F32):
            return ctx.enter_context(nc.sbuf_tensor(name, shape, dt))

        ident16 = sb("e_ident16", [P, P], F16)
        ones16 = sb("e_ones16", [P, BLOCK], F16)
        xg = sb("e_xg", [P, 4, 2, ROW])
        xt = sb("e_xt", [P, 2, 2, BLOCK], F16)
        sig = sb("e_sig", [P, 2, 2 * BLOCK])
        gs = sb("e_gs", [P, 2, 2 * BLOCK])
        hid = sb("e_hid", [P, 2, 2 * BLOCK])
        hid_hl = sb("e_hid_hl", [P, 2, 2, 2, BLOCK], F16)
        first_choice = sb("e_first", [P, 2, 2])
        wt = sb("e_wt", [P, 4, 2])
        dest = sb("e_dest", [P, 4, 2], I32)
        y = sb("e_y", [P, 4, 2, C])
        one, held = sb("e_one", [1, 1]), sb("e_held", [1, 1])
        ps = ctx.enter_context(nc.psum_tensor("e_ps", [P, 8, 2 * BLOCK], F32))
        s = Named({n: ctx.enter_context(nc.semaphore("e_" + n)) for n in """
            set_v set_g held nobody_in x0_in x1_in x2_in x3_in xT xt_done g_psum u_psum sig_done gs_done hid_done hh_done
            hl_done y_psum y_done meta r0_out r1_out r2_out r3_out""".split()})
        x_in = [s.x0_in, s.x1_in, s.x2_in, s.x3_in]
        r_out = [s.r0_out, s.r1_out, s.r2_out, s.r3_out]
        quads = BLOCKS // 4

        block = ctx.enter_context(nc.Block())

        @block.sync
        def _(sp):
            nobody = ffn["nobody"]
            fill = lambda row: rows_dram[row].rearrange("(n p) w -> p n w", p=P)
            sp.dma_start(rows_dram[E * REGION:E * REGION + BLOCK].rearrange("(n p) w -> p n w", p=P), nobody[:]).then_inc(s.nobody_in, 16)
            for e in range(E):
                row = sp.value_load(ffn["tail_i"][0:1, e:e + 1], min_val=e * REGION, max_val=(e + 1) * REGION - BLOCK)
                sp.dma_start(rows_dram[bass.ds(row, BLOCK)].rearrange("(n p) w -> p n w", p=P), nobody[:]).then_inc(s.nobody_in, 16)
            sp.wait_ge(s.nobody_in, 16 * (E + 1))

            def load(m):
                for i in range(4):
                    row = sp.value_load(ffn["first_i"][0:1, bass.ds(4 * m + i, 1)], min_val=0, max_val=E * REGION)
                    need(sp, s.meta, META_STEPS * (4 * m + i - 3))
                    sp.dma_start(xg[:, i], rows_dram[bass.ds(row, BLOCK)].rearrange("(n p) w -> p n w", p=P)).then_inc(x_in[i], 16)
            load(0)
            with sp.Fori(1, quads) as m:
                load(m)

        @block.gpsimd
        def _(pool):
            nc.gpsimd.memset(one[:], 0.0).then_inc(s.set_g, 1)
            pool.wait_ge(s.set_g, 1)

            def send(m):
                for i in range(4):
                    need(pool, s.held, 4 * m + i)
                    pool.wait_ge(s.y_done, 4 * m + i + 1)
                    nc.gpsimd.tensor_tensor(held[:], one[:], one[:], ALU.mult).then_inc(s.held, 1)
                    for n in range(2):
                        nc.gpsimd.indirect_dma_start(res_dram, bass.IndirectOffsetOnAxis(ap=dest[:, i, n:n + 1], axis=0),
                                                     y[:, i, n, :], None, bounds_check=2 * B * TOK - 1, oob_is_err=False).then_inc(r_out[i], 16)
            send(0)
            with pool.Fori(1, quads) as m:
                send(m)
            for r in r_out:
                pool.wait_ge(r, 16 * 2 * quads)

        @block.tensor
        def _(pe):
            t = nc.tensor
            pe.wait_ge(s.set_v, 2)

            def expert(k):
                return pe.value_load(ffn["expert_i"][0:1, bass.ds(k, 1)], min_val=0, max_val=E - 1)

            def xT(k, i):
                pe.wait_ge(x_in[i], 4 * (k - i) + 16)
                need(pe, s.xt_done, k - 1)
                dst = ps[:, i % 2, 0:BLOCK].bitcast(F16).rearrange("p (l n c) -> p l n c", l=2, n=2)
                src = xg[:, i].bitcast(F16)
                for l in range(2):
                    for n in range(2):
                        last = t.transpose(dst[:, l, n], src[:, n, l * C:(l + 1) * C], ident16[:])
                last.then_inc(s.xT, 1)

            def inner(k, i):
                e = expert(k)
                need(pe, s.xt_done, k + 1)
                x2 = [xt[:, i % 2, l, :] for l in range(2)]
                for bank, part, free, psum in ((2, 0, s.gs_done, s.g_psum), (4, 2, s.hid_done, s.u_psum)):
                    need(pe, free, k - 1)
                    for n in range(2):
                        at = (part + n) * P
                        o = ps[:, bank + i % 2, n * BLOCK:(n + 1) * BLOCK]
                        hi, lo = (w1_hl[:, bass.ds(e, 1), l, at:at + P].rearrange("p o c -> p (o c)") for l in range(2))
                        t.matmul(o, b1_hl[:, bass.ds(e, 1), at:at + P].rearrange("p o c -> p (o c)"), ones16[:], start=True, stop=False)
                        t.matmul(o, hi, x2[0], start=False, stop=False)
                        t.matmul(o, hi, x2[1], start=False, stop=False)
                        last = t.matmul(o, lo, x2[0], start=False, stop=True)
                    last.then_inc(psum, 1)

            def outer(k, i):
                e = expert(k)
                need(pe, s.hl_done, k + 1)
                need(pe, s.y_done, k - 1)
                for n in range(2):
                    o = ps[:, 6 + i % 2, n * C:(n + 1) * C]
                    t.matmul(o, ones16[:, 0:P], b2_hl[:, bass.ds(e, 1), :].rearrange("p o c -> p (o c)"), start=True, stop=False)
                    for q in range(2):
                        hi, lo = (hid_hl[:, i % 2, l, q, n * P:(n + 1) * P] for l in range(2))
                        whi, wlo = (w2_hl[:, bass.ds(e, 1), l, q, :].rearrange("p o c -> p (o c)") for l in range(2))
                        t.matmul(o, hi, whi, start=False, stop=False)
                        t.matmul(o, hi, wlo, start=False, stop=False)
                        last = t.matmul(o, lo, whi, start=False, stop=q == 1)
                last.then_inc(s.y_psum, 1)

            in_turns(pe, (0, xT), (1, inner), (3, outer))

        @block.scalar
        def _(act):
            a = nc.scalar

            def x(k, i):
                need(act, s.xT, k + 1)
                need(act, s.u_psum, k - 1)
                a.activation(xt[:, i % 2].rearrange("p l c -> p (l c)"), ps[:, i % 2, 0:BLOCK].bitcast(F16), ACT.Copy).then_inc(s.xt_done, 1)

            def sigmoid(k, i):
                need(act, s.g_psum, k + 1)
                need(act, s.gs_done, k - 1)
                a.activation(sig[:, i % 2], ps[:, 2 + i % 2], ACT.Sigmoid, scale=1.702 / WS).then_inc(s.sig_done, 1)

            def high(k, i):
                need(act, s.hid_done, k + 1)
                need(act, s.y_psum, k - 1)
                need(act, s.hl_done, k - 1)
                a.activation(hid_hl[:, i % 2, 0].rearrange("p q c -> p (q c)"), hid[:, i % 2], ACT.Copy).then_inc(s.hh_done, 1)

            def result(k, i):
                need(act, s.y_psum, k + 1)
                need(act, s.meta, META_STEPS * (k + 1))
                need(act, r_out[i], 8 * (k - i))
                for n in range(2):
                    ins = a.activation(y[:, i, n, :], ps[:, 6 + i % 2, n * C:(n + 1) * C], ACT.Copy, scale=wt[:, i, n:n + 1])
                ins.then_inc(s.y_done, 1)
            in_turns(act, (0, x), (1, sigmoid), (1, high), (3, result))

        @block.vector
        def _(dve):
            v = nc.vector
            step = chain(dve, s.set_v, 0)
            step(v.tensor_copy(ident16[:], ident))
            step(v.memset(ones16[:], 1.0))

            def meta(k, i):
                need(dve, x_in[i], 4 * (k - i) + 16)
                need(dve, s.xT, k + 1)
                need(dve, s.y_done, k - 3)
                need(dve, r_out[i], 8 * (k - i))
                step = chain(dve, s.meta, META_STEPS * k)
                word = lambda n: xg[:, i, :, C + n]
                one = first_choice[:, i % 2]
                step(v.tensor_scalar(one, word(2), ffn["expert"][:, bass.ds(k, 1)], None, ALU.is_equal))
                step(v.tensor_tensor(wt[:, i], one, word(1), ALU.mult), False)
                step(v.tensor_tensor(dest[:, i], word(3), one, ALU.subtract))
                step(v.tensor_tensor(wt[:, i], wt[:, i], word(0), ALU.add), False)

            def gated(k, i):
                need(dve, s.sig_done, k + 1)
                need(dve, s.hid_done, k - 1)
                v.scalar_tensor_tensor(gs[:, i % 2], ps[:, 2 + i % 2], 1.0 / (WS * WS), sig[:, i % 2], ALU.mult, ALU.mult).then_inc(s.gs_done, 1)
                need(dve, s.gs_done, k + 1)
                need(dve, s.u_psum, k + 1)
                need(dve, s.hl_done, k - 1)
                need(dve, s.hh_done, k - 1)
                v.scalar_tensor_tensor(hid[:, i % 2], ps[:, 4 + i % 2], WS, gs[:, i % 2], ALU.add, ALU.mult).then_inc(s.hid_done, 1)

            def low(k, i):
                need(dve, s.hh_done, k + 1)
                need(dve, s.y_psum, k - 1)
                v.tensor_tensor(hid_hl[:, i % 2, 1].rearrange("p q c -> p (q c)"), hid[:, i % 2],
                                hid_hl[:, i % 2, 0].rearrange("p q c -> p (q c)"), ALU.subtract).then_inc(s.hl_done, 1)
            in_turns(dve, (1, meta), (1, gated), (2, low))


def combine(nc, resid, res_dram, out):
    out_tok = out.rearrange("b a (tl j) c -> b (a tl) (j c)", j=TILES)
    res_tok = res_dram.rearrange("(b p j n) c -> b p (j n c)", p=P, j=TILES, n=2)
    with ExitStack() as ctx:
        yb = ctx.enter_context(nc.sbuf_tensor("c_y", [P, 4, 2 * TOK], F32))
        s = Named({n: ctx.enter_context(nc.semaphore("c_" + n)) for n in
                               "y0_in y1_in y2_in y3_in one_done both_done out_done".split()})
        y_in = [s.y0_in, s.y1_in, s.y2_in, s.y3_in]
        block = ctx.enter_context(nc.Block())

        @block.sync
        def _(sp):
            def load(m):
                for i in range(4):
                    need(sp, s.both_done, 4 * m + i - 3)
                    sp.dma_start(yb[:, i, :], res_tok[4 * m + i]).then_inc(y_in[i], 16)
            load(0)
            with sp.Fori(1, B // 4) as m:
                load(m)

        @block.vector
        def _(dve):
            with dve.Fori(0, B // 4) as m:
                for i in range(4):
                    b = 4 * m + i
                    y4 = yb[:, i, :].rearrange("p (j n c) -> p j n c", j=TILES, n=2)
                    r = resid[:, b, :].rearrange("p (j c) -> p j c", j=TILES)
                    dve.wait_ge(y_in[i], 16 * m + 16)
                    nc.vector.tensor_tensor(r, r, y4[:, :, 0, :], ALU.add).then_inc(s.one_done, 1)
                    dve.wait_ge(s.one_done, b + 1)
                    nc.vector.tensor_tensor(r, r, y4[:, :, 1, :], ALU.add).then_inc(s.both_done, 1)

        @block.scalar
        def _(act):
            with act.Fori(0, B) as b:
                act.wait_ge(s.both_done, b + 1)
                act.dma_start(out_tok[b], resid[:, b, :]).then_inc(s.out_done, 16)
            act.wait_ge(s.out_done, 16 * B)


def build(nc, t):
    rows_dram = nc.dram_tensor("rows", (E * REGION + BLOCK, ROW), F32, kind="Internal").ap()
    res_dram = nc.dram_tensor("results", (2 * B * TOK, C), F32, kind="Internal").ap()
    with ExitStack() as ctx:
        def sb(name, shape, dt=F32):
            return ctx.enter_context(nc.sbuf_tensor(name, shape, dt))

        early = sb("early", [P, EARLY.shape[1]])
        resid = sb("resid", [P, B, TOK])
        ones16 = sb("ones16", [P, P], F16)
        agent_attention(nc, early, resid, ones16, t["x"], t["L0_conv_coalition"], t["L0_conv_masks"], t["L0_conv_emb_W"],
                        *(t["L0_conv_" + n] for n in "Wq bq Wk bk Wv bv Wo bo".split()), t["early"])
        late = sb("late", [P, LATE.shape[1]])
        ffn = {
            "w1_hl": sb("w1_hl", [P, E, 2, 2 * I], F16), "b1_hl": sb("b1_hl", [P, E, 2 * I], F16),
            "w2_hl": sb("w2_hl", [P, E, 2, 2, C], F16), "b2_hl": sb("b2_hl", [P, E, C], F16),
            "cnt": sb("cnt", [P, E]), "cnti": sb("cnti", [P, E], I32), "nb": sb("nb", [P, E]),
            "delta": sb("delta", [P, E]), "cum": sb("cum", [P, E]), "tail_i": sb("tail_i", [P, E], I32),
            "expert": sb("expert", [P, BLOCKS]), "first": sb("first", [P, BLOCKS]), "over": sb("over", [P, BLOCKS]),
            "expert_i": sb("expert_i", [P, BLOCKS], I32), "first_i": sb("first_i", [P, BLOCKS], I32),
            "nobody": sb("nobody", [P, 2, ROW]),
        }
        ident = const(early, "ident")
        token_mixer(nc, late, resid, ones16, ident, t["late"], ffn, rows_dram, *(t["L1_attn_" + n] for n in "Wq bq Wk bk Wv bv".split()),
                    *(t["L1_ffn_" + n] for n in "router_w router_b gate_up_proj gate_up_proj_bias down_proj down_proj_bias".split()))
        experts(nc, ident, ffn, rows_dram, res_dram)
        combine(nc, resid, res_dram, t["out"])


_INS = """x L0_conv_coalition L0_conv_masks L0_conv_emb_W L0_conv_Wq L0_conv_bq L0_conv_Wk L0_conv_bk L0_conv_Wv L0_conv_bv
    L0_conv_Wo L0_conv_bo L1_attn_Wq L1_attn_bq L1_attn_Wk L1_attn_bk L1_attn_Wv L1_attn_bv L1_ffn_router_w L1_ffn_router_b
    L1_ffn_gate_up_proj L1_ffn_gate_up_proj_bias L1_ffn_down_proj L1_ffn_down_proj_bias""".split()


def kernel(**inputs):
    import concourse.bacc as bacc
    from concourse.bass_utils import run_bass_kernel_spmd

    nc = bacc.Bacc("TRN2", target_bir_lowering=False, num_devices=1)
    arrays, tensors = {}, {}
    for name, a in [(n, inputs[n]) for n in _INS] + [("early", EARLY), ("late", LATE)]:
        a = np.ascontiguousarray(a)
        arrays[f"in_{name}"] = a
        tensors[name] = nc.dram_tensor(f"in_{name}", a.shape, mybir.dt.from_np(a.dtype), kind="ExternalInput").ap()
    tensors["out"] = nc.dram_tensor("out_0", (B, A, T, C), F32, kind="ExternalOutput").ap()
    build(nc, tensors)
    return run_bass_kernel_spmd(nc, [arrays], core_ids=[0]).results[0]["out_0"]
```

```python
from contextlib import ExitStack

import numpy as np

import concourse.bass as bass
from concourse import mybir

F32, F16, I32 = mybir.dt.float32, mybir.dt.float16, mybir.dt.int32
ALU = mybir.AluOpType
ACT = mybir.ActivationFunctionType
AX = mybir.AxisListType

P = 128
B, A, T, C = 32, 16, 32, 128
H, HD = 8, 16
S = 5
TILES = A * T // P
TOK = A * T
PAIRS = B // 2
WS = 64.0
GN_EPS, LN_EPS, ATT_EPS = 1e-5, 1e-5, 1e-6
TABLE_STEP = 18
E, I = 8, 256
BLOCK = 256
REGION = B * TOK + BLOCK
BLOCKS = 2 * B * TOK // BLOCK + E
TURNS = BLOCKS // 4
ROW = C + 4
LN_STEPS, ROUTE_STEPS, PLACE_STEPS = 7, 22, 15
NO_SLOT = 1e6
SP_ = 64

CONST = {}


def _constants():
    parts, at = {0: [], 1: []}, [0, 0]

    def put(late, name, a):
        full = np.zeros((P, a.shape[1]), np.float32)
        full[: a.shape[0]] = a
        CONST[name] = (at[late], a.shape[1])
        at[late] += a.shape[1]
        parts[late].append(full)

    r = np.arange(P)
    put(0, "ident", np.eye(P))
    put(0, "block8", r[:, None] // HD == np.arange(H)[None, :])
    put(0, "group", (r[:, None] // 4 == r[None, :] // 4) / 8.0)
    put(0, "eye_qk", np.tile(np.eye(A), (S, 1)))
    put(1, "block_kv", (r[:, None] // HD == r[None, :] // HD) / float(TOK))
    put(1, "block_ks", (r[:, None] // HD == np.arange(H)[None, :]) / float(TOK))
    put(1, "before", (r[:, None] < r[None, :]) * 1.0)
    put(1, "rank_of", np.tile(float(E) - np.arange(E), (P, 8)))
    put(1, "region", np.tile(np.arange(E) * float(REGION), (P, 8)))
    put(1, "block_no", np.tile(np.arange(BLOCKS) * 1.0, (P, 1)))
    tok = np.arange(B)[None, :, None] * TOK + r[:, None, None] * TILES + np.arange(TILES)[None, None, :]
    put(1, "slot1", (2.0 * tok + 1).reshape(P, -1))
    return np.concatenate(parts[0], 1), np.concatenate(parts[1], 1)


EARLY, LATE = _constants()


class Named(dict):

    def __getattr__(self, name):
        return self[name]


def const(cst, name):
    at, n = CONST[name]
    return cst[:, at:at + n]


def need(eng, sem, count):
    if isinstance(count, int) and count <= 0:
        return
    eng.wait_ge(sem, count)


def most(count, top):
    return min(count, top) if isinstance(count, int) else count


def pipelined(eng, steps, depth, unroll, work):
    def body(m, n):
        for stage, f, *args in work:
            if not isinstance(m, int) or 0 <= m - stage < steps:
                f(m - stage, (n - stage) % unroll, *args)

    for m in range(depth):
        body(m, m)
    with eng.Fori(0, (steps - depth) // unroll) as turn:
        for n in range(depth, depth + unroll):
            body(unroll * turn + n, n)
    for m in range(steps, steps + depth - 1):
        body(m, m)


def agent_attention(nc, cst, resid, ones16, x, coalition, masks, emb_W, Wq, bq, Wk, bk, Wv, bv, Wo, bo, consts):
    with ExitStack() as ctx:
        def sb(name, shape, dt=F32):
            return ctx.enter_context(nc.sbuf_tensor(name, shape, dt))

        def sem(name):
            return ctx.enter_context(nc.semaphore(name))

        x_tok = x.rearrange("b a (tl j) c -> b (a tl) (j c)", j=TILES)

        arena = sb("arena", [P, 2 * 2 * 2 * TOK * H], F16)
        gxb = arena[:, 0:4 * 2 * TOK].bitcast(F32).rearrange("p (n c) -> p n c", n=4)
        carved = [4 * 2 * TOK]

        def carve(shape, dt=F32):
            n = int(np.prod(shape[1:])) * 2
            at = carved[0]
            carved[0] += n
            ap = arena[0:shape[0], at:at + n].bitcast(dt)
            if len(shape) == 3:
                ap = ap.rearrange("p (m n) -> p m n", m=shape[1])
            return ap

        ident, group, block8 = const(cst, "ident"), const(cst, "group"), const(cst, "block8")
        wstage = carve([P, 4, C])
        w_f = carve([P, 4, C])
        w_hl = sb("w_hl", [P, 2, 4, C], F16)
        bias0 = sb("bias0", [P, 4])
        bo_row = sb("bo_row", [1, C])
        brow = sb("brow", [1, C])
        bo_hl = sb("bo_hl", [64, TOK], F16)
        emb16 = sb("emb16", [A, C])
        embT = sb("embT", [P, A])
        coal = sb("coal", [A, 1], I32)
        shift = sb("shift", [P, B, A])
        gst6 = carve([P, B, 6])
        gstat = carve([P, B, 2])
        gsum = carve([P, 2, B])
        gmean = carve([P, 2, B])
        gtmp = carve([P, 2, B])
        half = carve([P, B])
        rstd = sb("rstd", [P, B])
        nmr = carve([P, B])
        mraw = carve([S * A, A], I32)
        mflt = carve([S * A, A])
        mrep = carve([S * A, H, A])
        mkq = carve([P, S, A])
        msum = sb("msum", [P, A, SP_])
        mspread = sb("mspread", [P, A // 2, P])
        bd = arena[:].rearrange("p (n u l g h q) -> p n u l g h q", n=2, u=2, l=2, h=H, q=A)
        bdq, bdp = bd[:, 0], bd[:, 1]
        xb = sb("xb", [P, 2, TOK])
        xi = sb("xi", [P, 2, TOK])
        xhl = sb("xhl", [P, 2, 2, TOK], F16)
        t32 = sb("t32", [P, 4, TOK])
        qhl = sb("qhl", [P, 2, 2, TOK], F16)
        khl = sb("khl", [P, 2, 2, TOK], F16)
        vhl = sb("vhl", [P, 6, 2, TOK], F16)
        sm = sb("sm", [P, 2, TOK])
        rmax = sb("rmax", [P, 2, T])
        pt = sb("pt", [P, 2, TOK])
        phl = sb("phl", [P, 2, 2, TOK], F16)
        recip = sb("recip", [P, A // 2, 2 * TILES * H])
        o32 = sb("o32", [P, 2, TOK])
        othl = sb("othl", [P, 2, 2, TOK], F16)

        ps = ctx.enter_context(nc.psum_tensor("ps", [P, 8, TOK], F32))
        bank_xy, bank_q, bank_k, bank_vo, bank_s, bank_t, bank_d = (ps[:, n, :] for n in range(7))

        s = Named({n: sem(n) for n in """
            consts_in weights_in masks_in coal_in emb_in resid_in gx0_in gx1_in gx2_in gx3_in x0_in x1_in
            setup_v spread_done half_set setup_pe gT_psum gst_done gvar_done gsum_done gmean_psum rstd_done shift_done
            xT_psum xi_done xh_done xl_done q_psum k_psum v_psum q32_done qh_done ql_done k32_done kh_done
            kl_done v32_done vh_done vl_done bdq_done s_psum rmax_done sm_done e_done et_psum et_done d_psum
            recip_done w_psum p_done ph_done pl_done bdp_done o_psum o32_done ot_psum ot32_done oth_done
            otl_done y_psum x1_done out_done""".split()})
        gx_in, x_in = [s.gx0_in, s.gx1_in, s.gx2_in, s.gx3_in], [s.x0_in, s.x1_in]

        block = ctx.enter_context(nc.Block())

        @block.sync
        def _(sp):
            sp.dma_start(cst[:], consts).then_inc(s.consts_in, 16)
            sp.dma_start(coal[:], coalition.rearrange("(a o) -> a o", o=1)).then_inc(s.coal_in, 16)
            sp.dma_start(mraw[:], masks.rearrange("s q k -> (s q) k")).then_inc(s.masks_in, 16)
            for n, w in enumerate((Wq, Wk, Wv, Wo)):
                sp.dma_start(wstage[:, n, :], w).then_inc(s.weights_in, 16)
            for n, v in enumerate((bq, bk, bv)):
                sp.dma_start(bias0[:, n:n + 1], v.rearrange("(c o) -> c o", o=1)).then_inc(s.weights_in, 16)
            sp.dma_start(bo_row[:], bo.rearrange("(o c) -> o c", o=1)).then_inc(s.weights_in, 16)

            def first_pass(m):
                for u in range(4):
                    need(sp, s.gT_psum, 4 * m + u - 3)
                    sp.dma_start(gxb[:, u, :], x_tok[4 * m + u]).then_inc(gx_in[u], 16)
            first_pass(0)
            with sp.Fori(1, B // 4) as m:
                first_pass(m)

            def second_pass(m):
                for u in range(2):
                    need(sp, s.xT_psum, 2 * m + u - 1)
                    sp.dma_start(xb[:, u, :], x_tok[2 * m + u]).then_inc(x_in[u], 16)
            second_pass(0)
            with sp.Fori(0, B) as b:
                sp.dma_start(resid[:, b, :], x_tok[b]).then_inc(s.resid_in, 16)
            with sp.Fori(1, PAIRS) as m:
                second_pass(m)

        @block.gpsimd
        def _(pool):
            g = nc.gpsimd
            g.memset(half[:], -0.5).then_inc(s.half_set, 1)
            pool.wait_ge(s.coal_in, 16)
            g.indirect_dma_start(emb16[:], None, emb_W, bass.IndirectOffsetOnAxis(ap=coal[:], axis=0)).then_inc(s.emb_in, 16)
            pool.wait_ge(s.half_set, 1)
            pool.wait_ge(s.gvar_done, 1)
            g.tensor_tensor(rstd[:], gtmp[:, 1, :], half[:], ALU.pow).then_inc(s.rstd_done, 1)

            def low(dst, full, high, full_done, high_done, done, n, free, freed):
                need(pool, full_done, n + 1)
                need(pool, high_done, n + 1)
                need(pool, free, freed)
                g.tensor_tensor(dst, full, high, ALU.subtract).then_inc(done, 1)

            def xl(k, ring, u):
                b = 2 * k + u
                low(xhl[:, u, 1, :], xi[:, u, :], xhl[:, u, 0, :], s.xi_done, s.xh_done, s.xl_done, b, s.v_psum, b - 1)

            def pl(k, ring, u):
                d = 2 * k + u
                low(phl[:, u, 1, :], pt[:, u, :], phl[:, u, 0, :], s.p_done, s.ph_done, s.pl_done, d, s.bdp_done, d - 1)

            def ql_kl(k, ring, u):
                b = 2 * k + u
                low(qhl[:, u, 1, :], t32[:, 0, :], qhl[:, u, 0, :], s.q32_done, s.qh_done, s.ql_done, b, s.bdq_done, b - 1)
                low(khl[:, u, 1, :], t32[:, 1, :], khl[:, u, 0, :], s.k32_done, s.kh_done, s.kl_done, b, s.s_psum, b - 1)

            def vl(k, ring, u):
                b, slot = 2 * k + u, 2 * ring + u
                low(vhl[:, slot, 1, :], t32[:, 2, :], vhl[:, slot, 0, :], s.v32_done, s.vh_done, s.vl_done, b, s.o_psum, b - 5)

            def otl(k, ring, u):
                e = 2 * k + u
                low(othl[:, u, 1, :], t32[:, 3, :], othl[:, u, 0, :], s.ot32_done, s.oth_done, s.otl_done, e, s.y_psum, e - 1)

            pipelined(pool, PAIRS, 4, 3, [
                (2, pl, 0), (0, xl, 0), (2, pl, 1), (0, xl, 1), (0, ql_kl, 0), (3, otl, 0), (3, otl, 1), (0, vl, 0),
                (0, ql_kl, 1), (0, vl, 1),
            ])

        @block.scalar
        def _(act):
            a = nc.scalar

            def xh(k, ring, u):
                b = 2 * k + u
                need(act, s.xi_done, b + 1)
                need(act, s.v_psum, b - 1)
                need(act, s.xl_done, b - 1)
                a.activation(xhl[:, u, 0, :], xi[:, u, :], ACT.Copy).then_inc(s.xh_done, 1)

            def exp(k, ring, u):
                c = 2 * k + u
                need(act, s.sm_done, c + 1)
                a.activation(sm[:, u, :], sm[:, u, :], ACT.Exp, scale=HD ** -0.5).then_inc(s.e_done, 1)

            def ph(k, ring, u):
                d = 2 * k + u
                need(act, s.p_done, d + 1)
                need(act, s.bdp_done, d - 1)
                need(act, s.pl_done, d - 1)
                a.activation(phl[:, u, 0, :], pt[:, u, :], ACT.Copy).then_inc(s.ph_done, 1)

            def o(k, ring, u):
                e = 2 * k + u
                need(act, s.o_psum, e + 1)
                need(act, s.ot_psum, e - 1)
                a.activation(o32[:, u, :], bank_vo, ACT.Copy, scale=1.0 / S).then_inc(s.o32_done, 1)

            def et(k, ring, u):
                c = 2 * k + u
                need(act, s.et_psum, c + 1)
                need(act, s.ph_done, c - 1)
                need(act, s.pl_done, c - 1)
                a.activation(pt[:, u, :], bank_t, ACT.Copy).then_inc(s.et_done, 1)

            def project(bank, n, bias, psum, low_done, full_done, dst, high_done, b, free, freed):
                need(act, psum, b + 1)
                need(act, low_done, b)
                need(act, free, freed)
                if bias is None:
                    a.activation(t32[:, n, :], bank, ACT.Copy, scale=1.0 / WS).then_inc(full_done, 1)
                    a.activation(dst, bank, ACT.Copy, scale=1.0 / WS).then_inc(high_done, 1)
                else:
                    a.activation(t32[:, n, :], bank, ACT.Identity, bias=bias, scale=1.0 / WS).then_inc(full_done, 1)
                    a.activation(dst, bank, ACT.Identity, bias=bias, scale=1.0 / WS).then_inc(high_done, 1)

            def q_k(k, ring, u):
                b = 2 * k + u
                project(bank_q, 0, bias0[:, 0:1], s.q_psum, s.ql_done, s.q32_done, qhl[:, u, 0, :], s.qh_done, b,
                        s.bdq_done, b - 1)
                project(bank_k, 1, bias0[:, 1:2], s.k_psum, s.kl_done, s.k32_done, khl[:, u, 0, :], s.kh_done, b,
                        s.s_psum, b - 1)

            def v(k, ring, u):
                b, slot = 2 * k + u, 2 * ring + u
                project(bank_vo, 2, None, s.v_psum, s.vl_done, s.v32_done, vhl[:, slot, 0, :], s.vh_done, b,
                        s.o_psum, b - 5)

            def ot(k, ring, u):
                e = 2 * k + u
                need(act, s.ot_psum, e + 1)
                need(act, s.otl_done, e)
                need(act, s.y_psum, e - 1)
                src = bank_t.rearrange("p (t j q) -> p j q t", j=TILES, q=A)
                a.activation(t32[:, 3, :].rearrange("p (j q t) -> p j q t", j=TILES, q=A), src, ACT.Copy).then_inc(s.ot32_done, 1)
                a.activation(othl[:, u, 0, :].rearrange("p (j q t) -> p j q t", j=TILES, q=A), src, ACT.Copy).then_inc(s.oth_done, 1)

            act.wait_ge(s.weights_in, 16 * 8)

            pipelined(act, PAIRS, 4, 3, [
                (1, exp, 0), (3, o, 0), (2, ph, 0), (2, ph, 1), (0, xh, 0), (1, et, 0), (1, exp, 1), (0, xh, 1),
                (0, q_k, 0), (1, et, 1), (3, o, 1), (3, ot, 0), (3, ot, 1), (0, v, 0), (0, q_k, 1), (0, v, 1),
            ])

        @block.tensor
        def _(pe):
            t = nc.tensor

            def first(m):
                for u in range(4):
                    pe.wait_ge(gx_in[u], 16 * (m + 1))
                    need(pe, s.gst_done, 4 * m + u - 3)
                    for j in range(TILES):
                        last = t.transpose(ps[:, u, j * P:(j + 1) * P], gxb[:, u, j * P:(j + 1) * P], ident)
                    last.then_inc(s.gT_psum, 1)
            pe.wait_ge(s.consts_in, 16)
            first(0)
            pe.wait_ge(s.setup_v, 4)
            t.matmul(ps[:, 4, 0:S * A], mrep[:], ident[0:S * A, 0:S * A], start=True, stop=True).then_inc(s.setup_pe, 1)
            pe.wait_ge(s.emb_in, 16)
            t.transpose(ps[:, 5, 0:A], emb16[:], ident[0:A, 0:A]).then_inc(s.setup_pe, 1)
            pe.wait_ge(s.weights_in, 16 * 8)
            t.matmul(ps[0:1, 6, 0:C], bias0[:, 2:3], wstage[:, 3, :], start=True, stop=True).then_inc(s.setup_pe, 1)
            with pe.Fori(1, B // 4) as m:
                first(m)
            pe.wait_ge(s.setup_v, TABLE_STEP)
            pe.wait_ge(s.gst_done, B)
            for q in range(A):
                last = t.transpose(ps[0:SP_, q // 4, (q % 4) * P:(q % 4 + 1) * P], msum[:, q, :], ident)
            last.then_inc(s.setup_pe, 1)
            pe.wait_ge(s.gsum_done, 1)
            t.matmul(ps[:, 7, 0:2 * B], group, gsum[:].rearrange("p n b -> p (n b)"), start=True, stop=True).then_inc(s.gmean_psum, 1)
            pe.wait_ge(s.spread_done, 1)

            def xT(k, ring, u):
                b = 2 * k + u
                need(pe, x_in[u], 16 * k + 16)
                need(pe, s.xi_done, b)
                need(pe, s.x1_done, b - 6 - u)
                for j in range(TILES):
                    last = t.transpose(bank_xy.rearrange("p (n j) -> p j n", j=TILES)[:, j, :], xb[:, u, j * P:(j + 1) * P], ident)
                last.then_inc(s.xT_psum, 1)

            def products(out, lhs, rhs, start=True, stop=True):
                t.matmul(out, lhs[0], rhs[0], start=start, stop=False)
                t.matmul(out, lhs[0], rhs[1], start=False, stop=False)
                return t.matmul(out, lhs[1], rhs[0], start=False, stop=stop)

            def qk(k, ring, u):
                c = 2 * k + u
                need(pe, s.bdq_done, c + 1)
                need(pe, s.kl_done, c + 1)
                need(pe, s.sm_done, c)
                for n in range(T):
                    last = products(bank_s[:, n * A:(n + 1) * A], [bdq[:, u, l, n] for l in range(2)],
                                    [khl[:, u, l, n * A:(n + 1) * A] for l in range(2)])
                last.then_inc(s.s_psum, 1)

            def q_k(k, ring, u):
                b = 2 * k + u
                need(pe, s.xl_done, b + 1)
                x2 = [xhl[:, u, l, :] for l in range(2)]
                need(pe, s.qh_done, b)
                products(bank_q, [w_hl[:, l, 0, :] for l in range(2)], x2).then_inc(s.q_psum, 1)
                need(pe, s.kh_done, b)
                products(bank_k, [w_hl[:, l, 1, :] for l in range(2)], x2).then_inc(s.k_psum, 1)

            def v(k, ring, u):
                b = 2 * k + u
                need(pe, s.vh_done, b)
                need(pe, s.o32_done, 2 * k - 4)
                for j in range(TILES):
                    last = products(bank_vo[:, j * P:(j + 1) * P], [xhl[:, u, l, j * P:(j + 1) * P] for l in range(2)],
                                    [w_hl[:, l, 2, :] for l in range(2)])
                last.then_inc(s.v_psum, 1)

            def et(k, ring, u):
                c = 2 * k + u
                need(pe, s.e_done, c + 1)
                need(pe, s.et_done, c)
                if u == 0:
                    need(pe, s.oth_done, c - 4)
                for j in range(TILES):
                    last = t.transpose(bank_t[:, j * P:(j + 1) * P], sm[:, u, j * P:(j + 1) * P], ident)
                last.then_inc(s.et_psum, 1)

            def sums(k, ring):
                need(pe, s.et_done, 2 * k + 2)
                need(pe, s.p_done, 2 * k)
                e4 = pt[:].rearrange("p u (g q) -> p q u g", q=A)
                for q in range(A):
                    lo = SP_ * (q % 2)
                    dst = bank_d[lo:lo + SP_, (q // 2) * 64:(q // 2 + 1) * 64]
                    last = t.matmul(dst, msum[:, q, :], e4[:, q], start=True, stop=True)
                last.then_inc(s.d_psum, 1)

            def weights(k, ring):
                need(pe, s.recip_done, k + 1)
                need(pe, s.p_done, 2 * k)
                for q in range(A):
                    lo = SP_ * (q % 2)
                    last = t.matmul(ps[:, 6 + q % 2, (q // 2) * 64:(q // 2 + 1) * 64], mspread[lo:lo + S * 8, q // 2, :],
                                    recip[lo:lo + S * 8, q // 2, :], start=True, stop=True)
                last.then_inc(s.w_psum, 1)

            def pv(k, ring, u):
                e, slot = 2 * k + u, 2 * ring + u
                need(pe, s.bdp_done, e + 1)
                if u:
                    need(pe, s.o32_done, e)
                else:
                    need(pe, s.vh_done, most(e + 6, B))
                    need(pe, s.vl_done, e + 2)
                for j in range(TILES):
                    for h in range(H):
                        n = j * H + h
                        last = products(bank_vo[:, n * HD:(n + 1) * HD], [bdp[:, u, l, n] for l in range(2)],
                                        [vhl[:, slot, l, n * HD:(n + 1) * HD] for l in range(2)])
                last.then_inc(s.o_psum, 1)

            def ot(k, ring, u):
                e = 2 * k + u
                need(pe, s.o32_done, e + 1)
                need(pe, s.oth_done, e)
                if u == 0:
                    need(pe, s.et_done, most(e + 6, B))
                for j in range(TILES):
                    last = t.transpose(bank_t[:, j * P:(j + 1) * P], o32[:, u, j * P:(j + 1) * P], ident)
                last.then_inc(s.ot_psum, 1)

            def y(k, ring, u):
                e = 2 * k + u
                need(pe, s.otl_done, e + 1)
                need(pe, s.x1_done, e)
                if u == 0:
                    need(pe, s.xi_done, most(e + 8, B))
                t.matmul(bank_xy, ones16[0:64, :], bo_hl[:], start=True, stop=False)
                for j in range(TILES):
                    o = bank_xy[:, j * P:(j + 1) * P]
                    last = products(o, [othl[:, u, l, j * P:(j + 1) * P] for l in range(2)],
                                    [w_hl[:, l, 3, :] for l in range(2)], start=False, stop=j == TILES - 1)
                last.then_inc(s.y_psum, 1)

            pipelined(pe, PAIRS, 4, 3, [
                (1, qk, 0), (3, pv, 0), (2, weights), (0, xT, 0), (1, qk, 1), (1, et, 0), (0, xT, 1), (0, q_k, 0),
                (1, et, 1), (3, pv, 1), (3, ot, 0), (1, sums), (0, v, 0), (3, ot, 1), (3, y, 0), (0, q_k, 1),
                (0, v, 1), (3, y, 1),
            ])

        @block.vector
        def _(dve):
            v = nc.vector
            steps = [0]

            def step(ins):
                ins.then_inc(s.setup_v, 1)
                steps[0] += 1
                dve.wait_ge(s.setup_v, steps[0])

            dve.wait_ge(s.consts_in, 16)
            dve.wait_ge(s.masks_in, 16)
            step(v.memset(ones16[:], 1.0))
            step(v.tensor_scalar(mflt[:], mraw[:], 0.0, None, ALU.is_gt))
            step(v.tensor_tensor(mflt[:], mflt[:], const(cst, "eye_qk")[0:S * A, :], ALU.max))
            step(v.tensor_copy(mrep[:], mflt[:].rearrange("p (o k) -> p o k", o=1).to_broadcast([S * A, H, A])))
            step(v.memset(bo_hl[:], 0.0))
            dve.wait_ge(s.weights_in, 16 * 8)
            step(v.tensor_scalar(w_f[:], wstage[:], WS, None, ALU.mult))
            step(v.tensor_copy(w_hl[:, 0], w_f[:]))
            step(v.tensor_tensor(w_hl[:, 1], w_f[:], w_hl[:, 0], ALU.subtract))
            dve.wait_ge(s.setup_pe, 1)
            step(v.tensor_copy(mkq[:].rearrange("p s q -> p (s q)"), ps[:, 4, 0:S * A]))
            for n in range(8):
                step(v.tensor_scalar(msum[:, :, n * S:(n + 1) * S], mkq[:].rearrange("p s q -> p q s"),
                                     block8[:, n:n + 1], None, ALU.mult))
            step(v.tensor_copy(msum[:, :, 8 * S:SP_], msum[:, :, 0:SP_ - 8 * S]))
            dve.wait_ge(s.setup_pe, 2)
            step(v.tensor_copy(embT[:], ps[:, 5, 0:A]))
            dve.wait_ge(s.setup_pe, 3)
            step(v.tensor_tensor(brow[:], ps[0:1, 6, 0:C], bo_row[:], ALU.add))
            step(v.tensor_scalar(brow[:], brow[:], WS, None, ALU.mult))
            row = brow[:].rearrange("p (o c) -> p o c", o=1).to_broadcast([1, TILES, C])
            hi, lo = (bo_hl[r:r + 1, :].rearrange("p (o c) -> p o c", o=TILES) for r in (0, 32))
            step(v.tensor_copy(hi, row))
            step(v.tensor_copy(lo, row))
            step(v.tensor_tensor(brow[:], brow[:], bo_hl[0:1, 0:C], ALU.subtract))
            step(v.tensor_copy(lo, row))

            with dve.Fori(0, B // 4) as m:
                for u in range(4):
                    dve.wait_ge(s.gT_psum, 4 * m + u + 1)
                    v.bn_stats(gst6[:, 4 * m + u, :], ps[:, u, :]).then_inc(s.gst_done, 1)
            dve.wait_ge(s.gst_done, B)
            even, dev_even, odd, dev_odd = (gst6[:, :, n] for n in (1, 2, 4, 5))
            step(v.tensor_tensor(gtmp[:, 0, :], even, even, ALU.mult))
            step(v.tensor_tensor(gtmp[:, 1, :], odd, odd, ALU.mult))
            step(v.tensor_tensor(gtmp[:, 1, :], gtmp[:, 0, :], gtmp[:, 1, :], ALU.add))
            step(v.tensor_tensor(gtmp[:, 0, :], dev_even, dev_odd, ALU.add))
            step(v.scalar_tensor_tensor(gsum[:, 1, :], gtmp[:, 0, :], 2.0 / TOK, gtmp[:, 1, :], ALU.mult, ALU.add))
            v.tensor_tensor(gsum[:, 0, :], even, odd, ALU.add).then_inc(s.gsum_done, 1)
            dve.wait_ge(s.setup_pe, 4)
            for q4 in range(4):
                src = ps[0:SP_, q4, :].rearrange("p (n r c) -> p n r c", n=2, r=2)
                for r in range(2):
                    ins = v.tensor_copy(mspread[SP_ * r:SP_ * (r + 1), 2 * q4:2 * q4 + 2, :], src[:, :, r, :])
            ins.then_inc(s.spread_done, 1)
            dve.wait_ge(s.spread_done, 1)
            dve.wait_ge(s.gmean_psum, 1)
            v.tensor_copy(gmean[:].rearrange("p n b -> p (n b)"), ps[:, 7, 0:2 * B]).then_inc(s.gst_done, 1)
            dve.wait_ge(s.gst_done, B + 1)
            step(v.tensor_tensor(gtmp[:, 0, :], gmean[:, 0, :], gmean[:, 0, :], ALU.mult))
            v.scalar_tensor_tensor(gtmp[:, 1, :], gmean[:, 1, :], GN_EPS, gtmp[:, 0, :], ALU.add, ALU.subtract).then_inc(s.gvar_done, 1)
            dve.wait_ge(s.rstd_done, 1)
            step(v.scalar_tensor_tensor(nmr[:], gmean[:, 0, :], -1.0, rstd[:], ALU.mult, ALU.mult))
            step(v.tensor_tensor(shift[:], embT[:].rearrange("p (o a) -> p o a", o=1).to_broadcast([P, B, A]),
                                 nmr[:].rearrange("p (b o) -> p b o", o=1).to_broadcast([P, B, A]), ALU.add))

            def xi_(k, ring, u):
                b = 2 * k + u
                need(dve, s.xT_psum, b + 1)
                need(dve, s.xl_done, b - 1)
                need(dve, s.xh_done, b - 1)
                v.scalar_tensor_tensor(xi[:, u, :].rearrange("p (t a) -> p t a", a=A), bank_xy.rearrange("p (a t) -> p t a", a=A),
                                       rstd[:, bass.ds(b, 1)],
                                       shift[:, bass.ds(b, 1), :].to_broadcast([P, T, A]), ALU.mult, ALU.add).then_inc(s.xi_done, 1)

            def shifted(k, ring, u):
                c = 2 * k + u
                need(dve, s.s_psum, c + 1)
                s3 = bank_s.rearrange("p (t k) -> p t k", k=A)
                v.tensor_reduce(rmax[:, u, :], s3, AX.X, ALU.max).then_inc(s.rmax_done, 1)
                need(dve, s.rmax_done, c + 1)
                need(dve, s.et_psum, c - 1)
                v.tensor_tensor(sm[:, u, :].rearrange("p (t k) -> p t k", k=A), s3,
                                rmax[:, u, :].rearrange("p (t o) -> p t o", o=1).to_broadcast([P, T, A]), ALU.subtract).then_inc(s.sm_done, 1)

            def p(k, ring, u):
                need(dve, s.w_psum, k + 1)
                w = ps[:, 6:8, :].rearrange("p r (n u g) -> p u g n r", n=A // 2, u=2)[:, u]
                e4 = pt[:, u, :].rearrange("p (g n r) -> p g n r", n=A // 2, r=2)
                v.tensor_tensor(e4, e4, w, ALU.mult).then_inc(s.p_done, 1)

            def spread(dst, src, done):
                for n in range(8):
                    ins = v.tensor_scalar(dst[:, :, :, n, :], src.rearrange("p l (g q) -> p l g q", q=A), block8[:, n:n + 1], None, ALU.mult)
                ins.then_inc(done, 1)

            def spread_q(k, ring, u):
                need(dve, s.qh_done, 2 * k + u + 1)
                need(dve, s.ql_done, 2 * k + u + 1)
                need(dve, s.s_psum, 2 * k + u - 1)
                spread(bdq[:, u], qhl[:, u], s.bdq_done)

            def spread_p(k, ring, u):
                need(dve, s.ph_done, 2 * k + u + 1)
                need(dve, s.pl_done, 2 * k + u + 1)
                need(dve, s.o_psum, 2 * k + u - 1)
                spread(bdp[:, u], phl[:, u], s.bdp_done)

            def reciprocals(k, ring):
                need(dve, s.d_psum, k + 1)
                need(dve, s.w_psum, k)
                v.reciprocal(recip[:].rearrange("p n g -> p (n g)"), bank_d).then_inc(s.recip_done, 1)

            def add(k, ring, u):
                e = 2 * k + u
                need(dve, s.y_psum, e + 1)
                r = resid[:, e, :]
                v.scalar_tensor_tensor(r, bank_xy, 1.0 / WS, r, ALU.mult, ALU.add).then_inc(s.x1_done, 1)

            dve.wait_ge(s.resid_in, 16 * B)
            pipelined(dve, PAIRS, 4, 3, [
                (1, shifted, 0), (2, p, 0), (2, p, 1), (0, xi_, 0), (1, shifted, 1), (0, xi_, 1), (2, spread_p, 0),
                (0, spread_q, 0), (3, add, 0), (1, reciprocals), (2, spread_p, 1), (3, add, 1), (0, spread_q, 1),
            ])


def chain(eng, sem, base):
    done = [0]

    def step(ins, wait=True):
        ins.then_inc(sem, 1)
        done[0] += 1
        if wait:
            eng.wait_ge(sem, base + done[0])
    return step


def token_mixer(nc, cst, resid, ones16, ident, late, ffn, rows_dram, Wq, bq, Wk, bk, Wv, bv, router_w, router_b,
                gate_up, gate_up_bias, down, down_bias):
    rank_of = const(cst, "rank_of")
    w1_hl, b1_hl, w2_hl, b2_hl = ffn["w1_hl"], ffn["b1_hl"], ffn["w2_hl"], ffn["b2_hl"]
    with ExitStack() as ctx:
        def sb(name, shape, dt=F32):
            return ctx.enter_context(nc.sbuf_tensor(name, shape, dt))

        wq = sb("m_wq", [P, C])
        wkv = sb("m_wkv", [P, 2, C])
        wr = sb("m_wr", [P, E])
        bq_col = sb("m_bq", [P, 1])
        bkv_f = sb("m_bkv_f", [1, 2, C])
        bkv_t = sb("m_bkv_t", [1, 2, C])
        bkv_hl = sb("m_bkv_hl", [64, 2, 2 * C], F16)
        rb = sb("m_rb", [P, E])
        w1_f = sb("m_w1_f", [P, E, 2 * I])
        w2_f = sb("m_w2_f", [P, E, 2, C])
        b1_f = sb("m_b1_f", [1, E * 2 * I])
        b2_f = sb("m_b2_f", [1, E * C])
        before16 = sb("m_before16", [P, P], F16)
        half = sb("m_half", [P, 8])
        st6 = sb("m_st6", [P, 2, 8, 6])
        stw = sb("m_stw", [P, 2, 6, 8])
        xn = sb("m_xn", [P, 2, TOK])
        xt = sb("m_xt", [P, 2, TOK])
        ef = sb("m_ef", [P, 2, TOK])
        rf = sb("m_rf", [P, 2, TOK])
        qf = sb("m_qf", [P, 2, TOK])
        kf = sb("m_kf", [P, 2, TOK])
        vo = sb("m_vo", [P, 2, TILES, C + 2])
        kv = sb("m_kv", [P, 2, C + H])
        den = sb("m_den", [P, 2, TILES, H])
        mix = sb("m_mix", [P, TOK])
        xn2 = sb("m_xn2", [P, 2, TOK])
        xt2 = sb("m_xt2", [P, 2, TOK])
        rows = sb("m_rows", [P, 4, TILES, ROW])
        place = sb("m_place", [P, 4, TILES, 2], I32)
        lg = sb("m_lg", [P, 8, E])
        oh = sb("m_oh", [P, 2, 8, E])
        tmp = sb("m_tmp", [P, 2, 8, E])
        best = sb("m_best", [P, 8, 8])
        oh16 = sb("m_oh16", [P, 8, E], F16)
        ahead16 = sb("m_ahead16", [P, 9, E], F16)
        spot = sb("m_spot", [P, 8, E])

        ps = ctx.enter_context(nc.psum_tensor("m_ps", [P, 8, TOK], F32))
        bank_x, bank_q, banks_kv, bank_s, banks_o, bank_r = ps[:, 0], ps[:, 1], ps[:, 2:4], ps[:, 4], ps[:, 5:7], ps[:, 7]

        s = Named({n: ctx.enter_context(nc.semaphore("m_" + n)) for n in """
            small_in w1_in w2_in b_in set_v set_a set_g kv_bias w1f_done w1h_done
            stat1 stat2 pow1 pow2 norm1 xT xt_done q_psum kv_psum qe_done ke_done v_done qf_done kf_done
            s_psum kv_done o_psum mix_step add_done norm2 hi_done lo_done xT2 xt2_done lg_psum route ew_done
            rank_psum place_step place_done rows_out table late_in""".split()})

        block = ctx.enter_context(nc.Block())

        @block.sync
        def _(sp):
            sp.dma_start(cst[:], late).then_inc(s.late_in, 16)
            sp.dma_start(wq[:], Wq).then_inc(s.small_in, 16)
            sp.dma_start(wkv[:, 0, :], Wk).then_inc(s.small_in, 16)
            sp.dma_start(wkv[:, 1, :], Wv).then_inc(s.small_in, 16)
            sp.dma_start(wr[:], router_w).then_inc(s.small_in, 16)
            sp.dma_start(bq_col[:], bq.rearrange("(c o) -> c o", o=1)).then_inc(s.small_in, 16)
            sp.dma_start(bkv_f[:, 0, :], bk.rearrange("(o c) -> o c", o=1)).then_inc(s.small_in, 16)
            sp.dma_start(bkv_f[:, 1, :], bv.rearrange("(o c) -> o c", o=1)).then_inc(s.small_in, 16)
            sp.dma_start(rb[:], router_b.rearrange("(o e) -> o e", o=1).to_broadcast([P, E])).then_inc(s.small_in, 16)
            sp.dma_start(w1_f[:], gate_up.rearrange("e c i -> c e i")).then_inc(s.w1_in, 16)
            sp.dma_start(w2_f[:], down.rearrange("e (n i) c -> i e n c", n=2)).then_inc(s.w2_in, 16)
            sp.dma_start(b1_f[:], gate_up_bias.rearrange("(o e) i -> o (e i)", o=1)).then_inc(s.b_in, 16)
            sp.dma_start(b2_f[:], down_bias.rearrange("(o e) c -> o (e c)", o=1)).then_inc(s.b_in, 16)

        @block.gpsimd
        def _(pool):
            g = nc.gpsimd
            g.memset(half[:], -0.5).then_inc(s.set_g, 1)
            pool.wait_ge(s.set_g, 1)

            def power(k, ring, n, stat, steps, norm, pow_done):
                pool.wait_ge(stat, steps * (k + 1))
                need(pool, norm, 2 * k)
                g.tensor_tensor(stw[:, n, 5, :], stw[:, n, 4, :], half[:], ALU.pow).then_inc(pow_done, 1)

            def rows_ready(k, ring):
                pool.wait_ge(s.place_done, k + 1)
                pool.wait_ge(s.lo_done, 2 * k + 2)
                need(pool, s.rows_out, 16 * 16 * k)

            def send(k, ring, u):
                slot = 2 * ring + u
                for j in range(TILES):
                    for n in range(2):
                        g.indirect_dma_start(rows_dram, bass.IndirectOffsetOnAxis(ap=place[:, slot, j, n:n + 1], axis=0),
                                             rows[:, slot, j, :], None).then_inc(s.rows_out, 16)

            pipelined(pool, PAIRS, 6, 2, [
                (5, rows_ready), (0, power, 0, s.stat1, LN_STEPS, s.norm1, s.pow1),
                (3, power, 1, s.stat2, LN_STEPS, s.norm2, s.pow2), (5, send, 0), (5, send, 1),
            ])
            pool.wait_ge(s.rows_out, 16 * 16 * PAIRS)

        @block.scalar
        def _(act):
            a = nc.scalar
            act.wait_ge(s.small_in, 16 * 8)
            act.wait_ge(s.w1_in, 16)
            a.activation(w1_f[:], w1_f[:], ACT.Copy, scale=2 * WS).then_inc(s.w1f_done, 1)
            act.wait_ge(s.w2_in, 16)
            a.activation(w2_f[:], w2_f[:], ACT.Copy, scale=WS).then_inc(s.w1f_done, 1)
            act.wait_ge(s.w1f_done, 2)
            a.activation(w1_hl[:, :, 0, :], w1_f[:], ACT.Copy).then_inc(s.w1h_done, 1)
            a.activation(w2_hl[:, :, 0], w2_f[:], ACT.Copy).then_inc(s.w1h_done, 1)

            def xt_(k, ring, u):
                b = 2 * k + u
                need(act, s.xT, b + 1)
                need(act, s.kv_psum, b - 1)
                need(act, s.q_psum, b - 1)
                a.activation(xt[:, u, :], bank_x, ACT.Copy).then_inc(s.xt_done, 1)

            def q(k, ring, u):
                b = 2 * k + u
                need(act, s.q_psum, b + 1)
                need(act, s.qf_done, b)
                a.activation(ef[:, 0, :], bank_q, ACT.Exp, bias=bq_col[:]).then_inc(s.qe_done, 1)
                a.activation(rf[:, 0, :], bank_q, ACT.Relu, bias=bq_col[:]).then_inc(s.qe_done, 1)

            def k_v(k, ring, u):
                b = 2 * k + u
                need(act, s.kv_psum, b + 1)
                need(act, s.kf_done, b)
                kv4 = banks_kv.rearrange("p n (i w c) -> p (n i) w c", i=2, w=2)
                a.activation(ef[:, 1, :].rearrange("p (j c) -> p j c", j=TILES), kv4[:, :, 0, :], ACT.Exp).then_inc(s.ke_done, 1)
                a.activation(rf[:, 1, :].rearrange("p (j c) -> p j c", j=TILES), kv4[:, :, 0, :], ACT.Relu).then_inc(s.ke_done, 1)
                need(act, s.s_psum, b - 1)
                a.activation(vo[:, u, :, 0:C], kv4[:, :, 1, :], ACT.Copy).then_inc(s.v_done, 1)

            def xt2_(k, ring, u):
                d = 2 * k + u
                need(act, s.xT2, d + 1)
                need(act, s.lg_psum, d - 1)
                a.activation(xt2[:, u, :], bank_r, ACT.Copy).then_inc(s.xt2_done, 1)

            def hi(k, ring, u):
                d, slot = 2 * k + u, 2 * ring + u
                need(act, s.norm2, d + 1)
                need(act, s.rows_out, 16 * 16 * (k - 1))
                dst = rows[:, slot].bitcast(F16)[:, :, 0:C]
                a.activation(dst, xn2[:, u, :].rearrange("p (j c) -> p j c", j=TILES), ACT.Copy).then_inc(s.hi_done, 1)

            def ew(k, ring):
                need(act, s.route, ROUTE_STEPS * k + 13)
                a.activation(best[:, 3, :], best[:, 2, :], ACT.Exp).then_inc(s.ew_done, 1)

            pipelined(act, PAIRS, 6, 2, [
                (1, xt_, 0), (4, xt2_, 0), (4, xt2_, 1), (1, xt_, 1), (1, q, 0), (1, k_v, 0), (4, ew), (1, q, 1),
                (4, hi, 0), (4, hi, 1), (1, k_v, 1),
            ])

        @block.tensor
        def _(pe):
            t = nc.tensor
            pe.wait_ge(s.set_v, 11)

            def xT(k, ring, u):
                b = 2 * k + u
                need(pe, s.norm1, b + 1)
                need(pe, s.xt_done, b)
                if u == 0:
                    need(pe, s.place_done, k - 3)
                for j in range(TILES):
                    last = t.transpose(bank_x[:, j * P:(j + 1) * P], xn[:, u, j * P:(j + 1) * P], ident)
                last.then_inc(s.xT, 1)

            def q(k, ring, u):
                b = 2 * k + u
                need(pe, s.xt_done, b + 1)
                need(pe, s.qe_done, 2 * b)
                t.matmul(bank_q, wq[:], xt[:, u, :], start=True, stop=True).then_inc(s.q_psum, 1)

            def k_v(k, ring, u):
                b = 2 * k + u
                need(pe, s.xt_done, b + 1)
                need(pe, s.v_done, b)
                for n in range(2):
                    t.matmul(banks_kv[:, n], ones16[0:64, :], bkv_hl[:].rearrange("p i c -> p (i c)"), start=True, stop=False)
                    for i in range(2):
                        j = 2 * n + i
                        last = t.matmul(banks_kv[:, n, i * 2 * C:(i + 1) * 2 * C], xt[:, u, j * P:(j + 1) * P],
                                        wkv[:].rearrange("p w c -> p (w c)"), start=False, stop=i == 1)
                last.then_inc(s.kv_psum, 1)

            def sums(k, ring, u):
                c = 2 * k + u
                need(pe, s.kf_done, c + 1)
                need(pe, s.v_done, c + 1)
                need(pe, s.kv_done, c)
                for j in range(TILES):
                    last = t.matmul(bank_s[:, 0:C + 2], kf[:, u, j * P:(j + 1) * P], vo[:, u, j, :], start=j == 0, stop=j == TILES - 1)
                last.then_inc(s.s_psum, 1)

            def outs(k, ring, u):
                c = 2 * k + u
                need(pe, s.kv_done, c + 1)
                need(pe, s.qf_done, c + 1)
                need(pe, s.add_done, c)
                for j in range(TILES):
                    last = t.matmul(banks_o[:, j // 2, (j % 2) * 256:(j % 2) * 256 + C + H], qf[:, u, j * P:(j + 1) * P], kv[:, u, :],
                                    start=True, stop=True)
                last.then_inc(s.o_psum, 1)

            def xT2(k, ring, u):
                d = 2 * k + u
                need(pe, s.norm2, d + 1)
                need(pe, s.xt2_done, d)
                for j in range(TILES):
                    last = t.transpose(bank_r[:, j * P:(j + 1) * P], xn2[:, u, j * P:(j + 1) * P], ident)
                last.then_inc(s.xT2, 1)

            def logits(k, ring, u):
                need(pe, s.xt2_done, 2 * k + u + 1)
                need(pe, s.place_done, k)
                need(pe, s.xt_done, most(2 * k + 8, B))
                for j in range(TILES):
                    n = (u * TILES + j) * E
                    last = t.matmul(bank_x[:, n:n + E], xt2[:, u, j * P:(j + 1) * P], wr[:], start=True, stop=True)
                last.then_inc(s.lg_psum, 1)

            def ranks(k, ring):
                need(pe, s.route, ROUTE_STEPS * k + ROUTE_STEPS)
                flat = bank_x[:, 64:64 + 8 * E]
                t.matmul(flat, before16[:], oh16[:].rearrange("p n e -> p (n e)"), start=True, stop=False)
                t.matmul(flat, ones16[:], ahead16[:, 0:8, :].rearrange("p n e -> p (n e)"), start=False, stop=True).then_inc(s.rank_psum, 1)

            pipelined(pe, PAIRS, 6, 2, [
                (2, sums, 0), (2, sums, 1), (1, xT, 0), (2, outs, 0), (1, xT, 1), (4, xT2, 0), (4, xT2, 1),
                (4, logits, 0), (4, logits, 1), (1, q, 0), (1, k_v, 0), (1, q, 1), (2, outs, 1), (4, ranks),
                (1, k_v, 1),
            ])
            pe.wait_ge(s.place_done, PAIRS)
            t.matmul(bank_s[:, 0:E], ones16[:], ahead16[:, 0, :], start=True, stop=True).then_inc(s.rank_psum, 1)

        @block.vector
        def _(dve):
            v = nc.vector
            dve.wait_ge(s.small_in, 16 * 8)
            dve.wait_ge(s.late_in, 16)
            step = chain(dve, s.set_v, 0)
            step(v.tensor_scalar(wq[:], wq[:], 2.0, None, ALU.mult), False)
            step(v.tensor_scalar(wkv[:], wkv[:], 2.0, None, ALU.mult), False)
            step(v.tensor_scalar(wr[:], wr[:], 2.0, None, ALU.mult), False)
            step(v.memset(bkv_hl[:], 0.0), False)
            step(v.memset(vo[:, :, :, C:C + 1], 1.0), False)
            step(v.memset(vo[:, :, :, C + 1:C + 2], 0.0), False)
            step(v.memset(ahead16[:], 0.0), False)
            step(v.tensor_copy(before16[:], const(cst, "before")))
            row = bkv_f[:].rearrange("p w c -> p (w c)")
            both = row.rearrange("p (o c) -> p o c", o=1).to_broadcast([1, 2, 2 * C])
            step(v.tensor_copy(bkv_hl[0:1], both))
            tmp_row = bkv_t[:].rearrange("p w c -> p (w c)")
            step(v.tensor_tensor(tmp_row, row, bkv_hl[0:1, 0, :], ALU.subtract))
            step(v.tensor_copy(bkv_hl[32:33], tmp_row.rearrange("p (o c) -> p o c", o=1).to_broadcast([1, 2, 2 * C])))
            step(v.memset(b1_hl[:], 0.0), False)
            step(v.memset(b2_hl[:], 0.0))
            dve.wait_ge(s.b_in, 32)
            for f, hl in ((b1_f[:], b1_hl[:].rearrange("p e i -> p (e i)")), (b2_f[:], b2_hl[:].rearrange("p e c -> p (e c)"))):
                step(v.tensor_scalar(f, f, WS, None, ALU.mult))
                step(v.tensor_copy(hl[0:1, :], f))
                step(v.tensor_tensor(f, f, hl[0:1, :], ALU.subtract))
                step(v.tensor_copy(hl[32:33, :], f))
            dve.wait_ge(s.w1h_done, 2)
            step(v.tensor_tensor(w1_hl[:, :, 1, :], w1_f[:], w1_hl[:, :, 0, :], ALU.subtract))
            step(v.tensor_tensor(w2_hl[:, :, 1], w2_f[:], w2_hl[:, :, 0], ALU.subtract))

            def stats(k, ring, n, sem):
                b = 2 * k
                step = chain(dve, sem, LN_STEPS * k)
                if n == 1:
                    dve.wait_ge(s.late_in, 16)
                    need(dve, s.add_done, b + 2)
                for u in range(2):
                    for j in range(TILES):
                        ins = v.bn_stats(st6[:, n, u * TILES + j, :], resid[:, b + u, j * C:(j + 1) * C])
                step(ins)
                even, dev_even, odd, dev_odd = (st6[:, n, :, i] for i in (1, 2, 4, 5))
                w = stw[:, n]
                step(v.tensor_tensor(w[:, 0], even, odd, ALU.subtract), False)
                step(v.tensor_tensor(w[:, 1], even, odd, ALU.add), False)
                step(v.scalar_tensor_tensor(w[:, 2], dev_even, C * LN_EPS, dev_odd, ALU.add, ALU.add))
                step(v.tensor_tensor(w[:, 0], w[:, 0], w[:, 0], ALU.mult), False)
                step(v.tensor_scalar(w[:, 3], w[:, 1], 0.5, None, ALU.mult))
                step(v.scalar_tensor_tensor(w[:, 4], w[:, 2], 4.0 / C, w[:, 0], ALU.mult, ALU.add))

            def norm(k, ring, u, n, dst, pow_done, done):
                b = 2 * k + u
                need(dve, pow_done, k + 1)
                if n == 0:
                    need(dve, s.xT, b - 1)
                else:
                    need(dve, s.xT2, b - 1)
                    need(dve, s.lo_done, b - 1)
                for j in range(TILES):
                    i = u * TILES + j
                    ins = v.tensor_scalar(dst[:, u, j * C:(j + 1) * C], resid[:, b, j * C:(j + 1) * C],
                                          stw[:, n, 3, i:i + 1], stw[:, n, 5, i:i + 1], ALU.subtract, ALU.mult)
                ins.then_inc(done, 1)

            def feature(k, ring, u):
                b = 2 * k + u
                need(dve, s.qe_done, 2 * b + 2)
                need(dve, s.o_psum, b - 1)
                v.scalar_tensor_tensor(qf[:, u, :], ef[:, 0, :], 1.0, rf[:, 0, :], ALU.min, ALU.add).then_inc(s.qf_done, 1)
                need(dve, s.ke_done, 2 * b + 2)
                need(dve, s.s_psum, b - 1)
                v.scalar_tensor_tensor(kf[:, u, :], ef[:, 1, :], 1.0, rf[:, 1, :], ALU.min, ALU.add).then_inc(s.kf_done, 1)

            def keys_values(k, ring, u):
                c = 2 * k + u
                need(dve, s.s_psum, c + 1)
                need(dve, s.o_psum, c - 1)
                v.tensor_tensor(kv[:, u, 0:C], bank_s[:, 0:C], const(cst, "block_kv"), ALU.mult)
                v.tensor_tensor(kv[:, u, C:C + H], bank_s[:, C:C + 1].to_broadcast([P, H]), const(cst, "block_ks"), ALU.mult).then_inc(s.kv_done, 1)

            def mixed(k, ring, u):
                c = 2 * k + u
                step = chain(dve, s.mix_step, 3 * c)
                need(dve, s.o_psum, c + 1)
                need(dve, s.add_done, c)
                o4 = banks_o.rearrange("p n (i c) -> p (n i) c", i=2)
                step(v.tensor_scalar(den[:, 0], o4[:, :, C:C + H], ATT_EPS / TOK, None, ALU.add))
                step(v.reciprocal(den[:, 1], den[:, 0]))
                weight = den[:, 1].rearrange("p j (h o) -> p j h o", o=1).to_broadcast([P, TILES, H, HD])
                step(v.tensor_tensor(mix[:].rearrange("p (j h d) -> p j h d", j=TILES, h=H),
                                     o4[:, :, 0:C].rearrange("p j (h d) -> p j h d", h=H), weight, ALU.mult))
                v.tensor_tensor(resid[:, c, :], resid[:, c, :], mix[:], ALU.add).then_inc(s.add_done, 1)

            def lo(k, ring, u):
                d, slot = 2 * k + u, 2 * ring + u
                need(dve, s.hi_done, d + 1)
                r = rows[:, slot].bitcast(F16)
                v.tensor_tensor(r[:, :, C:2 * C], xn2[:, u, :].rearrange("p (j c) -> p j c", j=TILES), r[:, :, 0:C],
                                ALU.subtract).then_inc(s.lo_done, 1)

            def route(k, ring):
                step = chain(dve, s.route, ROUTE_STEPS * k)
                need(dve, s.lg_psum, 2 * k + 2)
                shape = [P, 8, E]
                wide = lambda ap: ap.rearrange("p (n o) -> p n o", o=1).to_broadcast(shape)
                rank3 = rank_of.rearrange("p (n e) -> p n e", e=E)
                bias = rb[:].rearrange("p (o e) -> p o e", o=1).to_broadcast(shape)
                step(v.tensor_tensor(lg[:], bank_x[:, 0:8 * E].rearrange("p (n e) -> p n e", e=E), bias, ALU.add))
                for n in range(2):
                    step(v.tensor_reduce(best[:, n, :], lg[:], AX.X, ALU.max))
                    step(v.tensor_tensor(tmp[:, n], lg[:], wide(best[:, n, :]), ALU.is_equal))
                    step(v.tensor_tensor(tmp[:, n], tmp[:, n], rank3, ALU.mult))
                    step(v.tensor_reduce(best[:, 4 + n, :], tmp[:, n], AX.X, ALU.max))
                    if n == 0:
                        step(v.tensor_tensor(oh[:, 0], tmp[:, 0], wide(best[:, 4, :]), ALU.is_equal))
                        step(v.scalar_tensor_tensor(lg[:], oh[:, 0], -3e38, lg[:], ALU.mult, ALU.add))
                step(v.tensor_tensor(oh[:, 1], tmp[:, 1], wide(best[:, 5, :]), ALU.is_equal), False)
                step(v.tensor_tensor(best[:, 2, :], best[:, 1, :], best[:, 0, :], ALU.subtract))
                step(v.tensor_tensor(oh16[:], oh[:, 0], oh[:, 1], ALU.add))
                for n in range(8):
                    step(v.tensor_tensor(ahead16[:, n + 1, :], ahead16[:, n, :], oh16[:, n, :], ALU.add))

            def placed(k, ring):
                d, slot = 2 * k, 2 * ring
                step = chain(dve, s.place_step, PLACE_STEPS * k)
                need(dve, s.ew_done, k + 1)
                step(v.tensor_scalar(best[:, 6, :], best[:, 3, :], 1.0, None, ALU.add))
                step(v.reciprocal(best[:, 7, :], best[:, 6, :]))
                step(v.tensor_tensor(best[:, 6, :], best[:, 3, :], best[:, 7, :], ALU.mult))
                step(v.tensor_tensor(best[:, 7, :], best[:, 7, :], best[:, 6, :], ALU.subtract))
                w3 = lambda n: best[:, n, :].rearrange("p (u j) -> p u j", u=2)
                word = lambda n: rows[:, slot:slot + 2, :, C + n]
                step(v.tensor_scalar(word(0), w3(6), 1.0 / WS, None, ALU.mult), False)
                step(v.tensor_scalar(word(1), w3(7), 1.0 / WS, None, ALU.mult), False)
                step(v.tensor_copy(word(2), w3(4)), False)
                ids = const(cst, "slot1").rearrange("p (b j) -> p b j", j=TILES)
                step(v.tensor_copy(word(3), ids[:, bass.ds(d, 2), :]), False)
                need(dve, s.rank_psum, k + 1)
                region = const(cst, "region").rearrange("p (n e) -> p n e", e=E)
                step(v.tensor_tensor(spot[:], bank_x[:, 64:64 + 8 * E].rearrange("p (n e) -> p n e", e=E), region, ALU.add))
                step(v.tensor_tensor(tmp[:, 0], spot[:], oh[:, 0], ALU.mult), False)
                step(v.tensor_tensor(tmp[:, 1], spot[:], oh[:, 1], ALU.mult))
                for n in range(2):
                    step(v.tensor_reduce(best[:, n, :], tmp[:, n], AX.X, ALU.add))
                    v_place = place[:, slot:slot + 2, :, n]
                    step(v.tensor_copy(v_place, w3(n)))
                v.tensor_copy(ahead16[:, 0, :], ahead16[:, 8, :]).then_inc(s.place_done, 1)
                need(dve, s.place_done, k + 1)

            pipelined(dve, PAIRS, 6, 2, [
                (4, norm, 0, 1, xn2, s.pow2, s.norm2), (2, keys_values, 0), (1, norm, 0, 0, xn, s.pow1, s.norm1),
                (1, norm, 1, 0, xn, s.pow1, s.norm1), (0, stats, 0, s.stat1), (4, norm, 1, 1, xn2, s.pow2, s.norm2),
                (3, stats, 1, s.stat2), (2, keys_values, 1), (4, route), (2, mixed, 0), (1, feature, 0),
                (2, mixed, 1), (4, lo, 0), (4, lo, 1), (1, feature, 1), (4, placed),
            ])
            dve.wait_ge(s.rank_psum, PAIRS + 1)
            step = chain(dve, s.table, 0)
            cnt, cnti, nb, delta, cum = (ffn[n] for n in ("cnt", "cnti", "nb", "delta", "cum"))
            step(v.tensor_copy(cnt[:], bank_s[:, 0:E]))
            step(v.tensor_tensor(ffn["tail_i"][:], cnt[:], const(cst, "region")[:, 0:E], ALU.add), False)
            step(v.tensor_scalar(cnti[:], cnt[:], float(BLOCK - 1), None, ALU.add))
            step(v.tensor_scalar(cnti[:], cnti[:], BLOCK.bit_length() - 1, None, ALU.arith_shift_right))
            step(v.tensor_copy(nb[:], cnti[:]))
            step(v.tensor_scalar(delta[:], nb[:], -float(BLOCK), float(REGION), ALU.mult, ALU.add))
            step(v.tensor_copy(cum[:], nb[:]))
            for e in range(1, E):
                step(v.tensor_tensor(cum[:, e:e + 1], cum[:, e - 1:e], nb[:, e:e + 1], ALU.add))
            expert, first, over = ffn["expert"], ffn["first"], ffn["over"]
            number = const(cst, "block_no")
            step(v.memset(expert[:], float(E)), False)
            step(v.tensor_scalar(first[:], number, float(BLOCK), None, ALU.mult))
            for e in range(E):
                step(v.tensor_scalar(over[:], number, cum[:, e:e + 1], None, ALU.is_ge))
                step(v.tensor_tensor(expert[:], expert[:], over[:], ALU.subtract), False)
                step(v.scalar_tensor_tensor(first[:], over[:], delta[:, e:e + 1], first[:], ALU.mult, ALU.add))
            step(v.tensor_scalar(expert[:], expert[:], 1.0, None, ALU.max), False)
            step(v.tensor_scalar(first[:], first[:], float(E * REGION), None, ALU.min))
            step(v.tensor_copy(ffn["first_i"][:], first[:]))
            padded, turn = ffn["padded"], ffn["turn"]
            step(v.memset(padded[:], 0.0), False)
            step(v.memset(turn[:], 0.0))
            step(v.tensor_scalar(padded[:].rearrange("p t b -> p (t b)")[:, 4:4 + BLOCKS], expert[:], -1.0, float(E), ALU.mult, ALU.add))
            for n in range(6):
                at = 1 + n
                step(v.scalar_tensor_tensor(turn[:], padded[:, at // 4:at // 4 + TURNS + 1, at % 4], float(E ** n), turn[:], ALU.mult, ALU.add))
            step(v.tensor_copy(ffn["turn_i"][:], turn[:]))
            step(v.memset(ffn["nobody"][:], 0.0))
            step(v.memset(ffn["nobody"][:, :, C + 3:C + 4], NO_SLOT))


META_STEPS = 4


def in_turns(eng, *stages, start=None):
    def turn(m, exists):
        if start:
            start(m)
        for p in range(4):
            for lag, f in stages:
                if exists(4 * m + p - lag):
                    f(4 * m + p - lag, (p - lag) % 4)
    for m in range(2):
        turn(m, lambda k: k >= 0)
    with eng.Fori(2, TURNS) as m:
        turn(m, lambda k: True)
    turn(TURNS, lambda k: k < BLOCKS)


def experts(nc, ident, ffn, rows_dram, res_dram):
    w1_hl, b1_hl, w2_hl, b2_hl = ffn["w1_hl"], ffn["b1_hl"], ffn["w2_hl"], ffn["b2_hl"]
    with ExitStack() as ctx:
        def sb(name, shape, dt=F32):
            return ctx.enter_context(nc.sbuf_tensor(name, shape, dt))

        ident16 = sb("e_ident16", [P, P], F16)
        ones16 = sb("e_ones16", [P, BLOCK], F16)
        xg = sb("e_xg", [P, 4, 2, ROW])
        xt = sb("e_xt", [P, 2, 2, BLOCK], F16)
        sig = sb("e_sig", [P, 2, 2 * BLOCK])
        gs = sb("e_gs", [P, 2, 2 * BLOCK])
        hid = sb("e_hid", [P, 2, 2 * BLOCK])
        hid_hl = sb("e_hid_hl", [P, 2, 2, 2, BLOCK], F16)
        first_choice = sb("e_first", [P, 2, 2])
        wt = sb("e_wt", [P, 4, 2])
        dest = sb("e_dest", [P, 4, 2], I32)
        y = sb("e_y", [P, 4, 2, C])
        one, held = sb("e_one", [1, 1]), sb("e_held", [1, 1])
        ps = ctx.enter_context(nc.psum_tensor("e_ps", [P, 8, 2 * BLOCK], F32))
        s = Named({n: ctx.enter_context(nc.semaphore("e_" + n)) for n in """
            set_v set_g held nobody_in x0_in x1_in x2_in x3_in xT xt_done g_psum u_psum sig_done gs_done hid_done hh_done
            hl_done y_psum y_done meta r0_out r1_out r2_out r3_out""".split()})
        x_in = [s.x0_in, s.x1_in, s.x2_in, s.x3_in]
        r_out = [s.r0_out, s.r1_out, s.r2_out, s.r3_out]

        block = ctx.enter_context(nc.Block())

        @block.sync
        def _(sp):
            nobody = ffn["nobody"]
            fill = lambda row: rows_dram[row].rearrange("(n p) w -> p n w", p=P)
            sp.dma_start(rows_dram[E * REGION:E * REGION + BLOCK].rearrange("(n p) w -> p n w", p=P), nobody[:]).then_inc(s.nobody_in, 16)
            for e in range(E):
                row = sp.value_load(ffn["tail_i"][0:1, e:e + 1], min_val=e * REGION, max_val=(e + 1) * REGION - BLOCK)
                sp.dma_start(rows_dram[bass.ds(row, BLOCK)].rearrange("(n p) w -> p n w", p=P), nobody[:]).then_inc(s.nobody_in, 16)
            sp.wait_ge(s.nobody_in, 16 * (E + 1))

            def load(m):
                for i in range(4):
                    row = sp.value_load(ffn["first_i"][0:1, bass.ds(4 * m + i, 1)], min_val=0, max_val=E * REGION)
                    need(sp, s.meta, META_STEPS * (4 * m + i - 3))
                    sp.dma_start(xg[:, i], rows_dram[bass.ds(row, BLOCK)].rearrange("(n p) w -> p n w", p=P)).then_inc(x_in[i], 16)
            load(0)
            with sp.Fori(1, TURNS) as m:
                load(m)

        @block.gpsimd
        def _(pool):
            nc.gpsimd.memset(one[:], 0.0).then_inc(s.set_g, 1)
            pool.wait_ge(s.set_g, 1)

            def send(m):
                for i in range(4):
                    need(pool, s.held, 4 * m + i)
                    pool.wait_ge(s.y_done, 4 * m + i + 1)
                    nc.gpsimd.tensor_tensor(held[:], one[:], one[:], ALU.mult).then_inc(s.held, 1)
                    for n in range(2):
                        nc.gpsimd.indirect_dma_start(res_dram, bass.IndirectOffsetOnAxis(ap=dest[:, i, n:n + 1], axis=0),
                                                     y[:, i, n, :], None, bounds_check=2 * B * TOK - 1, oob_is_err=False).then_inc(r_out[i], 16)
            send(0)
            with pool.Fori(1, TURNS) as m:
                send(m)
            for r in r_out:
                pool.wait_ge(r, 16 * 2 * TURNS)

        @block.tensor
        def _(pe):
            t = nc.tensor
            pe.wait_ge(s.set_v, 2)

            now = []

            def look_up(m):
                word = pe.value_load(ffn["turn_i"][0:1, bass.ds(m, 1)], min_val=0, max_val=E ** 6 - 1)
                now[:] = [(word // E ** n) % E for n in range(6)]

            def xT(k, i):
                pe.wait_ge(x_in[i], 4 * (k - i) + 16)
                need(pe, s.xt_done, k - 1)
                dst = ps[:, i % 2, 0:BLOCK].bitcast(F16).rearrange("p (l n c) -> p l n c", l=2, n=2)
                src = xg[:, i].bitcast(F16)
                for l in range(2):
                    for n in range(2):
                        last = t.transpose(dst[:, l, n], src[:, n, l * C:(l + 1) * C], ident16[:])
                last.then_inc(s.xT, 1)

            def inner(k, i):
                e = now[2 + (i + 1) % 4]
                need(pe, s.xt_done, k + 1)
                x2 = [xt[:, i % 2, l, :] for l in range(2)]
                for bank, part, free, psum in ((2, 0, s.gs_done, s.g_psum), (4, 2, s.hid_done, s.u_psum)):
                    need(pe, free, k - 1)
                    for n in range(2):
                        at = (part + n) * P
                        o = ps[:, bank + i % 2, n * BLOCK:(n + 1) * BLOCK]
                        hi, lo = (w1_hl[:, bass.ds(e, 1), l, at:at + P].rearrange("p o c -> p (o c)") for l in range(2))
                        t.matmul(o, b1_hl[:, bass.ds(e, 1), at:at + P].rearrange("p o c -> p (o c)"), ones16[:], start=True, stop=False)
                        t.matmul(o, hi, x2[0], start=False, stop=False)
                        t.matmul(o, hi, x2[1], start=False, stop=False)
                        last = t.matmul(o, lo, x2[0], start=False, stop=True)
                    last.then_inc(psum, 1)

            def outer(k, i):
                e = now[(i + 3) % 4]
                need(pe, s.hl_done, k + 1)
                need(pe, s.y_done, k - 1)
                for n in range(2):
                    o = ps[:, 6 + i % 2, n * C:(n + 1) * C]
                    t.matmul(o, ones16[:, 0:P], b2_hl[:, bass.ds(e, 1), :].rearrange("p o c -> p (o c)"), start=True, stop=False)
                    for q in range(2):
                        hi, lo = (hid_hl[:, i % 2, l, q, n * P:(n + 1) * P] for l in range(2))
                        whi, wlo = (w2_hl[:, bass.ds(e, 1), l, q, :].rearrange("p o c -> p (o c)") for l in range(2))
                        t.matmul(o, hi, whi, start=False, stop=False)
                        t.matmul(o, hi, wlo, start=False, stop=False)
                        last = t.matmul(o, lo, whi, start=False, stop=q == 1)
                last.then_inc(s.y_psum, 1)

            in_turns(pe, (0, xT), (1, inner), (3, outer), start=look_up)

        @block.scalar
        def _(act):
            a = nc.scalar

            def x(k, i):
                need(act, s.xT, k + 1)
                need(act, s.u_psum, k - 1)
                a.activation(xt[:, i % 2].rearrange("p l c -> p (l c)"), ps[:, i % 2, 0:BLOCK].bitcast(F16), ACT.Copy).then_inc(s.xt_done, 1)

            def sigmoid(k, i):
                need(act, s.g_psum, k + 1)
                need(act, s.gs_done, k - 1)
                a.activation(sig[:, i % 2], ps[:, 2 + i % 2], ACT.Sigmoid, scale=1.702 / WS).then_inc(s.sig_done, 1)

            def high(k, i):
                need(act, s.hid_done, k + 1)
                need(act, s.y_psum, k - 1)
                need(act, s.hl_done, k - 1)
                a.activation(hid_hl[:, i % 2, 0].rearrange("p q c -> p (q c)"), hid[:, i % 2], ACT.Copy).then_inc(s.hh_done, 1)

            def result(k, i):
                need(act, s.y_psum, k + 1)
                need(act, s.meta, META_STEPS * (k + 1))
                need(act, r_out[i], 8 * (k - i))
                for n in range(2):
                    ins = a.activation(y[:, i, n, :], ps[:, 6 + i % 2, n * C:(n + 1) * C], ACT.Copy, scale=wt[:, i, n:n + 1])
                ins.then_inc(s.y_done, 1)
            in_turns(act, (0, x), (2, high), (1, sigmoid), (4, result))

        @block.vector
        def _(dve):
            v = nc.vector
            step = chain(dve, s.set_v, 0)
            step(v.tensor_copy(ident16[:], ident))
            step(v.memset(ones16[:], 1.0))

            def meta(k, i):
                need(dve, x_in[i], 4 * (k - i) + 16)
                need(dve, s.xT, k + 1)
                need(dve, s.y_done, k - 3)
                need(dve, r_out[i], 8 * (k - i))
                step = chain(dve, s.meta, META_STEPS * k)
                word = lambda n: xg[:, i, :, C + n]
                one = first_choice[:, i % 2]
                step(v.tensor_scalar(one, word(2), ffn["expert"][:, bass.ds(k, 1)], None, ALU.is_equal))
                step(v.tensor_tensor(wt[:, i], one, word(1), ALU.mult), False)
                step(v.tensor_tensor(dest[:, i], word(3), one, ALU.subtract))
                step(v.tensor_tensor(wt[:, i], wt[:, i], word(0), ALU.add), False)

            def gated(k, i):
                need(dve, s.sig_done, k + 1)
                need(dve, s.hid_done, k - 1)
                v.scalar_tensor_tensor(gs[:, i % 2], ps[:, 2 + i % 2], 1.0 / (WS * WS), sig[:, i % 2], ALU.mult, ALU.mult).then_inc(s.gs_done, 1)
                need(dve, s.gs_done, k + 1)
                need(dve, s.u_psum, k + 1)
                need(dve, s.hl_done, k - 1)
                need(dve, s.hh_done, k - 1)
                v.scalar_tensor_tensor(hid[:, i % 2], ps[:, 4 + i % 2], WS, gs[:, i % 2], ALU.add, ALU.mult).then_inc(s.hid_done, 1)

            def low(k, i):
                need(dve, s.hh_done, k + 1)
                need(dve, s.y_psum, k - 1)
                v.tensor_tensor(hid_hl[:, i % 2, 1].rearrange("p q c -> p (q c)"), hid[:, i % 2],
                                hid_hl[:, i % 2, 0].rearrange("p q c -> p (q c)"), ALU.subtract).then_inc(s.hl_done, 1)
            in_turns(dve, (2, meta), (2, low), (1, gated))


def combine(nc, resid, res_dram, out):
    out_tok = out.rearrange("b a (tl j) c -> b (a tl) (j c)", j=TILES)
    res_tok = res_dram.rearrange("(b p j n) c -> b p (j n c)", p=P, j=TILES, n=2)
    with ExitStack() as ctx:
        yb = ctx.enter_context(nc.sbuf_tensor("c_y", [P, 4, 2 * TOK], F32))
        s = Named({n: ctx.enter_context(nc.semaphore("c_" + n)) for n in
                               "y0_in y1_in y2_in y3_in one_done both_done out_done".split()})
        y_in = [s.y0_in, s.y1_in, s.y2_in, s.y3_in]
        block = ctx.enter_context(nc.Block())

        @block.sync
        def _(sp):
            def load(m):
                for i in range(4):
                    need(sp, s.both_done, 4 * m + i - 3)
                    sp.dma_start(yb[:, i, :], res_tok[4 * m + i]).then_inc(y_in[i], 16)
            load(0)
            with sp.Fori(1, B // 4) as m:
                load(m)

        @block.vector
        def _(dve):
            with dve.Fori(0, B // 4) as m:
                for i in range(4):
                    b = 4 * m + i
                    y4 = yb[:, i, :].rearrange("p (j n c) -> p j n c", j=TILES, n=2)
                    r = resid[:, b, :].rearrange("p (j c) -> p j c", j=TILES)
                    dve.wait_ge(y_in[i], 16 * m + 16)
                    nc.vector.tensor_tensor(r, r, y4[:, :, 0, :], ALU.add).then_inc(s.one_done, 1)
                    dve.wait_ge(s.one_done, b + 1)
                    nc.vector.tensor_tensor(r, r, y4[:, :, 1, :], ALU.add).then_inc(s.both_done, 1)

        @block.scalar
        def _(act):
            with act.Fori(0, B) as b:
                act.wait_ge(s.both_done, b + 1)
                act.dma_start(out_tok[b], resid[:, b, :]).then_inc(s.out_done, 16)
            act.wait_ge(s.out_done, 16 * B)


def build(nc, t):
    rows_dram = nc.dram_tensor("rows", (E * REGION + BLOCK, ROW), F32, kind="Internal").ap()
    res_dram = nc.dram_tensor("results", (2 * B * TOK, C), F32, kind="Internal").ap()
    with ExitStack() as ctx:
        def sb(name, shape, dt=F32):
            return ctx.enter_context(nc.sbuf_tensor(name, shape, dt))

        early = sb("early", [P, EARLY.shape[1]])
        resid = sb("resid", [P, B, TOK])
        ones16 = sb("ones16", [P, P], F16)
        agent_attention(nc, early, resid, ones16, t["x"], t["L0_conv_coalition"], t["L0_conv_masks"], t["L0_conv_emb_W"],
                        *(t["L0_conv_" + n] for n in "Wq bq Wk bk Wv bv Wo bo".split()), t["early"])
        late = sb("late", [P, LATE.shape[1]])
        ffn = {
            "w1_hl": sb("w1_hl", [P, E, 2, 2 * I], F16), "b1_hl": sb("b1_hl", [P, E, 2 * I], F16),
            "w2_hl": sb("w2_hl", [P, E, 2, 2, C], F16), "b2_hl": sb("b2_hl", [P, E, C], F16),
            "cnt": sb("cnt", [P, E]), "cnti": sb("cnti", [P, E], I32), "nb": sb("nb", [P, E]),
            "delta": sb("delta", [P, E]), "cum": sb("cum", [P, E]), "tail_i": sb("tail_i", [P, E], I32),
            "expert": sb("expert", [P, BLOCKS]), "first": sb("first", [P, BLOCKS]), "over": sb("over", [P, BLOCKS]),
            "padded": sb("padded", [P, TURNS + 2, 4]), "turn": sb("turn", [P, TURNS + 1]), "turn_i": sb("turn_i", [P, TURNS + 1], I32), "first_i": sb("first_i", [P, BLOCKS], I32),
            "nobody": sb("nobody", [P, 2, ROW]),
        }
        ident = const(early, "ident")
        token_mixer(nc, late, resid, ones16, ident, t["late"], ffn, rows_dram, *(t["L1_attn_" + n] for n in "Wq bq Wk bk Wv bv".split()),
                    *(t["L1_ffn_" + n] for n in "router_w router_b gate_up_proj gate_up_proj_bias down_proj down_proj_bias".split()))
        experts(nc, ident, ffn, rows_dram, res_dram)
        combine(nc, resid, res_dram, t["out"])


_INS = """x L0_conv_coalition L0_conv_masks L0_conv_emb_W L0_conv_Wq L0_conv_bq L0_conv_Wk L0_conv_bk L0_conv_Wv L0_conv_bv
    L0_conv_Wo L0_conv_bo L1_attn_Wq L1_attn_bq L1_attn_Wk L1_attn_bk L1_attn_Wv L1_attn_bv L1_ffn_router_w L1_ffn_router_b
    L1_ffn_gate_up_proj L1_ffn_gate_up_proj_bias L1_ffn_down_proj L1_ffn_down_proj_bias""".split()


def kernel(**inputs):
    import concourse.bacc as bacc
    from concourse.bass_utils import run_bass_kernel_spmd

    nc = bacc.Bacc("TRN2", target_bir_lowering=False, num_devices=1)
    arrays, tensors = {}, {}
    for name, a in [(n, inputs[n]) for n in _INS] + [("early", EARLY), ("late", LATE)]:
        a = np.ascontiguousarray(a)
        arrays[f"in_{name}"] = a
        tensors[name] = nc.dram_tensor(f"in_{name}", a.shape, mybir.dt.from_np(a.dtype), kind="ExternalInput").ap()
    tensors["out"] = nc.dram_tensor("out_0", (B, A, T, C), F32, kind="ExternalOutput").ap()
    build(nc, tensors)
    return run_bass_kernel_spmd(nc, [arrays], core_ids=[0]).results[0]["out_0"]
```

```python
from contextlib import ExitStack

import numpy as np

import concourse.bass as bass
from concourse import mybir

F32, F16, BF16, I32 = mybir.dt.float32, mybir.dt.float16, mybir.dt.bfloat16, mybir.dt.int32
ALU = mybir.AluOpType
ACT = mybir.ActivationFunctionType
AX = mybir.AxisListType

P = 128
B, A, T, C = 32, 16, 32, 128
H, HD = 8, 16
S = 5
TILES = A * T // P
TOK = A * T
PAIRS = B // 2
GROUP = 4
WS = 64.0
GN_EPS, LN_EPS, ATT_EPS = 1e-5, 1e-5, 1e-6
ON_DVE = 7
TABLE_STEP = 18
E, I = 8, 256
BLOCK = 256
REGION = B * TOK + BLOCK
BLOCKS = 2 * B * TOK // BLOCK + E
TURN = 8
TURNS = BLOCKS // TURN
NOW = TURN + 2
ROW = C + 4
LN_STEPS, ROUTE_STEPS, PLACE_STEPS = 7, 22, 15
NO_SLOT = 1e6
HALF = 64

CONST = {}


def _constants():
    parts, at = {0: [], 1: []}, [0, 0]

    def put(late, name, a):
        full = np.zeros((P, a.shape[1]), np.float32)
        full[: a.shape[0]] = a
        CONST[name] = (at[late], a.shape[1])
        at[late] += a.shape[1]
        parts[late].append(full)

    r = np.arange(P)
    put(0, "ident", np.eye(P))
    put(0, "block8", r[:, None] // HD == np.arange(H)[None, :])
    put(0, "group", (r[:, None] // 4 == r[None, :] // 4) / 8.0)
    put(0, "eye_qk", np.tile(np.eye(A), (S, 1)))
    put(1, "block_kv", (r[:, None] // HD == r[None, :] // HD) / float(TOK))
    put(1, "block_ks", (r[:, None] // HD == np.arange(H)[None, :]) / float(TOK))
    put(1, "before", (r[:, None] < r[None, :]) * 1.0)
    put(1, "rank_of", np.tile(float(E) - np.arange(E), (P, 8)))
    put(1, "region", np.tile(np.arange(E) * float(REGION), (P, 8)))
    put(1, "block_no", np.tile(np.arange(BLOCKS) * 1.0, (P, 1)))
    tok = np.arange(B)[None, :, None] * TOK + r[:, None, None] * TILES + np.arange(TILES)[None, None, :]
    put(1, "slot1", (2.0 * tok + 1).reshape(P, -1))
    return np.concatenate(parts[0], 1), np.concatenate(parts[1], 1)


EARLY, LATE = _constants()


class Named(dict):

    def __getattr__(self, name):
        return self[name]


def const(cst, name):
    at, n = CONST[name]
    return cst[:, at:at + n]


def need(eng, sem, count):
    if isinstance(count, int) and count <= 0:
        return
    eng.wait_ge(sem, count)


def most(count, top):
    return min(count, top) if isinstance(count, int) else count


def pipelined(eng, steps, depth, unroll, work):
    def body(m, n):
        for together in work:
            running = []
            for stage, f, *args in together if isinstance(together, list) else [together]:
                if not isinstance(m, int) or 0 <= m - stage < steps:
                    running.append(f(m - stage, (n - stage) % unroll, *args) or iter(()))
            while running:
                for one in running[:2]:
                    if next(one, "end") == "end":
                        running.remove(one)

    for m in range(depth):
        body(m, m)
    with eng.Fori(0, (steps - depth) // unroll) as turn:
        for n in range(depth, depth + unroll):
            body(unroll * turn + n, n)
    for m in range(steps, steps + depth - 1):
        body(m, m)


def agent_attention(nc, cst, resid, ones16, x, coalition, masks, emb_W, Wq, bq, Wk, bk, Wv, bv, Wo, bo, consts):
    with ExitStack() as ctx:
        def sb(name, shape, dt=F32):
            return ctx.enter_context(nc.sbuf_tensor(name, shape, dt))

        def sem(name):
            return ctx.enter_context(nc.semaphore(name))

        x_tok = x.rearrange("b a (tl j) c -> b (a tl) (j c)", j=TILES)

        arena = sb("arena", [P, 2 * 2 * 2 * TOK * H], F16)
        carved = [0]

        def carve(shape, dt=F32):
            n = int(np.prod(shape[1:])) * 2
            at = carved[0]
            carved[0] += n
            ap = arena[0:shape[0], at:at + n].bitcast(dt)
            if len(shape) == 3:
                ap = ap.rearrange("p (m n) -> p m n", m=shape[1])
            return ap

        ident, group, block8 = const(cst, "ident"), const(cst, "group"), const(cst, "block8")
        wstage = carve([P, 4, C])
        w_f = carve([P, 4, C])
        w_hl = sb("w_hl", [P, 2, 4, C], F16)
        bias0 = sb("bias0", [P, 4])
        bo_row = sb("bo_row", [1, C])
        brow = sb("brow", [1, C])
        bo_hl = sb("bo_hl", [64, TOK], F16)
        emb16 = sb("emb16", [A, C])
        embT = sb("embT", [P, A])
        coal = sb("coal", [A, 1], I32)
        shift = sb("shift", [P, B, A])
        gst6 = carve([P, B, 6])
        gsum = carve([P, 2, B])
        gmean = carve([P, 2, B])
        gtmp = carve([P, 2, B])
        half = carve([P, B])
        rstd = sb("rstd", [P, B])
        nmr = carve([P, B])
        mraw = carve([S * A, A], I32)
        mflt = carve([S * A, A])
        mrep = carve([S * A, H, A])
        mkq = carve([P, S, A])
        msum = sb("msum", [P, A, HALF])
        mspread = sb("mspread", [P, A // 2, P], BF16)
        bd = arena[:].rearrange("p (n u l g h q) -> p n u l g h q", n=2, u=2, l=2, h=H, q=A)
        bdq, bdp = bd[:, 0], bd[:, 1]
        xb = sb("xb", [P, 2, TOK])
        xi = sb("xi", [P, 2, TOK])
        xhl = sb("xhl", [P, 2, 2, TOK], F16)
        t32 = sb("t32", [P, 4, TOK])
        qhl = sb("qhl", [P, 2, 2, TOK], F16)
        khl = sb("khl", [P, 2, 2, TOK], F16)
        vhl = sb("vhl", [P, 6, 2, TOK], F16)
        sm = sb("sm", [P, 2, TOK])
        rmax = sb("rmax", [P, 2, T])
        pt = sb("pt", [P, 2, TOK])
        phl = sb("phl", [P, 2, 2, TOK], F16)
        recip = sb("recip", [P, A // 2, 2 * TILES * H])
        rparts = sb("rparts", [P, 3, A // 2, 2 * TILES * H], BF16)
        o32 = sb("o32", [P, 2, TOK])
        othl = sb("othl", [P, 2, 2, TOK], F16)

        ps = ctx.enter_context(nc.psum_tensor("ps", [P, 8, TOK], F32))
        bank_xy, bank_q, bank_k, bank_vo, bank_s, bank_t, bank_d = (ps[:, n, :] for n in range(7))

        s = Named({n: sem(n) for n in """
            consts_in weights_in masks_in coal_in emb_in r0_in r1_in r2_in r3_in r4_in r5_in r6_in r7_in x0_in x1_in
            setup_v spread_done half_set setup_pe gT_psum gst_done gvar_done gsum_done gmean_psum rstd_done
            xT_psum xi_done xh_done xl_done q_psum k_psum v_psum q32_done qh_done ql_done k32_done kh_done
            kl_done v32_done vh_done vl_done bdq_done s_psum rmax_done sm_done e_done et_psum et_done d_psum
            recip_done rh_done rest_done rm_done rl_done bdq_rest_done bdp_rest_done w_psum p_done ph_done pl_done
            bdp_done o_psum o32_done ot_psum ot32_done oth_done
            otl_done y_psum x1_done out_done""".split()})
        x_in = [s.x0_in, s.x1_in]
        r_in = [s.r0_in, s.r1_in, s.r2_in, s.r3_in, s.r4_in, s.r5_in, s.r6_in, s.r7_in]

        block = ctx.enter_context(nc.Block())

        @block.sync
        def _(sp):
            sp.dma_start(cst[:], consts).then_inc(s.consts_in, 16)
            sp.dma_start(coal[:], coalition.rearrange("(a o) -> a o", o=1)).then_inc(s.coal_in, 16)
            sp.dma_start(mraw[:], masks.rearrange("s q k -> (s q) k")).then_inc(s.masks_in, 16)
            for n, w in enumerate((Wq, Wk, Wv, Wo)):
                sp.dma_start(wstage[:, n, :], w).then_inc(s.weights_in, 16)
            for n, v in enumerate((bq, bk, bv)):
                sp.dma_start(bias0[:, n:n + 1], v.rearrange("(c o) -> c o", o=1)).then_inc(s.weights_in, 16)
            sp.dma_start(bo_row[:], bo.rearrange("(o c) -> o c", o=1)).then_inc(s.weights_in, 16)

            for g, loaded in enumerate(r_in):
                part = slice(GROUP * g, GROUP * (g + 1))
                sp.dma_start(resid[:, part, :], x_tok[part].rearrange("b p c -> p b c")).then_inc(loaded, 16)

            def second_pass(m):
                for u in range(2):
                    need(sp, s.xT_psum, 2 * m + u - 1)
                    sp.dma_start(xb[:, u, :], x_tok[2 * m + u]).then_inc(x_in[u], 16)
            second_pass(0)
            with sp.Fori(1, PAIRS) as m:
                second_pass(m)

        @block.gpsimd
        def _(pool):
            g = nc.gpsimd
            g.memset(half[:], -0.5).then_inc(s.half_set, 1)
            pool.wait_ge(s.coal_in, 16)
            g.indirect_dma_start(emb16[:], None, emb_W, bass.IndirectOffsetOnAxis(ap=coal[:], axis=0)).then_inc(s.emb_in, 16)
            pool.wait_ge(s.half_set, 1)
            pool.wait_ge(s.gvar_done, 1)
            g.tensor_tensor(rstd[:], gtmp[:, 1, :], half[:], ALU.pow).then_inc(s.rstd_done, 1)

            def low(dst, full, high, full_done, high_done, done, n, free, freed):
                need(pool, full_done, n + 1)
                need(pool, high_done, n + 1)
                need(pool, free, freed)
                g.tensor_tensor(dst, full, high, ALU.subtract).then_inc(done, 1)

            def recip_rest(k, ring):
                need(pool, s.rh_done, k + 1)
                g.tensor_tensor(recip[:], recip[:], rparts[:, 0], ALU.subtract).then_inc(s.rest_done, 1)

            def recip_low(k, ring):
                need(pool, s.rm_done, k + 1)
                g.tensor_tensor(rparts[:, 2], recip[:], rparts[:, 1], ALU.subtract).then_inc(s.rl_done, 1)

            def xl(k, ring, u):
                b = 2 * k + u
                low(xhl[:, u, 1, :], xi[:, u, :], xhl[:, u, 0, :], s.xi_done, s.xh_done, s.xl_done, b, s.v_psum, b - 1)

            def pl(k, ring, u):
                d = 2 * k + u
                need(pool, s.bdp_rest_done, d - 1)
                low(phl[:, u, 1, :], pt[:, u, :], phl[:, u, 0, :], s.p_done, s.ph_done, s.pl_done, d, s.bdp_done, d - 1)

            def ql_kl(k, ring, u):
                b = 2 * k + u
                need(pool, s.bdq_rest_done, b - 1)
                low(qhl[:, u, 1, :], t32[:, 0, :], qhl[:, u, 0, :], s.q32_done, s.qh_done, s.ql_done, b, s.bdq_done, b - 1)
                low(khl[:, u, 1, :], t32[:, 1, :], khl[:, u, 0, :], s.k32_done, s.kh_done, s.kl_done, b, s.s_psum, b - 1)

            def vl(k, ring, u):
                b, slot = 2 * k + u, 2 * ring + u
                low(vhl[:, slot, 1, :], t32[:, 2, :], vhl[:, slot, 0, :], s.v32_done, s.vh_done, s.vl_done, b, s.o_psum, b - 5)

            def otl(k, ring, u):
                e = 2 * k + u
                low(othl[:, u, 1, :], t32[:, 3, :], othl[:, u, 0, :], s.ot32_done, s.oth_done, s.otl_done, e, s.y_psum, e - 1)

            pipelined(pool, PAIRS, 4, 3, [
                (0, xl, 0), (2, pl, 0), (0, xl, 1), (2, pl, 1), (0, ql_kl, 0), (3, otl, 0), (3, otl, 1), (0, vl, 0),
                (0, ql_kl, 1), (1, recip_rest), (1, recip_low), (0, vl, 1),
            ])

        @block.scalar
        def _(act):
            a = nc.scalar

            def xh(k, ring, u):
                b = 2 * k + u
                need(act, s.xi_done, b + 1)
                need(act, s.v_psum, b - 1)
                need(act, s.xl_done, b - 1)
                a.activation(xhl[:, u, 0, :], xi[:, u, :], ACT.Copy).then_inc(s.xh_done, 1)

            def spread_rest(dst, src, done):
                for n in range(ON_DVE, H):
                    ins = a.activation(dst[:, :, :, n, :], src.rearrange("p l (g q) -> p l g q", q=A), ACT.Copy, scale=block8[:, n:n + 1])
                ins.then_inc(done, 1)

            def spread_q(k, ring, u):
                need(act, s.qh_done, 2 * k + u + 1)
                need(act, s.ql_done, 2 * k + u + 1)
                need(act, s.s_psum, 2 * k + u - 1)
                spread_rest(bdq[:, u], qhl[:, u], s.bdq_rest_done)

            def spread_p(k, ring, u):
                need(act, s.ph_done, 2 * k + u + 1)
                need(act, s.pl_done, 2 * k + u + 1)
                need(act, s.o_psum, 2 * k + u - 1)
                spread_rest(bdp[:, u], phl[:, u], s.bdp_rest_done)

            def recip_high(k, ring):
                need(act, s.recip_done, k + 1)
                a.activation(rparts[:, 0], recip[:], ACT.Copy).then_inc(s.rh_done, 1)

            def recip_middle(k, ring):
                need(act, s.rest_done, k + 1)
                a.activation(rparts[:, 1], recip[:], ACT.Copy).then_inc(s.rm_done, 1)

            def exp(k, ring, u):
                c = 2 * k + u
                need(act, s.sm_done, c + 1)
                a.activation(sm[:, u, :], sm[:, u, :], ACT.Exp, scale=HD ** -0.5).then_inc(s.e_done, 1)

            def ph(k, ring, u):
                d = 2 * k + u
                need(act, s.p_done, d + 1)
                need(act, s.bdp_done, d - 1)
                need(act, s.pl_done, d - 1)
                need(act, s.bdp_rest_done, d - 1)
                a.activation(phl[:, u, 0, :], pt[:, u, :], ACT.Copy).then_inc(s.ph_done, 1)

            def o(k, ring, u):
                e = 2 * k + u
                need(act, s.o_psum, e + 1)
                need(act, s.ot_psum, e - 1)
                a.activation(o32[:, u, :], bank_vo, ACT.Copy, scale=1.0 / S).then_inc(s.o32_done, 1)

            def et(k, ring, u):
                c = 2 * k + u
                need(act, s.et_psum, c + 1)
                need(act, s.ph_done, c - 1)
                need(act, s.pl_done, c - 1)
                a.activation(pt[:, u, :], bank_t, ACT.Copy).then_inc(s.et_done, 1)

            def project(bank, n, bias, psum, low_done, full_done, dst, high_done, b, free, freed):
                need(act, psum, b + 1)
                need(act, low_done, b)
                need(act, free, freed)
                if bias is None:
                    a.activation(t32[:, n, :], bank, ACT.Copy, scale=1.0 / WS).then_inc(full_done, 1)
                    a.activation(dst, bank, ACT.Copy, scale=1.0 / WS).then_inc(high_done, 1)
                else:
                    a.activation(t32[:, n, :], bank, ACT.Identity, bias=bias, scale=1.0 / WS).then_inc(full_done, 1)
                    a.activation(dst, bank, ACT.Identity, bias=bias, scale=1.0 / WS).then_inc(high_done, 1)

            def q_k(k, ring, u):
                b = 2 * k + u
                need(act, s.bdq_rest_done, b - 1)
                project(bank_q, 0, bias0[:, 0:1], s.q_psum, s.ql_done, s.q32_done, qhl[:, u, 0, :], s.qh_done, b,
                        s.bdq_done, b - 1)
                project(bank_k, 1, bias0[:, 1:2], s.k_psum, s.kl_done, s.k32_done, khl[:, u, 0, :], s.kh_done, b,
                        s.s_psum, b - 1)

            def v(k, ring, u):
                b, slot = 2 * k + u, 2 * ring + u
                project(bank_vo, 2, None, s.v_psum, s.vl_done, s.v32_done, vhl[:, slot, 0, :], s.vh_done, b,
                        s.o_psum, b - 5)

            def ot(k, ring, u):
                e = 2 * k + u
                need(act, s.ot_psum, e + 1)
                need(act, s.otl_done, e)
                need(act, s.y_psum, e - 1)
                src = bank_t.rearrange("p (t j q) -> p j q t", j=TILES, q=A)
                a.activation(t32[:, 3, :].rearrange("p (j q t) -> p j q t", j=TILES, q=A), src, ACT.Copy).then_inc(s.ot32_done, 1)
                a.activation(othl[:, u, 0, :].rearrange("p (j q t) -> p j q t", j=TILES, q=A), src, ACT.Copy).then_inc(s.oth_done, 1)

            act.wait_ge(s.weights_in, 16 * 8)

            pipelined(act, PAIRS, 4, 3, [
                (1, exp, 0), (3, o, 0), (0, xh, 0), (2, ph, 0), (0, xh, 1), (2, ph, 1), (1, et, 0), (1, exp, 1),
                (0, q_k, 0), (1, et, 1), (2, spread_p, 0), (3, o, 1), (3, ot, 0), (0, spread_q, 0), (3, ot, 1),
                (0, v, 0), (0, q_k, 1), (0, v, 1), (1, recip_high), (1, recip_middle), (0, spread_q, 1),
                (2, spread_p, 1),
            ])

        @block.tensor
        def _(pe):
            t = nc.tensor

            def first(g):
                pe.wait_ge(r_in[g], 16)
                for b in range(GROUP * g, GROUP * (g + 1)):
                    need(pe, s.gst_done, b - 3)
                    for j in range(TILES):
                        last = t.transpose(ps[:, b % 4, j * P:(j + 1) * P], resid[:, b, j * P:(j + 1) * P], ident)
                    last.then_inc(s.gT_psum, 1)
            pe.wait_ge(s.consts_in, 16)
            first(0)
            pe.wait_ge(s.setup_v, 4)
            t.matmul(ps[:, 4, 0:S * A], mrep[:], ident[0:S * A, 0:S * A], start=True, stop=True).then_inc(s.setup_pe, 1)
            pe.wait_ge(s.emb_in, 16)
            t.transpose(ps[:, 5, 0:A], emb16[:], ident[0:A, 0:A]).then_inc(s.setup_pe, 1)
            pe.wait_ge(s.weights_in, 16 * 8)
            t.matmul(ps[0:1, 6, 0:C], bias0[:, 2:3], wstage[:, 3, :], start=True, stop=True).then_inc(s.setup_pe, 1)
            for g in range(1, B // GROUP):
                first(g)
            pe.wait_ge(s.setup_v, TABLE_STEP)
            pe.wait_ge(s.gst_done, B)
            for q in range(A):
                last = t.transpose(ps[0:HALF, q // 4, (q % 4) * P:(q % 4 + 1) * P], msum[:, q, :], ident)
            last.then_inc(s.setup_pe, 1)
            pe.wait_ge(s.gsum_done, 1)
            t.matmul(ps[:, 7, 0:2 * B], group, gsum[:].rearrange("p n b -> p (n b)"), start=True, stop=True).then_inc(s.gmean_psum, 1)
            pe.wait_ge(s.spread_done, 1)

            def xT(k, ring, u):
                b = 2 * k + u
                need(pe, x_in[u], 16 * k + 16)
                need(pe, s.xi_done, b)
                need(pe, s.x1_done, b - 6 - u)
                for j in range(TILES):
                    last = t.transpose(bank_xy.rearrange("p (n j) -> p j n", j=TILES)[:, j, :], xb[:, u, j * P:(j + 1) * P], ident)
                last.then_inc(s.xT_psum, 1)

            def products(out, lhs, rhs, start=True, stop=True):
                t.matmul(out, lhs[0], rhs[0], start=start, stop=False)
                t.matmul(out, lhs[0], rhs[1], start=False, stop=False)
                return t.matmul(out, lhs[1], rhs[0], start=False, stop=stop)

            def qk(k, ring, u):
                c = 2 * k + u
                need(pe, s.bdq_done, c + 1)
                need(pe, s.bdq_rest_done, c + 1)
                need(pe, s.kl_done, c + 1)
                need(pe, s.sm_done, c)
                for n in range(T):
                    last = products(bank_s[:, n * A:(n + 1) * A], [bdq[:, u, l, n] for l in range(2)],
                                    [khl[:, u, l, n * A:(n + 1) * A] for l in range(2)])
                last.then_inc(s.s_psum, 1)

            def q_k(k, ring, u):
                b = 2 * k + u
                need(pe, s.xl_done, b + 1)
                x2 = [xhl[:, u, l, :] for l in range(2)]
                need(pe, s.qh_done, b)
                products(bank_q, [w_hl[:, l, 0, :] for l in range(2)], x2).then_inc(s.q_psum, 1)
                need(pe, s.kh_done, b)
                products(bank_k, [w_hl[:, l, 1, :] for l in range(2)], x2).then_inc(s.k_psum, 1)

            def v(k, ring, u):
                b = 2 * k + u
                need(pe, s.vh_done, b)
                need(pe, s.o32_done, 2 * k - 4)
                for j in range(TILES):
                    last = products(bank_vo[:, j * P:(j + 1) * P], [xhl[:, u, l, j * P:(j + 1) * P] for l in range(2)],
                                    [w_hl[:, l, 2, :] for l in range(2)])
                last.then_inc(s.v_psum, 1)

            def et(k, ring, u):
                c = 2 * k + u
                need(pe, s.e_done, c + 1)
                need(pe, s.et_done, c)
                if u == 0:
                    need(pe, s.oth_done, c - 4)
                for j in range(TILES):
                    last = t.transpose(bank_t[:, j * P:(j + 1) * P], sm[:, u, j * P:(j + 1) * P], ident)
                last.then_inc(s.et_psum, 1)

            def sums(k, ring):
                need(pe, s.et_done, 2 * k + 2)
                need(pe, s.p_done, 2 * k)
                e4 = pt[:].rearrange("p u (g q) -> p q u g", q=A)
                for q in range(A):
                    lo = HALF * (q % 2)
                    dst = bank_d[lo:lo + HALF, (q // 2) * 64:(q // 2 + 1) * 64]
                    last = t.matmul(dst, msum[:, q, :], e4[:, q], start=True, stop=True)
                last.then_inc(s.d_psum, 1)

            def weights(k, ring):
                need(pe, s.rl_done, k + 1)
                need(pe, s.p_done, 2 * k)
                for q in range(A):
                    lo = HALF * (q % 2)
                    for part in range(3):
                        last = t.matmul(ps[:, 6 + q % 2, (q // 2) * 64:(q // 2 + 1) * 64], mspread[lo:lo + S * 8, q // 2, :],
                                        rparts[lo:lo + S * 8, part, q // 2, :], start=part == 0, stop=part == 2)
                last.then_inc(s.w_psum, 1)

            def pv(k, ring, u):
                e, slot = 2 * k + u, 2 * ring + u
                need(pe, s.bdp_done, e + 1)
                need(pe, s.bdp_rest_done, e + 1)
                if u:
                    need(pe, s.o32_done, e)
                else:
                    need(pe, s.vh_done, most(e + 6, B))
                    need(pe, s.vl_done, e + 2)
                for j in range(TILES):
                    for h in range(H):
                        n = j * H + h
                        last = products(bank_vo[:, n * HD:(n + 1) * HD], [bdp[:, u, l, n] for l in range(2)],
                                        [vhl[:, slot, l, n * HD:(n + 1) * HD] for l in range(2)])
                last.then_inc(s.o_psum, 1)

            def ot(k, ring, u):
                e = 2 * k + u
                need(pe, s.o32_done, e + 1)
                need(pe, s.oth_done, e)
                if u == 0:
                    need(pe, s.et_done, most(e + 6, B))
                for j in range(TILES):
                    last = t.transpose(bank_t[:, j * P:(j + 1) * P], o32[:, u, j * P:(j + 1) * P], ident)
                last.then_inc(s.ot_psum, 1)

            def y(k, ring, u):
                e = 2 * k + u
                need(pe, s.otl_done, e + 1)
                need(pe, s.x1_done, e)
                if u == 0:
                    need(pe, s.xi_done, most(e + 8, B))
                t.matmul(bank_xy, ones16[0:64, :], bo_hl[:], start=True, stop=False)
                for j in range(TILES):
                    o = bank_xy[:, j * P:(j + 1) * P]
                    last = products(o, [othl[:, u, l, j * P:(j + 1) * P] for l in range(2)],
                                    [w_hl[:, l, 3, :] for l in range(2)], start=False, stop=j == TILES - 1)
                last.then_inc(s.y_psum, 1)

            pipelined(pe, PAIRS, 4, 3, [
                (1, qk, 0), (3, pv, 0), (0, xT, 0), (2, weights), (0, xT, 1), (1, qk, 1), (1, et, 0), (0, q_k, 0),
                (1, et, 1), (3, pv, 1), (3, ot, 0), (1, sums), (0, v, 0), (3, ot, 1), (0, q_k, 1), (3, y, 0),
                (0, v, 1), (3, y, 1),
            ])

        @block.vector
        def _(dve):
            v = nc.vector
            steps = [0]

            def step(ins):
                ins.then_inc(s.setup_v, 1)
                steps[0] += 1
                dve.wait_ge(s.setup_v, steps[0])

            dve.wait_ge(s.consts_in, 16)
            dve.wait_ge(s.masks_in, 16)
            step(v.memset(ones16[:], 1.0))
            step(v.tensor_scalar(mflt[:], mraw[:], 0.0, None, ALU.is_gt))
            step(v.tensor_tensor(mflt[:], mflt[:], const(cst, "eye_qk")[0:S * A, :], ALU.max))
            step(v.tensor_copy(mrep[:], mflt[:].rearrange("p (o k) -> p o k", o=1).to_broadcast([S * A, H, A])))
            step(v.memset(bo_hl[:], 0.0))
            dve.wait_ge(s.weights_in, 16 * 8)
            step(v.tensor_scalar(w_f[:], wstage[:], WS, None, ALU.mult))
            step(v.tensor_copy(w_hl[:, 0], w_f[:]))
            step(v.tensor_tensor(w_hl[:, 1], w_f[:], w_hl[:, 0], ALU.subtract))
            dve.wait_ge(s.setup_pe, 1)
            step(v.tensor_copy(mkq[:].rearrange("p s q -> p (s q)"), ps[:, 4, 0:S * A]))
            for n in range(8):
                step(v.tensor_scalar(msum[:, :, n * S:(n + 1) * S], mkq[:].rearrange("p s q -> p q s"),
                                     block8[:, n:n + 1], None, ALU.mult))
            step(v.tensor_copy(msum[:, :, 8 * S:HALF], msum[:, :, 0:HALF - 8 * S]))
            dve.wait_ge(s.setup_pe, 2)
            step(v.tensor_copy(embT[:], ps[:, 5, 0:A]))
            dve.wait_ge(s.setup_pe, 3)
            step(v.tensor_tensor(brow[:], ps[0:1, 6, 0:C], bo_row[:], ALU.add))
            step(v.tensor_scalar(brow[:], brow[:], WS, None, ALU.mult))
            row = brow[:].rearrange("p (o c) -> p o c", o=1).to_broadcast([1, TILES, C])
            hi, lo = (bo_hl[r:r + 1, :].rearrange("p (o c) -> p o c", o=TILES) for r in (0, 32))
            step(v.tensor_copy(hi, row))
            step(v.tensor_copy(lo, row))
            step(v.tensor_tensor(brow[:], brow[:], bo_hl[0:1, 0:C], ALU.subtract))
            step(v.tensor_copy(lo, row))

            for b in range(B):
                dve.wait_ge(s.gT_psum, b + 1)
                v.bn_stats(gst6[:, b, :], ps[:, b % 4, :]).then_inc(s.gst_done, 1)
            dve.wait_ge(s.gst_done, B)
            even, dev_even, odd, dev_odd = (gst6[:, :, n] for n in (1, 2, 4, 5))
            step(v.tensor_tensor(gtmp[:, 0, :], even, even, ALU.mult))
            step(v.tensor_tensor(gtmp[:, 1, :], odd, odd, ALU.mult))
            step(v.tensor_tensor(gtmp[:, 1, :], gtmp[:, 0, :], gtmp[:, 1, :], ALU.add))
            step(v.tensor_tensor(gtmp[:, 0, :], dev_even, dev_odd, ALU.add))
            step(v.scalar_tensor_tensor(gsum[:, 1, :], gtmp[:, 0, :], 2.0 / TOK, gtmp[:, 1, :], ALU.mult, ALU.add))
            v.tensor_tensor(gsum[:, 0, :], even, odd, ALU.add).then_inc(s.gsum_done, 1)
            dve.wait_ge(s.setup_pe, 4)
            for q4 in range(4):
                src = ps[0:HALF, q4, :].rearrange("p (n r c) -> p n r c", n=2, r=2)
                for r in range(2):
                    ins = v.tensor_copy(mspread[HALF * r:HALF * (r + 1), 2 * q4:2 * q4 + 2, :], src[:, :, r, :])
            ins.then_inc(s.spread_done, 1)
            dve.wait_ge(s.spread_done, 1)
            dve.wait_ge(s.gmean_psum, 1)
            v.tensor_copy(gmean[:].rearrange("p n b -> p (n b)"), ps[:, 7, 0:2 * B]).then_inc(s.gst_done, 1)
            dve.wait_ge(s.gst_done, B + 1)
            step(v.tensor_tensor(gtmp[:, 0, :], gmean[:, 0, :], gmean[:, 0, :], ALU.mult))
            v.scalar_tensor_tensor(gtmp[:, 1, :], gmean[:, 1, :], GN_EPS, gtmp[:, 0, :], ALU.add, ALU.subtract).then_inc(s.gvar_done, 1)
            dve.wait_ge(s.rstd_done, 1)
            step(v.scalar_tensor_tensor(nmr[:], gmean[:, 0, :], -1.0, rstd[:], ALU.mult, ALU.mult))
            step(v.tensor_tensor(shift[:], embT[:].rearrange("p (o a) -> p o a", o=1).to_broadcast([P, B, A]),
                                 nmr[:].rearrange("p (b o) -> p b o", o=1).to_broadcast([P, B, A]), ALU.add))

            def xi_(k, ring, u):
                b = 2 * k + u
                need(dve, s.xT_psum, b + 1)
                need(dve, s.xl_done, b - 1)
                need(dve, s.xh_done, b - 1)
                v.scalar_tensor_tensor(xi[:, u, :].rearrange("p (t a) -> p t a", a=A), bank_xy.rearrange("p (a t) -> p t a", a=A),
                                       rstd[:, bass.ds(b, 1)],
                                       shift[:, bass.ds(b, 1), :].to_broadcast([P, T, A]), ALU.mult, ALU.add).then_inc(s.xi_done, 1)

            def shifted(k, ring, u):
                c = 2 * k + u
                need(dve, s.s_psum, c + 1)
                s3 = bank_s.rearrange("p (t k) -> p t k", k=A)
                v.tensor_reduce(rmax[:, u, :], s3, AX.X, ALU.max).then_inc(s.rmax_done, 1)
                need(dve, s.rmax_done, c + 1)
                need(dve, s.et_psum, c - 1)
                v.tensor_tensor(sm[:, u, :].rearrange("p (t k) -> p t k", k=A), s3,
                                rmax[:, u, :].rearrange("p (t o) -> p t o", o=1).to_broadcast([P, T, A]), ALU.subtract).then_inc(s.sm_done, 1)

            def p(k, ring, u):
                need(dve, s.w_psum, k + 1)
                w = ps[:, 6:8, :].rearrange("p r (n u g) -> p u g n r", n=A // 2, u=2)[:, u]
                e4 = pt[:, u, :].rearrange("p (g n r) -> p g n r", n=A // 2, r=2)
                v.tensor_tensor(e4, e4, w, ALU.mult).then_inc(s.p_done, 1)

            def spread(dst, src, done):
                for n in range(ON_DVE):
                    ins = v.tensor_scalar(dst[:, :, :, n, :], src.rearrange("p l (g q) -> p l g q", q=A), block8[:, n:n + 1], None, ALU.mult)
                ins.then_inc(done, 1)

            def spread_q(k, ring, u):
                need(dve, s.qh_done, 2 * k + u + 1)
                need(dve, s.ql_done, 2 * k + u + 1)
                need(dve, s.s_psum, 2 * k + u - 1)
                spread(bdq[:, u], qhl[:, u], s.bdq_done)

            def spread_p(k, ring, u):
                need(dve, s.ph_done, 2 * k + u + 1)
                need(dve, s.pl_done, 2 * k + u + 1)
                need(dve, s.o_psum, 2 * k + u - 1)
                spread(bdp[:, u], phl[:, u], s.bdp_done)

            def reciprocals(k, ring):
                need(dve, s.d_psum, k + 1)
                need(dve, s.w_psum, k)
                v.reciprocal(recip[:].rearrange("p n g -> p (n g)"), bank_d).then_inc(s.recip_done, 1)

            def add(k, ring, u):
                e = 2 * k + u
                need(dve, s.y_psum, e + 1)
                r = resid[:, e, :]
                v.scalar_tensor_tensor(r, bank_xy, 1.0 / WS, r, ALU.mult, ALU.add).then_inc(s.x1_done, 1)

            for loaded in r_in:
                dve.wait_ge(loaded, 16)
            pipelined(dve, PAIRS, 4, 3, [
                (0, xi_, 0), (1, shifted, 0), (2, p, 0), (2, p, 1), (0, xi_, 1), (1, shifted, 1), (2, spread_p, 0),
                (0, spread_q, 0), (1, reciprocals), (3, add, 0), (2, spread_p, 1), (3, add, 1), (0, spread_q, 1),
            ])


def chain(eng, sem, base):
    done = [0]

    def step(ins, wait=True):
        ins.then_inc(sem, 1)
        done[0] += 1
        if wait:
            eng.wait_ge(sem, base + done[0])
    return step


def woven_chain(eng, sem, base):
    done = [0]

    def step(ins, wait=True):
        ins.then_inc(sem, 1)
        done[0] += 1
        count = base + done[0]
        yield
        if wait:
            eng.wait_ge(sem, count)
    return step


def token_mixer(nc, cst, resid, ones16, ident, late, ffn, rows_dram, Wq, bq, Wk, bk, Wv, bv, router_w, router_b,
                gate_up, gate_up_bias, down, down_bias):
    rank_of = const(cst, "rank_of")
    w1_hl, b1_hl, w2_hl, b2_hl = ffn["w1_hl"], ffn["b1_hl"], ffn["w2_hl"], ffn["b2_hl"]
    with ExitStack() as ctx:
        def sb(name, shape, dt=F32):
            return ctx.enter_context(nc.sbuf_tensor(name, shape, dt))

        wq = sb("m_wq", [P, C])
        wkv = sb("m_wkv", [P, 2, C])
        wr = sb("m_wr", [P, E])
        bq_col = sb("m_bq", [P, 1])
        bkv_f = sb("m_bkv_f", [1, 2, C])
        bkv_t = sb("m_bkv_t", [1, 2, C])
        bkv_hl = sb("m_bkv_hl", [64, 2, 2 * C], F16)
        rb = sb("m_rb", [P, E])
        w1_f = sb("m_w1_f", [P, E, 2 * I])
        w2_f = sb("m_w2_f", [P, E, 2, C])
        b1_f = sb("m_b1_f", [1, E * 2 * I])
        b2_f = sb("m_b2_f", [1, E * C])
        before16 = sb("m_before16", [P, P], F16)
        half = sb("m_half", [P, 8])
        st6 = sb("m_st6", [P, 2, 8, 6])
        stw = sb("m_stw", [P, 2, 6, 8])
        xn = sb("m_xn", [P, 2, TOK])
        xt = sb("m_xt", [P, 2, TOK])
        ef = sb("m_ef", [P, 2, TOK])
        rf = sb("m_rf", [P, 2, TOK])
        qf = sb("m_qf", [P, 2, TOK])
        kf = sb("m_kf", [P, 2, TOK])
        vo = sb("m_vo", [P, 2, TILES, C + 2])
        kv = sb("m_kv", [P, 2, C + H])
        den = sb("m_den", [P, 2, TILES, H])
        mix = sb("m_mix", [P, TOK])
        xn2 = sb("m_xn2", [P, 2, TOK])
        xt2 = sb("m_xt2", [P, 2, TOK])
        rows = sb("m_rows", [P, 4, TILES, ROW])
        place = sb("m_place", [P, 4, TILES, 2], I32)
        lg = sb("m_lg", [P, 8, E])
        oh = sb("m_oh", [P, 2, 8, E])
        tmp = sb("m_tmp", [P, 2, 8, E])
        best = sb("m_best", [P, 8, 8])
        oh16 = sb("m_oh16", [P, 8, E], F16)
        ahead16 = sb("m_ahead16", [P, 9, E], F16)
        spot = sb("m_spot", [P, 8, E])

        ps = ctx.enter_context(nc.psum_tensor("m_ps", [P, 8, TOK], F32))
        bank_x, bank_q, banks_kv, bank_s, banks_o, bank_r = ps[:, 0], ps[:, 1], ps[:, 2:4], ps[:, 4], ps[:, 5:7], ps[:, 7]

        s = Named({n: ctx.enter_context(nc.semaphore("m_" + n)) for n in """
            small_in w1_in w2_in b_in set_v set_g wf_done wh_done wl_done bf_done b_zero bh_done bl_done
            stat1 stat2 pow1 pow2 norm1 xT xt_done q_psum kv_psum qe_done ke_done v_done qf_done kf_done
            s_psum kv_done o_psum mix_step add_done norm2 hi_done lo_done xT2 xt2_done lg_psum route ew_done
            rank_psum place_step place_done rows_out table late_in nobody_in""".split()})

        b1_row, b2_row = b1_hl[:].rearrange("p e i -> p (e i)"), b2_hl[:].rearrange("p e c -> p (e c)")

        block = ctx.enter_context(nc.Block())

        @block.sync
        def _(sp):
            sp.dma_start(cst[:], late).then_inc(s.late_in, 16)
            sp.dma_start(wq[:], Wq).then_inc(s.small_in, 16)
            sp.dma_start(wkv[:, 0, :], Wk).then_inc(s.small_in, 16)
            sp.dma_start(wkv[:, 1, :], Wv).then_inc(s.small_in, 16)
            sp.dma_start(wr[:], router_w).then_inc(s.small_in, 16)
            sp.dma_start(bq_col[:], bq.rearrange("(c o) -> c o", o=1)).then_inc(s.small_in, 16)
            sp.dma_start(bkv_f[:, 0, :], bk.rearrange("(o c) -> o c", o=1)).then_inc(s.small_in, 16)
            sp.dma_start(bkv_f[:, 1, :], bv.rearrange("(o c) -> o c", o=1)).then_inc(s.small_in, 16)
            sp.dma_start(rb[:], router_b.rearrange("(o e) -> o e", o=1).to_broadcast([P, E])).then_inc(s.small_in, 16)
            sp.dma_start(w1_f[:], gate_up.rearrange("e c i -> c e i")).then_inc(s.w1_in, 16)
            sp.dma_start(w2_f[:], down.rearrange("e (n i) c -> i e n c", n=2)).then_inc(s.w2_in, 16)
            sp.dma_start(b1_f[:], gate_up_bias.rearrange("(o e) i -> o (e i)", o=1)).then_inc(s.b_in, 16)
            sp.dma_start(b2_f[:], down_bias.rearrange("(o e) c -> o (e c)", o=1)).then_inc(s.b_in, 16)

            sp.wait_ge(s.set_v, 10)
            sp.dma_start(rows_dram[E * REGION:E * REGION + BLOCK].rearrange("(n p) w -> p n w", p=P), ffn["nobody"][:]).then_inc(s.nobody_in, 16)
            sp.wait_ge(s.table, 2)
            for e in range(E):
                row = sp.value_load(ffn["tail_i"][0:1, e:e + 1], min_val=e * REGION, max_val=(e + 1) * REGION - BLOCK)
                sp.dma_start(rows_dram[bass.ds(row, BLOCK)].rearrange("(n p) w -> p n w", p=P), ffn["nobody"][:]).then_inc(s.nobody_in, 16)
            sp.wait_ge(s.nobody_in, 16 * (E + 1))

        @block.gpsimd
        def _(pool):
            g = nc.gpsimd
            g.memset(half[:], -0.5).then_inc(s.set_g, 1)
            g.memset(b1_hl[:], 0.0).then_inc(s.b_zero, 1)
            g.memset(b2_hl[:], 0.0).then_inc(s.b_zero, 1)
            pool.wait_ge(s.set_g, 1)

            def biases_low(k, ring):
                if not isinstance(k, int) or k != 2:
                    return
                pool.wait_ge(s.bh_done, 2)
                g.tensor_tensor(b1_f[:], b1_f[:], b1_row[0:1, :], ALU.subtract).then_inc(s.bl_done, 1)
                g.tensor_tensor(b2_f[:], b2_f[:], b2_row[0:1, :], ALU.subtract).then_inc(s.bl_done, 1)

            def power(k, ring, n, stat, steps, norm, pow_done):
                pool.wait_ge(stat, steps * (k + 1))
                need(pool, norm, 2 * k)
                g.tensor_tensor(stw[:, n, 5, :], stw[:, n, 4, :], half[:], ALU.pow).then_inc(pow_done, 1)

            def rows_ready(k, ring):
                pool.wait_ge(s.place_done, k + 1)
                pool.wait_ge(s.lo_done, 2 * k + 2)
                need(pool, s.rows_out, 16 * 16 * k)

            def send(k, ring, u):
                slot = 2 * ring + u
                for j in range(TILES):
                    for n in range(2):
                        g.indirect_dma_start(rows_dram, bass.IndirectOffsetOnAxis(ap=place[:, slot, j, n:n + 1], axis=0),
                                             rows[:, slot, j, :], None).then_inc(s.rows_out, 16)

            pipelined(pool, PAIRS, 6, 2, [
                (5, rows_ready), (3, power, 1, s.stat2, LN_STEPS, s.norm2, s.pow2),
                (0, power, 0, s.stat1, LN_STEPS, s.norm1, s.pow1), (0, biases_low), (5, send, 0), (5, send, 1),
            ])
            pool.wait_ge(s.rows_out, 16 * 16 * PAIRS)

        @block.scalar
        def _(act):
            a = nc.scalar
            act.wait_ge(s.small_in, 16 * 8)

            def weights(k, ring):
                if not isinstance(k, int) or not 1 <= k < 5:
                    return
                two = slice(2 * (k - 1), 2 * k)
                act.wait_ge(s.w1_in, 16)
                a.activation(w1_f[:, two], w1_f[:, two], ACT.Copy, scale=2 * WS).then_inc(s.wf_done, 1)
                act.wait_ge(s.w2_in, 16)
                a.activation(w2_f[:, two], w2_f[:, two], ACT.Copy, scale=WS).then_inc(s.wf_done, 1)
                act.wait_ge(s.wf_done, 2 * k)
                a.activation(w1_hl[:, two, 0, :], w1_f[:, two], ACT.Copy).then_inc(s.wh_done, 1)
                a.activation(w2_hl[:, two, 0], w2_f[:, two], ACT.Copy).then_inc(s.wh_done, 1)

            def biases(k, ring):
                if not isinstance(k, int) or k > 3:
                    return
                if k == 0:
                    act.wait_ge(s.b_in, 32)
                    a.activation(b1_f[:], b1_f[:], ACT.Copy, scale=WS).then_inc(s.bf_done, 1)
                    a.activation(b2_f[:], b2_f[:], ACT.Copy, scale=WS).then_inc(s.bf_done, 1)
                if k == 1:
                    act.wait_ge(s.bf_done, 2)
                    act.wait_ge(s.b_zero, 2)
                    a.activation(b1_row[0:1, :], b1_f[:], ACT.Copy).then_inc(s.bh_done, 1)
                    a.activation(b2_row[0:1, :], b2_f[:], ACT.Copy).then_inc(s.bh_done, 1)
                if k == 3:
                    act.wait_ge(s.bl_done, 2)
                    a.activation(b1_row[32:33, :], b1_f[:], ACT.Copy).then_inc(s.bh_done, 1)
                    a.activation(b2_row[32:33, :], b2_f[:], ACT.Copy).then_inc(s.bh_done, 1)

            def xt_(k, ring, u):
                b = 2 * k + u
                need(act, s.xT, b + 1)
                need(act, s.kv_psum, b - 1)
                need(act, s.q_psum, b - 1)
                a.activation(xt[:, u, :], bank_x, ACT.Copy).then_inc(s.xt_done, 1)

            def q(k, ring, u):
                b = 2 * k + u
                need(act, s.q_psum, b + 1)
                need(act, s.qf_done, b)
                a.activation(ef[:, 0, :], bank_q, ACT.Exp, bias=bq_col[:]).then_inc(s.qe_done, 1)
                a.activation(rf[:, 0, :], bank_q, ACT.Relu, bias=bq_col[:]).then_inc(s.qe_done, 1)

            def k_v(k, ring, u):
                b = 2 * k + u
                need(act, s.kv_psum, b + 1)
                need(act, s.kf_done, b)
                kv4 = banks_kv.rearrange("p n (i w c) -> p (n i) w c", i=2, w=2)
                a.activation(ef[:, 1, :].rearrange("p (j c) -> p j c", j=TILES), kv4[:, :, 0, :], ACT.Exp).then_inc(s.ke_done, 1)
                a.activation(rf[:, 1, :].rearrange("p (j c) -> p j c", j=TILES), kv4[:, :, 0, :], ACT.Relu).then_inc(s.ke_done, 1)
                need(act, s.s_psum, b - 1)
                a.activation(vo[:, u, :, 0:C], kv4[:, :, 1, :], ACT.Copy).then_inc(s.v_done, 1)

            def xt2_(k, ring, u):
                d = 2 * k + u
                need(act, s.xT2, d + 1)
                need(act, s.lg_psum, d - 1)
                a.activation(xt2[:, u, :], bank_r, ACT.Copy).then_inc(s.xt2_done, 1)

            def hi(k, ring, u):
                d, slot = 2 * k + u, 2 * ring + u
                need(act, s.norm2, d + 1)
                need(act, s.rows_out, 16 * 16 * (k - 1))
                dst = rows[:, slot].bitcast(F16)[:, :, 0:C]
                a.activation(dst, xn2[:, u, :].rearrange("p (j c) -> p j c", j=TILES), ACT.Copy).then_inc(s.hi_done, 1)

            def ew(k, ring):
                need(act, s.route, ROUTE_STEPS * k + 13)
                a.activation(best[:, 3, :], best[:, 2, :], ACT.Exp).then_inc(s.ew_done, 1)

            pipelined(act, PAIRS, 6, 2, [
                (1, xt_, 0), (4, xt2_, 0), (1, xt_, 1), (4, xt2_, 1), (0, weights), (1, q, 0), (1, k_v, 0), (4, ew),
                (4, hi, 0), (4, hi, 1), (1, q, 1), (1, k_v, 1), (0, biases),
            ])

        @block.tensor
        def _(pe):
            t = nc.tensor
            pe.wait_ge(s.set_v, 13)

            def xT(k, ring, u):
                b = 2 * k + u
                need(pe, s.norm1, b + 1)
                need(pe, s.xt_done, b)
                if u == 0:
                    need(pe, s.place_done, k - 3)
                for j in range(TILES):
                    last = t.transpose(bank_x[:, j * P:(j + 1) * P], xn[:, u, j * P:(j + 1) * P], ident)
                last.then_inc(s.xT, 1)

            def q(k, ring, u):
                b = 2 * k + u
                need(pe, s.xt_done, b + 1)
                need(pe, s.qe_done, 2 * b)
                t.matmul(bank_q, wq[:], xt[:, u, :], start=True, stop=True).then_inc(s.q_psum, 1)

            def k_v(k, ring, u):
                b = 2 * k + u
                need(pe, s.xt_done, b + 1)
                need(pe, s.v_done, b)
                for n in range(2):
                    t.matmul(banks_kv[:, n], ones16[0:64, :], bkv_hl[:].rearrange("p i c -> p (i c)"), start=True, stop=False)
                    for i in range(2):
                        j = 2 * n + i
                        last = t.matmul(banks_kv[:, n, i * 2 * C:(i + 1) * 2 * C], xt[:, u, j * P:(j + 1) * P],
                                        wkv[:].rearrange("p w c -> p (w c)"), start=False, stop=i == 1)
                last.then_inc(s.kv_psum, 1)

            def sums(k, ring, u):
                c = 2 * k + u
                need(pe, s.kf_done, c + 1)
                need(pe, s.v_done, c + 1)
                need(pe, s.kv_done, c)
                for j in range(TILES):
                    last = t.matmul(bank_s[:, 0:C + 2], kf[:, u, j * P:(j + 1) * P], vo[:, u, j, :], start=j == 0, stop=j == TILES - 1)
                last.then_inc(s.s_psum, 1)

            def outs(k, ring, u):
                c = 2 * k + u
                need(pe, s.kv_done, c + 1)
                need(pe, s.qf_done, c + 1)
                need(pe, s.add_done, c)
                for j in range(TILES):
                    last = t.matmul(banks_o[:, j // 2, (j % 2) * 256:(j % 2) * 256 + C + H], qf[:, u, j * P:(j + 1) * P], kv[:, u, :],
                                    start=True, stop=True)
                last.then_inc(s.o_psum, 1)

            def xT2(k, ring, u):
                d = 2 * k + u
                need(pe, s.norm2, d + 1)
                need(pe, s.xt2_done, d)
                for j in range(TILES):
                    last = t.transpose(bank_r[:, j * P:(j + 1) * P], xn2[:, u, j * P:(j + 1) * P], ident)
                last.then_inc(s.xT2, 1)

            def logits(k, ring, u):
                need(pe, s.xt2_done, 2 * k + u + 1)
                need(pe, s.place_done, k)
                need(pe, s.xt_done, most(2 * k + 8, B))
                for j in range(TILES):
                    n = (u * TILES + j) * E
                    last = t.matmul(bank_x[:, n:n + E], xt2[:, u, j * P:(j + 1) * P], wr[:], start=True, stop=True)
                last.then_inc(s.lg_psum, 1)

            def ranks(k, ring):
                need(pe, s.route, ROUTE_STEPS * k + ROUTE_STEPS)
                flat = bank_x[:, 64:64 + 8 * E]
                t.matmul(flat, before16[:], oh16[:].rearrange("p n e -> p (n e)"), start=True, stop=False)
                t.matmul(flat, ones16[:], ahead16[:, 0:8, :].rearrange("p n e -> p (n e)"), start=False, stop=True).then_inc(s.rank_psum, 1)

            pipelined(pe, PAIRS, 6, 2, [
                (2, sums, 0), (2, sums, 1), (1, xT, 0), (4, xT2, 0), (2, outs, 0), (1, xT, 1), (4, xT2, 1),
                (4, logits, 0), (4, logits, 1), (1, q, 0), (1, k_v, 0), (4, ranks), (2, outs, 1), (1, q, 1),
                (1, k_v, 1),
            ])
            pe.wait_ge(s.place_done, PAIRS)
            t.matmul(bank_s[:, 0:E], ones16[:], ahead16[:, 0, :], start=True, stop=True).then_inc(s.rank_psum, 1)

        @block.vector
        def _(dve):
            v = nc.vector
            dve.wait_ge(s.small_in, 16 * 8)
            dve.wait_ge(s.late_in, 16)
            step = chain(dve, s.set_v, 0)
            step(v.tensor_scalar(wq[:], wq[:], 2.0, None, ALU.mult), False)
            step(v.tensor_scalar(wkv[:], wkv[:], 2.0, None, ALU.mult), False)
            step(v.tensor_scalar(wr[:], wr[:], 2.0, None, ALU.mult), False)
            step(v.memset(bkv_hl[:], 0.0), False)
            step(v.memset(vo[:, :, :, C:C + 1], 1.0), False)
            step(v.memset(vo[:, :, :, C + 1:C + 2], 0.0), False)
            step(v.memset(ahead16[:], 0.0), False)
            step(v.memset(ffn["nobody"][:], 0.0))
            step(v.memset(ffn["nobody"][:, :, C + 3:C + 4], NO_SLOT), False)
            step(v.tensor_copy(before16[:], const(cst, "before")))
            row = bkv_f[:].rearrange("p w c -> p (w c)")
            both = row.rearrange("p (o c) -> p o c", o=1).to_broadcast([1, 2, 2 * C])
            step(v.tensor_copy(bkv_hl[0:1], both))
            tmp_row = bkv_t[:].rearrange("p w c -> p (w c)")
            step(v.tensor_tensor(tmp_row, row, bkv_hl[0:1, 0, :], ALU.subtract))
            step(v.tensor_copy(bkv_hl[32:33], tmp_row.rearrange("p (o c) -> p o c", o=1).to_broadcast([1, 2, 2 * C])))

            def weights_low(k, ring):
                if not isinstance(k, int) or k < PAIRS - 4:
                    return
                two = slice(2 * (k - PAIRS + 4), 2 * (k - PAIRS + 5))
                dve.wait_ge(s.wh_done, 8)
                v.tensor_tensor(w1_hl[:, two, 1, :], w1_f[:, two], w1_hl[:, two, 0, :], ALU.subtract).then_inc(s.wl_done, 1)
                v.tensor_tensor(w2_hl[:, two, 1], w2_f[:, two], w2_hl[:, two, 0], ALU.subtract).then_inc(s.wl_done, 1)

            def stats(k, ring, n, sem):
                b = 2 * k
                step = woven_chain(dve, sem, LN_STEPS * k)
                if n == 1:
                    dve.wait_ge(s.late_in, 16)
                    need(dve, s.add_done, b + 2)
                for u in range(2):
                    for j in range(TILES):
                        ins = v.bn_stats(st6[:, n, u * TILES + j, :], resid[:, b + u, j * C:(j + 1) * C])
                        if u * TILES + j < 2 * TILES - 1:
                            yield
                yield from step(ins)
                even, dev_even, odd, dev_odd = (st6[:, n, :, i] for i in (1, 2, 4, 5))
                w = stw[:, n]
                yield from step(v.tensor_tensor(w[:, 0], even, odd, ALU.subtract), False)
                yield from step(v.tensor_tensor(w[:, 1], even, odd, ALU.add), False)
                yield from step(v.scalar_tensor_tensor(w[:, 2], dev_even, C * LN_EPS, dev_odd, ALU.add, ALU.add))
                yield from step(v.tensor_tensor(w[:, 0], w[:, 0], w[:, 0], ALU.mult), False)
                yield from step(v.tensor_scalar(w[:, 3], w[:, 1], 0.5, None, ALU.mult))
                yield from step(v.scalar_tensor_tensor(w[:, 4], w[:, 2], 4.0 / C, w[:, 0], ALU.mult, ALU.add), False)

            def norm(k, ring, u, n, dst, pow_done, done):
                b = 2 * k + u
                need(dve, pow_done, k + 1)
                if n == 0:
                    need(dve, s.xT, b - 1)
                else:
                    need(dve, s.xT2, b - 1)
                    need(dve, s.lo_done, b - 1)
                for j in range(TILES):
                    i = u * TILES + j
                    ins = v.tensor_scalar(dst[:, u, j * C:(j + 1) * C], resid[:, b, j * C:(j + 1) * C],
                                          stw[:, n, 3, i:i + 1], stw[:, n, 5, i:i + 1], ALU.subtract, ALU.mult)
                    if j == TILES - 1:
                        ins.then_inc(done, 1)
                    yield

            def feature(k, ring, u):
                b = 2 * k + u
                need(dve, s.qe_done, 2 * b + 2)
                need(dve, s.o_psum, b - 1)
                v.scalar_tensor_tensor(qf[:, u, :], ef[:, 0, :], 1.0, rf[:, 0, :], ALU.min, ALU.add).then_inc(s.qf_done, 1)
                need(dve, s.ke_done, 2 * b + 2)
                need(dve, s.s_psum, b - 1)
                v.scalar_tensor_tensor(kf[:, u, :], ef[:, 1, :], 1.0, rf[:, 1, :], ALU.min, ALU.add).then_inc(s.kf_done, 1)

            def keys_values(k, ring, u):
                c = 2 * k + u
                need(dve, s.s_psum, c + 1)
                need(dve, s.o_psum, c - 1)
                v.tensor_tensor(kv[:, u, 0:C], bank_s[:, 0:C], const(cst, "block_kv"), ALU.mult)
                v.tensor_tensor(kv[:, u, C:C + H], bank_s[:, C:C + 1].to_broadcast([P, H]), const(cst, "block_ks"), ALU.mult).then_inc(s.kv_done, 1)

            def mixed(k, ring, u):
                c = 2 * k + u
                step = chain(dve, s.mix_step, 3 * c)
                need(dve, s.o_psum, c + 1)
                need(dve, s.add_done, c)
                o4 = banks_o.rearrange("p n (i c) -> p (n i) c", i=2)
                step(v.tensor_scalar(den[:, 0], o4[:, :, C:C + H], ATT_EPS / TOK, None, ALU.add))
                step(v.reciprocal(den[:, 1], den[:, 0]))
                weight = den[:, 1].rearrange("p j (h o) -> p j h o", o=1).to_broadcast([P, TILES, H, HD])
                step(v.tensor_tensor(mix[:].rearrange("p (j h d) -> p j h d", j=TILES, h=H),
                                     o4[:, :, 0:C].rearrange("p j (h d) -> p j h d", h=H), weight, ALU.mult))
                v.tensor_tensor(resid[:, c, :], resid[:, c, :], mix[:], ALU.add).then_inc(s.add_done, 1)

            def lo(k, ring, u):
                d, slot = 2 * k + u, 2 * ring + u
                need(dve, s.hi_done, d + 1)
                r = rows[:, slot].bitcast(F16)
                v.tensor_tensor(r[:, :, C:2 * C], xn2[:, u, :].rearrange("p (j c) -> p j c", j=TILES), r[:, :, 0:C],
                                ALU.subtract).then_inc(s.lo_done, 1)

            def route(k, ring):
                step = woven_chain(dve, s.route, ROUTE_STEPS * k)
                need(dve, s.lg_psum, 2 * k + 2)
                shape = [P, 8, E]
                wide = lambda ap: ap.rearrange("p (n o) -> p n o", o=1).to_broadcast(shape)
                rank3 = rank_of.rearrange("p (n e) -> p n e", e=E)
                bias = rb[:].rearrange("p (o e) -> p o e", o=1).to_broadcast(shape)
                yield from step(v.tensor_tensor(lg[:], bank_x[:, 0:8 * E].rearrange("p (n e) -> p n e", e=E), bias, ALU.add))
                for n in range(2):
                    yield from step(v.tensor_reduce(best[:, n, :], lg[:], AX.X, ALU.max))
                    yield from step(v.tensor_tensor(tmp[:, n], lg[:], wide(best[:, n, :]), ALU.is_equal))
                    yield from step(v.tensor_tensor(tmp[:, n], tmp[:, n], rank3, ALU.mult))
                    yield from step(v.tensor_reduce(best[:, 4 + n, :], tmp[:, n], AX.X, ALU.max))
                    if n == 0:
                        yield from step(v.tensor_tensor(oh[:, 0], tmp[:, 0], wide(best[:, 4, :]), ALU.is_equal))
                        yield from step(v.scalar_tensor_tensor(lg[:], oh[:, 0], -3e38, lg[:], ALU.mult, ALU.add))
                yield from step(v.tensor_tensor(oh[:, 1], tmp[:, 1], wide(best[:, 5, :]), ALU.is_equal), False)
                yield from step(v.tensor_tensor(best[:, 2, :], best[:, 1, :], best[:, 0, :], ALU.subtract))
                yield from step(v.tensor_tensor(oh16[:], oh[:, 0], oh[:, 1], ALU.add))
                for n in range(8):
                    yield from step(v.tensor_tensor(ahead16[:, n + 1, :], ahead16[:, n, :], oh16[:, n, :], ALU.add), n < 7)

            def placed(k, ring):
                d, slot = 2 * k, 2 * ring
                step = chain(dve, s.place_step, PLACE_STEPS * k)
                need(dve, s.route, ROUTE_STEPS * k + ROUTE_STEPS)
                need(dve, s.ew_done, k + 1)
                step(v.tensor_scalar(best[:, 6, :], best[:, 3, :], 1.0, None, ALU.add))
                step(v.reciprocal(best[:, 7, :], best[:, 6, :]))
                step(v.tensor_tensor(best[:, 6, :], best[:, 3, :], best[:, 7, :], ALU.mult))
                step(v.tensor_tensor(best[:, 7, :], best[:, 7, :], best[:, 6, :], ALU.subtract))
                w3 = lambda n: best[:, n, :].rearrange("p (u j) -> p u j", u=2)
                word = lambda n: rows[:, slot:slot + 2, :, C + n]
                need(dve, s.rows_out, 16 * 16 * (k - 1))
                step(v.tensor_scalar(word(0), w3(6), 1.0 / WS, None, ALU.mult), False)
                step(v.tensor_scalar(word(1), w3(7), 1.0 / WS, None, ALU.mult), False)
                step(v.tensor_copy(word(2), w3(4)), False)
                ids = const(cst, "slot1").rearrange("p (b j) -> p b j", j=TILES)
                step(v.tensor_copy(word(3), ids[:, bass.ds(d, 2), :]), False)
                need(dve, s.rank_psum, k + 1)
                region = const(cst, "region").rearrange("p (n e) -> p n e", e=E)
                step(v.tensor_tensor(spot[:], bank_x[:, 64:64 + 8 * E].rearrange("p (n e) -> p n e", e=E), region, ALU.add))
                step(v.tensor_tensor(tmp[:, 0], spot[:], oh[:, 0], ALU.mult), False)
                step(v.tensor_tensor(tmp[:, 1], spot[:], oh[:, 1], ALU.mult))
                for n in range(2):
                    step(v.tensor_reduce(best[:, n, :], tmp[:, n], AX.X, ALU.add))
                    v_place = place[:, slot:slot + 2, :, n]
                    step(v.tensor_copy(v_place, w3(n)))
                v.tensor_copy(ahead16[:, 0, :], ahead16[:, 8, :]).then_inc(s.place_done, 1)
                need(dve, s.place_done, k + 1)

            pipelined(dve, PAIRS, 6, 2, [
                (2, keys_values, 0), (1, norm, 0, 0, xn, s.pow1, s.norm1), (4, norm, 0, 1, xn2, s.pow2, s.norm2),
                (1, norm, 1, 0, xn, s.pow1, s.norm1), (4, norm, 1, 1, xn2, s.pow2, s.norm2), (2, keys_values, 1),
                (2, mixed, 0), [(4, route), (0, stats, 0, s.stat1), (3, stats, 1, s.stat2)], (4, placed),
                (1, feature, 0), (2, mixed, 1), (4, lo, 0), (4, lo, 1), (5, weights_low), (1, feature, 1),
            ])
            dve.wait_ge(s.rank_psum, PAIRS + 1)
            step = chain(dve, s.table, 0)
            cnt, cnti, nb, delta, cum = (ffn[n] for n in ("cnt", "cnti", "nb", "delta", "cum"))
            step(v.tensor_copy(cnt[:], bank_s[:, 0:E]))
            step(v.tensor_tensor(ffn["tail_i"][:], cnt[:], const(cst, "region")[:, 0:E], ALU.add), False)
            step(v.tensor_scalar(cnti[:], cnt[:], float(BLOCK - 1), None, ALU.add))
            step(v.tensor_scalar(cnti[:], cnti[:], BLOCK.bit_length() - 1, None, ALU.arith_shift_right))
            step(v.tensor_copy(nb[:], cnti[:]))
            step(v.tensor_scalar(delta[:], nb[:], -float(BLOCK), float(REGION), ALU.mult, ALU.add))
            step(v.tensor_copy(cum[:], nb[:]))
            for e in range(1, E):
                step(v.tensor_tensor(cum[:, e:e + 1], cum[:, e - 1:e], nb[:, e:e + 1], ALU.add))
            expert, first, over = ffn["expert"], ffn["first"], ffn["over"]
            number = const(cst, "block_no")
            step(v.memset(expert[:], float(E)), False)
            step(v.tensor_scalar(first[:], number, float(BLOCK), None, ALU.mult))
            for e in range(E):
                step(v.tensor_scalar(over[:], number, cum[:, e:e + 1], None, ALU.is_ge))
                step(v.tensor_tensor(expert[:], expert[:], over[:], ALU.subtract), False)
                step(v.scalar_tensor_tensor(first[:], over[:], delta[:, e:e + 1], first[:], ALU.mult, ALU.add))
            step(v.tensor_scalar(expert[:], expert[:], 1.0, None, ALU.max), False)
            step(v.tensor_scalar(first[:], first[:], float(E * REGION), None, ALU.min))
            step(v.tensor_copy(ffn["first_i"][:], first[:]))
            padded, turn = ffn["padded"], ffn["turn"]
            step(v.memset(padded[:], 0.0), False)
            step(v.memset(turn[:], 0.0))
            step(v.tensor_scalar(padded[:].rearrange("p t b -> p (t b)")[:, TURN:TURN + BLOCKS], expert[:], -1.0, float(E), ALU.mult, ALU.add))
            for n in range(NOW):
                at = TURN - 3 + n
                step(v.scalar_tensor_tensor(turn[:, 2 * n // NOW, :], padded[:, at // TURN:at // TURN + TURNS + 1, at % TURN],
                                            float(E ** (n % (NOW // 2))), turn[:, 2 * n // NOW, :], ALU.mult, ALU.add))
            turn_i = ffn["turn_i"]
            step(v.tensor_copy(turn_i[:], turn[:]))
            step(v.tensor_scalar(turn_i[:, 1, :], turn_i[:, 1, :], 3 * (NOW // 2), None, ALU.logical_shift_left))
            step(v.tensor_tensor(turn_i[:, 0, :], turn_i[:, 0, :], turn_i[:, 1, :], ALU.bitwise_or))


META_STEPS = 4


def in_turns(eng, *stages, start=None):
    def turn(m, exists):
        if start:
            start(m)
        for p in range(TURN):
            for lag, f in stages:
                if exists(TURN * m + p - lag):
                    f(TURN * m + p - lag, (p - lag) % 4, (p - lag) % TURN)
    turn(0, lambda k: k >= 0)
    with eng.Fori(1, TURNS) as m:
        turn(m, lambda k: True)
    turn(TURNS, lambda k: k < BLOCKS)


def experts(nc, ident, ffn, rows_dram, res_dram):
    w1_hl, b1_hl, w2_hl, b2_hl = ffn["w1_hl"], ffn["b1_hl"], ffn["w2_hl"], ffn["b2_hl"]
    with ExitStack() as ctx:
        def sb(name, shape, dt=F32):
            return ctx.enter_context(nc.sbuf_tensor(name, shape, dt))

        ident16 = sb("e_ident16", [P, P], F16)
        ones16 = sb("e_ones16", [P, BLOCK], F16)
        xg = sb("e_xg", [P, 4, 2, ROW])
        xt = sb("e_xt", [P, 2, 2, BLOCK], F16)
        sig = sb("e_sig", [P, 2, 2 * BLOCK])
        gs = sb("e_gs", [P, 2, 2 * BLOCK])
        hid = sb("e_hid", [P, 2, 2 * BLOCK])
        hid_hl = sb("e_hid_hl", [P, 2, 2, 2, BLOCK], F16)
        first_choice = sb("e_first", [P, 2, 2])
        wt = sb("e_wt", [P, 4, 2])
        dest = sb("e_dest", [P, 4, 2], I32)
        y = sb("e_y", [P, 4, 2, C])
        one, held = sb("e_one", [1, 1]), sb("e_held", [1, 1])
        ps = ctx.enter_context(nc.psum_tensor("e_ps", [P, 8, 2 * BLOCK], F32))
        s = Named({n: ctx.enter_context(nc.semaphore("e_" + n)) for n in """
            set_v set_g held x0_in x1_in x2_in x3_in xT xt_done g_psum u_psum sig_done gs_done hid_done hh_done
            hl_done y_psum y_done meta r0_out r1_out r2_out r3_out""".split()})
        x_in = [s.x0_in, s.x1_in, s.x2_in, s.x3_in]
        r_out = [s.r0_out, s.r1_out, s.r2_out, s.r3_out]

        block = ctx.enter_context(nc.Block())

        @block.sync
        def _(sp):
            def load(m):
                for i in range(4):
                    row = sp.value_load(ffn["first_i"][0:1, bass.ds(4 * m + i, 1)], min_val=0, max_val=E * REGION)
                    need(sp, s.meta, META_STEPS * (4 * m + i - 3))
                    sp.dma_start(xg[:, i], rows_dram[bass.ds(row, BLOCK)].rearrange("(n p) w -> p n w", p=P)).then_inc(x_in[i], 16)
            load(0)
            with sp.Fori(1, BLOCKS // 4) as m:
                load(m)

        @block.gpsimd
        def _(pool):
            nc.gpsimd.memset(one[:], 0.0).then_inc(s.set_g, 1)
            pool.wait_ge(s.set_g, 1)

            def send(m):
                for i in range(4):
                    need(pool, s.held, 4 * m + i)
                    pool.wait_ge(s.y_done, 4 * m + i + 1)
                    nc.gpsimd.tensor_tensor(held[:], one[:], one[:], ALU.mult).then_inc(s.held, 1)
                    for n in range(2):
                        nc.gpsimd.indirect_dma_start(res_dram, bass.IndirectOffsetOnAxis(ap=dest[:, i, n:n + 1], axis=0),
                                                     y[:, i, n, :], None, bounds_check=2 * B * TOK - 1, oob_is_err=False).then_inc(r_out[i], 16)
            send(0)
            with pool.Fori(1, BLOCKS // 4) as m:
                send(m)
            for r in r_out:
                pool.wait_ge(r, 16 * 2 * BLOCKS // 4)

        @block.tensor
        def _(pe):
            t = nc.tensor
            pe.wait_ge(s.set_v, 2)

            now = []

            def look_up(m):
                word = pe.value_load(ffn["turn_i"][0:1, 0, bass.ds(m, 1)], min_val=0, max_val=E ** NOW - 1)
                now[:] = [(word // E ** n) % E for n in range(NOW)]

            def xT(k, i, j):
                pe.wait_ge(x_in[i], 4 * (k - i) + 16)
                need(pe, s.xt_done, k - 1)
                dst = ps[:, i % 2, 0:BLOCK].bitcast(F16).rearrange("p (l n c) -> p l n c", l=2, n=2)
                src = xg[:, i].bitcast(F16)
                for l in range(2):
                    for n in range(2):
                        last = t.transpose(dst[:, l, n], src[:, n, l * C:(l + 1) * C], ident16[:])
                last.then_inc(s.xT, 1)

            def inner(k, i, j):
                e = now[2 + (j + 1) % TURN]
                need(pe, s.xt_done, k + 1)
                x2 = [xt[:, i % 2, l, :] for l in range(2)]
                for bank, part, free, psum in ((2, 0, s.gs_done, s.g_psum), (4, 2, s.hid_done, s.u_psum)):
                    need(pe, free, k - 1)
                    for n in range(2):
                        at = (part + n) * P
                        o = ps[:, bank + i % 2, n * BLOCK:(n + 1) * BLOCK]
                        hi, lo = (w1_hl[:, bass.ds(e, 1), l, at:at + P].rearrange("p o c -> p (o c)") for l in range(2))
                        t.matmul(o, b1_hl[:, bass.ds(e, 1), at:at + P].rearrange("p o c -> p (o c)"), ones16[:], start=True, stop=False)
                        t.matmul(o, hi, x2[0], start=False, stop=False)
                        t.matmul(o, hi, x2[1], start=False, stop=False)
                        last = t.matmul(o, lo, x2[0], start=False, stop=True)
                    last.then_inc(psum, 1)

            def outer(k, i, j):
                e = now[(j + 3) % TURN]
                need(pe, s.hl_done, k + 1)
                need(pe, s.y_done, k - 1)
                for n in range(2):
                    o = ps[:, 6 + i % 2, n * C:(n + 1) * C]
                    t.matmul(o, ones16[:, 0:P], b2_hl[:, bass.ds(e, 1), :].rearrange("p o c -> p (o c)"), start=True, stop=False)
                    for q in range(2):
                        hi, lo = (hid_hl[:, i % 2, l, q, n * P:(n + 1) * P] for l in range(2))
                        whi, wlo = (w2_hl[:, bass.ds(e, 1), l, q, :].rearrange("p o c -> p (o c)") for l in range(2))
                        t.matmul(o, hi, whi, start=False, stop=False)
                        t.matmul(o, hi, wlo, start=False, stop=False)
                        last = t.matmul(o, lo, whi, start=False, stop=q == 1)
                last.then_inc(s.y_psum, 1)

            in_turns(pe, (0, xT), (1, inner), (3, outer), start=look_up)

        @block.scalar
        def _(act):
            a = nc.scalar

            def x(k, i, j):
                need(act, s.xT, k + 1)
                need(act, s.u_psum, k - 1)
                a.activation(xt[:, i % 2].rearrange("p l c -> p (l c)"), ps[:, i % 2, 0:BLOCK].bitcast(F16), ACT.Copy).then_inc(s.xt_done, 1)

            def sigmoid(k, i, j):
                need(act, s.g_psum, k + 1)
                need(act, s.gs_done, k - 1)
                a.activation(sig[:, i % 2], ps[:, 2 + i % 2], ACT.Sigmoid, scale=1.702 / WS).then_inc(s.sig_done, 1)

            def high(k, i, j):
                need(act, s.hid_done, k + 1)
                need(act, s.y_psum, k - 1)
                need(act, s.hl_done, k - 1)
                a.activation(hid_hl[:, i % 2, 0].rearrange("p q c -> p (q c)"), hid[:, i % 2], ACT.Copy).then_inc(s.hh_done, 1)

            def result(k, i, j):
                need(act, s.y_psum, k + 1)
                need(act, s.meta, META_STEPS * (k + 1))
                need(act, r_out[i], 8 * (k - i))
                for n in range(2):
                    ins = a.activation(y[:, i, n, :], ps[:, 6 + i % 2, n * C:(n + 1) * C], ACT.Copy, scale=wt[:, i, n:n + 1])
                ins.then_inc(s.y_done, 1)
            in_turns(act, (0, x), (2, high), (1, sigmoid), (4, result))

        @block.vector
        def _(dve):
            v = nc.vector
            step = chain(dve, s.set_v, 0)
            step(v.tensor_copy(ident16[:], ident))
            step(v.memset(ones16[:], 1.0))

            def meta(k, i, j):
                need(dve, x_in[i], 4 * (k - i) + 16)
                need(dve, s.xT, k + 1)
                need(dve, s.y_done, k - 3)
                need(dve, r_out[i], 8 * (k - i))
                step = chain(dve, s.meta, META_STEPS * k)
                word = lambda n: xg[:, i, :, C + n]
                one = first_choice[:, i % 2]
                step(v.tensor_scalar(one, word(2), ffn["expert"][:, bass.ds(k, 1)], None, ALU.is_equal))
                step(v.tensor_tensor(wt[:, i], one, word(1), ALU.mult), False)
                step(v.tensor_tensor(dest[:, i], word(3), one, ALU.subtract))
                step(v.tensor_tensor(wt[:, i], wt[:, i], word(0), ALU.add), False)

            def gated(k, i, j):
                need(dve, s.sig_done, k + 1)
                need(dve, s.hid_done, k - 1)
                v.scalar_tensor_tensor(gs[:, i % 2], ps[:, 2 + i % 2], 1.0 / (WS * WS), sig[:, i % 2], ALU.mult, ALU.mult).then_inc(s.gs_done, 1)
                need(dve, s.gs_done, k + 1)
                need(dve, s.u_psum, k + 1)
                need(dve, s.hl_done, k - 1)
                need(dve, s.hh_done, k - 1)
                v.scalar_tensor_tensor(hid[:, i % 2], ps[:, 4 + i % 2], WS, gs[:, i % 2], ALU.add, ALU.mult).then_inc(s.hid_done, 1)

            def low(k, i, j):
                need(dve, s.hh_done, k + 1)
                need(dve, s.y_psum, k - 1)
                v.tensor_tensor(hid_hl[:, i % 2, 1].rearrange("p q c -> p (q c)"), hid[:, i % 2],
                                hid_hl[:, i % 2, 0].rearrange("p q c -> p (q c)"), ALU.subtract).then_inc(s.hl_done, 1)
            in_turns(dve, (2, meta), (2, low), (1, gated))


def combine(nc, resid, res_dram, out):
    out_tok = out.rearrange("b a (tl j) c -> b (a tl) (j c)", j=TILES)
    res_tok = res_dram.rearrange("(b p j n) c -> b p (j n c)", p=P, j=TILES, n=2)
    with ExitStack() as ctx:
        yb = ctx.enter_context(nc.sbuf_tensor("c_y", [P, 4, 2 * TOK], F32))
        s = Named({n: ctx.enter_context(nc.semaphore("c_" + n)) for n in
                               "y0_in y1_in y2_in y3_in one_done both_done out_done".split()})
        y_in = [s.y0_in, s.y1_in, s.y2_in, s.y3_in]
        block = ctx.enter_context(nc.Block())

        @block.sync
        def _(sp):
            def load(m):
                for i in range(4):
                    need(sp, s.both_done, 4 * m + i - 3)
                    sp.dma_start(yb[:, i, :], res_tok[4 * m + i]).then_inc(y_in[i], 16)
            load(0)
            with sp.Fori(1, B // 4) as m:
                load(m)

        @block.vector
        def _(dve):
            with dve.Fori(0, B // 4) as m:
                for i in range(4):
                    b = 4 * m + i
                    y4 = yb[:, i, :].rearrange("p (j n c) -> p j n c", j=TILES, n=2)
                    r = resid[:, b, :].rearrange("p (j c) -> p j c", j=TILES)
                    dve.wait_ge(y_in[i], 16 * m + 16)
                    nc.vector.tensor_tensor(r, r, y4[:, :, 0, :], ALU.add).then_inc(s.one_done, 1)
                    dve.wait_ge(s.one_done, b + 1)
                    nc.vector.tensor_tensor(r, r, y4[:, :, 1, :], ALU.add).then_inc(s.both_done, 1)

        @block.scalar
        def _(act):
            with act.Fori(0, B) as b:
                act.wait_ge(s.both_done, b + 1)
                act.dma_start(out_tok[b], resid[:, b, :]).then_inc(s.out_done, 16)
            act.wait_ge(s.out_done, 16 * B)


def build(nc, t):
    rows_dram = nc.dram_tensor("rows", (E * REGION + BLOCK, ROW), F32, kind="Internal").ap()
    res_dram = nc.dram_tensor("results", (2 * B * TOK, C), F32, kind="Internal").ap()
    with ExitStack() as ctx:
        def sb(name, shape, dt=F32):
            return ctx.enter_context(nc.sbuf_tensor(name, shape, dt))

        early = sb("early", [P, EARLY.shape[1]])
        resid = sb("resid", [P, B, TOK])
        ones16 = sb("ones16", [P, P], F16)
        agent_attention(nc, early, resid, ones16, t["x"], t["L0_conv_coalition"], t["L0_conv_masks"], t["L0_conv_emb_W"],
                        *(t["L0_conv_" + n] for n in "Wq bq Wk bk Wv bv Wo bo".split()), t["early"])
        late = sb("late", [P, LATE.shape[1]])
        ffn = {
            "w1_hl": sb("w1_hl", [P, E, 2, 2 * I], F16), "b1_hl": sb("b1_hl", [P, E, 2 * I], F16),
            "w2_hl": sb("w2_hl", [P, E, 2, 2, C], F16), "b2_hl": sb("b2_hl", [P, E, C], F16),
            "cnt": sb("cnt", [P, E]), "cnti": sb("cnti", [P, E], I32), "nb": sb("nb", [P, E]),
            "delta": sb("delta", [P, E]), "cum": sb("cum", [P, E]), "tail_i": sb("tail_i", [P, E], I32),
            "expert": sb("expert", [P, BLOCKS]), "first": sb("first", [P, BLOCKS]), "over": sb("over", [P, BLOCKS]),
            "padded": sb("padded", [P, TURNS + 2, TURN]), "turn": sb("turn", [P, 2, TURNS + 1]), "turn_i": sb("turn_i", [P, 2, TURNS + 1], I32), "first_i": sb("first_i", [P, BLOCKS], I32),
            "nobody": sb("nobody", [P, 2, ROW]),
        }
        ident = const(early, "ident")
        token_mixer(nc, late, resid, ones16, ident, t["late"], ffn, rows_dram, *(t["L1_attn_" + n] for n in "Wq bq Wk bk Wv bv".split()),
                    *(t["L1_ffn_" + n] for n in "router_w router_b gate_up_proj gate_up_proj_bias down_proj down_proj_bias".split()))
        experts(nc, ident, ffn, rows_dram, res_dram)
        combine(nc, resid, res_dram, t["out"])


_INS = """x L0_conv_coalition L0_conv_masks L0_conv_emb_W L0_conv_Wq L0_conv_bq L0_conv_Wk L0_conv_bk L0_conv_Wv L0_conv_bv
    L0_conv_Wo L0_conv_bo L1_attn_Wq L1_attn_bq L1_attn_Wk L1_attn_bk L1_attn_Wv L1_attn_bv L1_ffn_router_w L1_ffn_router_b
    L1_ffn_gate_up_proj L1_ffn_gate_up_proj_bias L1_ffn_down_proj L1_ffn_down_proj_bias""".split()


def kernel(**inputs):
    import concourse.bacc as bacc
    from concourse.bass_utils import run_bass_kernel_spmd

    nc = bacc.Bacc("TRN2", target_bir_lowering=False, num_devices=1)
    arrays, tensors = {}, {}
    for name, a in [(n, inputs[n]) for n in _INS] + [("early", EARLY), ("late", LATE)]:
        a = np.ascontiguousarray(a)
        arrays[f"in_{name}"] = a
        tensors[name] = nc.dram_tensor(f"in_{name}", a.shape, mybir.dt.from_np(a.dtype), kind="ExternalInput").ap()
    tensors["out"] = nc.dram_tensor("out_0", (B, A, T, C), F32, kind="ExternalOutput").ap()
    build(nc, tensors)
    return run_bass_kernel_spmd(nc, [arrays], core_ids=[0]).results[0]["out_0"]
```
